# Optimizing a Trainium2 kernel written in Bass

```python
import numpy as np
import jax
import jax.numpy as jnp

def _softmax(x, axis=-1):
    return jax.nn.softmax(x, axis=axis)

def _gelu(x):
    return jax.nn.gelu(x, approximate=True)

def _silu(x):
    return jax.nn.silu(x)

def _sigmoid(x):
    return jax.nn.sigmoid(x)

def _layernorm(x, axis=-1, eps=1e-05):
    m = jnp.mean(x, axis=axis, keepdims=True)
    v = jnp.var(x, axis=axis, keepdims=True)
    return (x - m) / jnp.sqrt(v + eps)

def _scatter_add(tgt, idx, src, axis=0):
    return tgt.at[idx].add(src)

def _segment_sum(src, seg, n):
    return jax.ops.segment_sum(src, seg, n)
kernel_name = 'mk_early_fusion_d1_tok_img256_r4_315856'

def setup_inputs(seed: int=0):
    np.random.seed(seed)
    _w = jnp.asarray

    def _rec_inputs():
        import jax
        import jax.numpy as jnp
        _rk = jax.random.key(seed)
        x = -0.000125008 + 0.999885 * jax.random.normal(jax.random.fold_in(_rk, 1), (32, 64, 128, 128), jnp.float32)
        txt = 7.55513e-05 + 0.28436 * jax.random.normal(jax.random.fold_in(_rk, 2), (32, 128, 64), jnp.float32)
        return (x, txt)
    x, txt = _rec_inputs()

    def _L0_tok_setup():
        import jax, jax.numpy as jnp
        import numpy as np
        D_MODEL = 64
        NHEAD = 8
        DS = 4
        OFFSET_SCALE = 4.0

        def bilinear_sample(fm, pts):
            B, C, H, W = fm.shape
            x = (pts[..., 0] + 1.0) * 0.5 * (W - 1)
            y = (pts[..., 1] + 1.0) * 0.5 * (H - 1)
            x0 = jnp.clip(jnp.floor(x), 0.0, W - 2)
            y0 = jnp.clip(jnp.floor(y), 0.0, H - 2)
            wx = jnp.clip(x - x0, 0.0, 1.0)
            wy = jnp.clip(y - y0, 0.0, 1.0)
            x0i = x0.astype(jnp.int32)
            y0i = y0.astype(jnp.int32)
            fm2 = fm.reshape(B, C, H * W)
            N, P = (pts.shape[1], pts.shape[2])

            def gather(yi, xi):
                idx = (yi * W + xi).reshape(B, N * P)
                g = jnp.take_along_axis(fm2, idx[:, None, :], axis=2)
                return g.reshape(B, C, N, P)
            v00 = gather(y0i, x0i)
            v01 = gather(y0i, x0i + 1)
            v10 = gather(y0i + 1, x0i)
            v11 = gather(y0i + 1, x0i + 1)
            wx_ = wx[:, None]
            wy_ = wy[:, None]
            out = v00 * (1 - wx_) * (1 - wy_) + v01 * wx_ * (1 - wy_) + v10 * (1 - wx_) * wy_ + v11 * wx_ * wy_
            return jnp.moveaxis(out, 1, -1)

        def layer_norm(x, g, b, eps=1e-05):
            mu = jnp.mean(x, axis=-1, keepdims=True)
            var = jnp.var(x, axis=-1, keepdims=True)
            return (x - mu) * jax.lax.rsqrt(var + eps) * g + b

        def reference_points(B, H, W):
            yc = jnp.linspace(-1.0, 1.0, H // DS)
            xc = jnp.linspace(-1.0, 1.0, W // DS)
            yg, xg = jnp.meshgrid(yc, xc, indexing='ij')
            ref = jnp.stack([xg.reshape(-1), yg.reshape(-1)], axis=-1)
            return jnp.broadcast_to(ref[None], (B,) + ref.shape)
        key = jax.random.key(seed)
        ks = jax.random.split(key, 6)
        B, C, H, W = (8, D_MODEL, 128, 128)
        s = 0.05
        return {'feature_map': jax.random.normal(ks[0], (B, C, H, W), jnp.float32), 'W_q': jax.random.normal(ks[1], (C, C), jnp.float32) * s, 'W_k': jax.random.normal(ks[2], (C, C), jnp.float32) * s, 'W_v': jax.random.normal(ks[3], (C, C), jnp.float32) * s, 'W_o1': jax.random.normal(ks[4], (C, C // DS), jnp.float32) * s, 'b_o1': jnp.zeros((C // DS,), jnp.float32), 'ln_g': jnp.ones((C // DS,), jnp.float32), 'ln_b': jnp.zeros((C // DS,), jnp.float32), 'W_o2': jax.random.normal(ks[5], (C // DS, NHEAD * 2), jnp.float32) * s, 'b_o2': jnp.zeros((NHEAD * 2,), jnp.float32)}
    _L0_tok_all = _L0_tok_setup()
    _L0_tok_in = {k: v for k, v in _L0_tok_all.items() if k in ('W_q', 'W_k', 'W_v', 'W_o1', 'b_o1', 'ln_g', 'ln_b', 'W_o2', 'b_o2')}
    del _L0_tok_all

    def _L0_attn_setup():
        import math
        import jax, jax.numpy as jnp
        import numpy as np
        D, DK, DV = (64, 64, 64)
        key = jax.random.key(seed)
        ks = jax.random.split(key, 7)
        s = 1.0 / math.sqrt(D)
        return {'x': jax.random.normal(ks[0], (4, 1024, D), dtype=jnp.float32), 'Wq': jax.random.uniform(ks[1], (D, DK), jnp.float32, -s, s), 'bq': jax.random.uniform(ks[2], (DK,), jnp.float32, -s, s), 'Wk': jax.random.uniform(ks[3], (D, DK), jnp.float32, -s, s), 'bk': jax.random.uniform(ks[4], (DK,), jnp.float32, -s, s), 'Wv': jax.random.uniform(ks[5], (D, DV), jnp.float32, -s, s), 'bv': jax.random.uniform(ks[6], (DV,), jnp.float32, -s, s)}
    _L0_attn_all = _L0_attn_setup()
    _L0_attn_in = {k: v for k, v in _L0_attn_all.items() if k in ('Wq', 'bq', 'Wk', 'bk', 'Wv', 'bv')}
    del _L0_attn_all

    def _L0_ffn_setup():
        import jax, jax.numpy as jnp
        import numpy as np
        B, S, H, F, E, K = (8, 1024, 64, 128, 16, 2)
        EPS = 1e-05
        key = jax.random.key(seed)
        ks = jax.random.split(key, 9)
        sc = 0.02
        return {'x': jax.random.normal(ks[0], (B, S, H), dtype=jnp.float32), 'gate_w': jax.random.normal(ks[1], (H, E), dtype=jnp.float32) * sc, 'gate_b': jnp.zeros((E,), dtype=jnp.float32), 'w1': jax.random.normal(ks[2], (E, H, F), dtype=jnp.float32) * sc, 'b1': jnp.zeros((E, F), dtype=jnp.float32), 'w2': jax.random.normal(ks[3], (E, F, H), dtype=jnp.float32) * sc, 'b2': jnp.zeros((E, H), dtype=jnp.float32), 'gamma': jnp.ones((H,), dtype=jnp.float32), 'beta': jnp.zeros((H,), dtype=jnp.float32)}
    _L0_ffn_all = _L0_ffn_setup()
    _L0_ffn_in = {k: v for k, v in _L0_ffn_all.items() if k in ('gate_w', 'gate_b', 'w1', 'b1', 'w2', 'b2', 'gamma', 'beta')}
    del _L0_ffn_all
    return {'x': x, 'txt': txt, 'L0_tok_W_q': _L0_tok_in['W_q'], 'L0_tok_W_k': _L0_tok_in['W_k'], 'L0_tok_W_v': _L0_tok_in['W_v'], 'L0_tok_W_o1': _L0_tok_in['W_o1'], 'L0_tok_b_o1': _L0_tok_in['b_o1'], 'L0_tok_ln_g': _L0_tok_in['ln_g'], 'L0_tok_ln_b': _L0_tok_in['ln_b'], 'L0_tok_W_o2': _L0_tok_in['W_o2'], 'L0_tok_b_o2': _L0_tok_in['b_o2'], 'L0_attn_Wq': _L0_attn_in['Wq'], 'L0_attn_bq': _L0_attn_in['bq'], 'L0_attn_Wk': _L0_attn_in['Wk'], 'L0_attn_bk': _L0_attn_in['bk'], 'L0_attn_Wv': _L0_attn_in['Wv'], 'L0_attn_bv': _L0_attn_in['bv'], 'L0_ffn_gate_w': _L0_ffn_in['gate_w'], 'L0_ffn_gate_b': _L0_ffn_in['gate_b'], 'L0_ffn_w1': _L0_ffn_in['w1'], 'L0_ffn_b1': _L0_ffn_in['b1'], 'L0_ffn_w2': _L0_ffn_in['w2'], 'L0_ffn_b2': _L0_ffn_in['b2'], 'L0_ffn_gamma': _L0_ffn_in['gamma'], 'L0_ffn_beta': _L0_ffn_in['beta']}

def reference(x, txt, L0_tok_W_q, L0_tok_W_k, L0_tok_W_v, L0_tok_W_o1, L0_tok_b_o1, L0_tok_ln_g, L0_tok_ln_b, L0_tok_W_o2, L0_tok_b_o2, L0_attn_Wq, L0_attn_bq, L0_attn_Wk, L0_attn_bk, L0_attn_Wv, L0_attn_bv, L0_ffn_gate_w, L0_ffn_gate_b, L0_ffn_w1, L0_ffn_b1, L0_ffn_w2, L0_ffn_b2, L0_ffn_gamma, L0_ffn_beta):
    import jax
    import jax.numpy as jnp

    def _L0_tok_ref(feature_map, W_q, W_k, W_v, W_o1, b_o1, ln_g, ln_b, W_o2, b_o2):
        import jax, jax.numpy as jnp
        import numpy as np
        D_MODEL = 64
        NHEAD = 8
        DS = 4
        OFFSET_SCALE = 4.0

        def bilinear_sample(fm, pts):
            B, C, H, W = fm.shape
            x = (pts[..., 0] + 1.0) * 0.5 * (W - 1)
            y = (pts[..., 1] + 1.0) * 0.5 * (H - 1)
            x0 = jnp.clip(jnp.floor(x), 0.0, W - 2)
            y0 = jnp.clip(jnp.floor(y), 0.0, H - 2)
            wx = jnp.clip(x - x0, 0.0, 1.0)
            wy = jnp.clip(y - y0, 0.0, 1.0)
            x0i = x0.astype(jnp.int32)
            y0i = y0.astype(jnp.int32)
            fm2 = fm.reshape(B, C, H * W)
            N, P = (pts.shape[1], pts.shape[2])

            def gather(yi, xi):
                idx = (yi * W + xi).reshape(B, N * P)
                g = jnp.take_along_axis(fm2, idx[:, None, :], axis=2)
                return g.reshape(B, C, N, P)
            v00 = gather(y0i, x0i)
            v01 = gather(y0i, x0i + 1)
            v10 = gather(y0i + 1, x0i)
            v11 = gather(y0i + 1, x0i + 1)
            wx_ = wx[:, None]
            wy_ = wy[:, None]
            out = v00 * (1 - wx_) * (1 - wy_) + v01 * wx_ * (1 - wy_) + v10 * (1 - wx_) * wy_ + v11 * wx_ * wy_
            return jnp.moveaxis(out, 1, -1)

        def layer_norm(x, g, b, eps=1e-05):
            mu = jnp.mean(x, axis=-1, keepdims=True)
            var = jnp.var(x, axis=-1, keepdims=True)
            return (x - mu) * jax.lax.rsqrt(var + eps) * g + b

        def reference_points(B, H, W):
            yc = jnp.linspace(-1.0, 1.0, H // DS)
            xc = jnp.linspace(-1.0, 1.0, W // DS)
            yg, xg = jnp.meshgrid(yc, xc, indexing='ij')
            ref = jnp.stack([xg.reshape(-1), yg.reshape(-1)], axis=-1)
            return jnp.broadcast_to(ref[None], (B,) + ref.shape)
        B, C, H, W = feature_map.shape
        dh = C // NHEAD
        ref = reference_points(B, H, W)
        Nq = ref.shape[1]
        q_feat = bilinear_sample(feature_map, ref[:, :, None, :])[:, :, 0]
        queries = q_feat @ W_q.T
        h = jax.nn.gelu(layer_norm(q_feat @ W_o1 + b_o1, ln_g, ln_b))
        off = (h @ W_o2 + b_o2).reshape(B, Nq, NHEAD, 2) * OFFSET_SCALE
        scale = jnp.array([2.0 / (W - 1), 2.0 / (H - 1)], jnp.float32)
        sampling_points = ref[:, :, None, :] + off * scale
        sampled = bilinear_sample(feature_map, sampling_points)
        keys = jnp.einsum('bnpc,dc->bnpd', sampled, W_k)
        values = jnp.einsum('bnpc,dc->bnpd', sampled, W_v)
        q = queries.reshape(B, Nq, NHEAD, dh)
        k = keys.reshape(B, Nq, NHEAD, NHEAD, dh)
        v = values.reshape(B, Nq, NHEAD, NHEAD, dh)
        scores = jnp.einsum('bnhd,bnphd->bnhp', q, k) / jnp.sqrt(jnp.float32(dh))
        attn = jax.nn.softmax(scores, axis=-1)
        out = jnp.einsum('bnhp,bnphd->bnhd', attn, v).reshape(B, Nq, C)
        return out

    def _L0_attn_ref(x, Wq, bq, Wk, bk, Wv, bv):
        import math
        import jax, jax.numpy as jnp
        import numpy as np
        D, DK, DV = (64, 64, 64)
        q = x @ Wq + bq
        k = x @ Wk + bk
        v = x @ Wv + bv
        scores = jnp.einsum('bqd,bkd->bqk', q, k) / math.sqrt(DK)
        S = x.shape[1]
        causal = jnp.tril(jnp.ones((S, S), dtype=bool))
        scores = jnp.where(causal, scores, -jnp.inf)
        attn = jax.nn.softmax(scores, axis=-1)
        return jnp.einsum('bqk,bkd->bqd', attn, v)

    def _L0_ffn_ref(x, gate_w, gate_b, w1, b1, w2, b2, gamma, beta):
        import jax, jax.numpy as jnp
        import numpy as np
        B, S, H, F, E, K = (8, 1024, 64, 128, 16, 2)
        EPS = 1e-05
        gate_logits = x @ gate_w + gate_b
        topk_vals, topk_idx = jax.lax.top_k(gate_logits, K)
        topk_w = jax.nn.softmax(topk_vals, axis=-1)
        h = jax.nn.relu(jnp.einsum('bsh,ehf->bsef', x, w1) + b1)
        expert_out = jnp.einsum('bsef,efh->bseh', h, w2) + b2
        sel = jnp.take_along_axis(expert_out, topk_idx[:, :, :, None], axis=2)
        moe = jnp.sum(topk_w[..., None] * sel, axis=2)
        y = x + moe
        mu = jnp.mean(y, axis=-1, keepdims=True)
        var = jnp.var(y, axis=-1, keepdims=True)
        return (y - mu) / jnp.sqrt(var + EPS) * gamma + beta
    h = _L0_tok_ref(x, L0_tok_W_q, L0_tok_W_k, L0_tok_W_v, L0_tok_W_o1, L0_tok_b_o1, L0_tok_ln_g, L0_tok_ln_b, L0_tok_W_o2, L0_tok_b_o2)
    h = jnp.concatenate([h, txt], axis=1)
    h = h + _L0_attn_ref(_layernorm(h, axis=-1), L0_attn_Wq, L0_attn_bq, L0_attn_Wk, L0_attn_bk, L0_attn_Wv, L0_attn_bv)
    h = h + _L0_ffn_ref(_layernorm(h, axis=-1), L0_ffn_gate_w, L0_ffn_gate_b, L0_ffn_w1, L0_ffn_b1, L0_ffn_w2, L0_ffn_b2, L0_ffn_gamma, L0_ffn_beta)
    return h

_drawn_inputs = setup_inputs


def setup_inputs(seed=0):
    import zlib

    import numpy as np

    out = dict(_drawn_inputs(seed))
    spreads = {'L0_tok_b_o1': (0.0, 0.1),
     'L0_tok_ln_g': (1.0, 0.2),
     'L0_tok_ln_b': (0.0, 0.1),
     'L0_tok_b_o2': (0.0, 0.1),
     'L0_ffn_gate_b': (0.0, 0.1),
     'L0_ffn_b1': (0.0, 0.8),
     'L0_ffn_b2': (0.0, 0.1),
     'L0_ffn_gamma': (1.0, 0.2),
     'L0_ffn_beta': (0.0, 0.1)}
    factors = {'L0_attn_bk': 8.0, 'L0_ffn_w1': 4.439, 'L0_ffn_w2': 3.214}
    for name, (base, spread) in spreads.items():
        noise = np.random.default_rng([zlib.crc32(name.encode()), seed]).standard_normal(out[name].shape)
        drawn = base * np.exp(spread * noise) if base else spread * noise
        out[name] = jnp.asarray(drawn.astype(out[name].dtype))
    for name, factor in factors.items():
        out[name] = (out[name] * factor).astype(out[name].dtype)
    return out
```

```python
from contextlib import ExitStack

import concourse.bass as bass
from concourse import mybir
import numpy as np

F32 = mybir.dt.float32
F32R = mybir.dt.float32r
I32 = mybir.dt.int32
U32 = mybir.dt.uint32
ALU = mybir.AluOpType
ACT = mybir.ActivationFunctionType
X_AXIS = mybir.AxisListType.X

P = 128
B, C, H, W = 32, 64, 128, 128
TXT = 128
PAIRS = B // 2
GRID = 32
NQ = GRID * GRID
QT_N = NQ // P
S = NQ + TXT
ST_N = S // P
NP_, NH, DH = 8, 8, 8
F, E = 128, 16
O1W = C // 4
GROUPS = 2 * QT_N
NCH = QT_N
CR = H // NCH
HR = CR // 2
NG = 8
EPS = 1e-5
RNE = 8388608.0
RSQRT_SEED = float(0x5F3759DF)
MASKED = -1.0e30
QK_SCALE = DH ** -0.5
ATT_SCALE = C ** -0.5
CC = 3
NCC = ST_N // CC
EH = E // 2
BANK = 512


def grid_coordinates():
    step = np.arange(GRID, dtype=np.float32) / np.float32(GRID - 1)
    ref = np.float32(-1.0) * (np.float32(1.0) - step) + np.float32(1.0) * step
    pix = (ref + np.float32(1.0)) * np.float32(0.5) * np.float32(W - 1)
    low = np.clip(np.floor(pix), 0, W - 2).astype(np.int64)
    return pix.astype(np.float32), low, np.clip(pix - low, 0, 1).astype(np.float32)


IDENT, MASK, GX, GY, RANK, GRIDW = 0, 128, 256, 257, 265, 281
NCONST = GRIDW + GRID * 2 * GRID


def constants():
    pix, low, frac = grid_coordinates()
    c = np.zeros((P, NCONST), np.float32)
    c[:, IDENT:IDENT + P] = np.eye(P, dtype=np.float32)
    c[:, MASK:MASK + P] = np.where(np.arange(P)[None, :] > np.arange(P)[:, None], np.float32(MASKED), np.float32(0))
    c[:, GX] = pix[np.arange(P) % GRID]
    for t in range(QT_N):
        c[:, GY + t] = pix[4 * t + np.arange(P) // GRID]
    c[:, RANK:RANK + E] = E - np.arange(E)
    m = c[:, GRIDW:].reshape(P, GRID, 2, GRID)
    for i in range(GRID):
        for k, wy in ((0, np.float32(1) - frac[i]), (1, frac[i])):
            for j in range(GRID):
                m[low[j], i, k, j] += wy * (np.float32(1) - frac[j])
                m[low[j] + 1, i, k, j] += wy * frac[j]
    return c


class Pair:

    def __init__(self, off, eng=None, turn=None):
        self.off, self.eng, self.turn, self.products = off, eng, turn, {}

    def __add__(self, n):
        p = Pair(self.off + n, self.eng, self.turn)
        p.products = self.products
        return p

    def __sub__(self, n):
        return self + -n

    def times(self, per, k=0):
        if self.turn is None:
            return self.off * per + k
        if per not in self.products:
            self.products[per] = self.eng.snap(self.turn * (2 * per))
        return self.products[per] + (self.off * per + k)


class Signal:

    def __init__(self, sem, per, spare=0):
        self.sem, self.per, self.spare = sem, per, spare

    def rise(self, pair, k):
        assert pair.off * self.per + k + self.spare > 0, "a wait's value has to stay positive"
        return self.sem, pair.times(self.per, k + self.spare)


def build(nc, x, txt, w, out, tables):
    _, LOW, _ = grid_coordinates()
    ctx = ExitStack()
    with ctx:
        def sb(name, shape, dt=F32):
            return ctx.enter_context(nc.sbuf_tensor(name, shape, dt))

        signals = []

        def sig(name, per, spare=0):
            s = Signal(ctx.enter_context(nc.semaphore(name)), per, spare)
            signals.append(s)
            return s

        const = sb("const", [P, NCONST])
        ident = const[:, IDENT:IDENT + P]
        mask = const[:, MASK:MASK + P]
        gridw = const[:, GRIDW:].rearrange("p (i k j) -> p i k j", i=GRID, k=2)
        w_proj = sb("w_proj", [P, 2 * (C + O1W)])
        w_o2 = sb("w_o2", [P, P])
        w_kv = sb("w_kv", [P, 2 * C])
        rows16 = sb("rows16", [P, 5, 16])
        bo1, lng, lnb, bo2, gateb = (rows16[:, n, :] for n in range(5))
        rows64 = sb("rows64", [P, 3, C])
        bv, gamma, beta = (rows64[:, n, :] for n in range(3))
        bqk = sb("bqk", [P, 2])
        b1 = sb("b1", [P, E])
        NATT = 2 * P + C
        wa_h = sb("wa_h", [P, NATT], F32R)
        wa_l = sb("wa_l", [P, NATT], F32R)
        wg_h = sb("wg_h", [P, E], F32R)
        wg_l = sb("wg_l", [P, E], F32R)
        w1_h = sb("w1_h", [P, E * F], F32R)
        w1_l = sb("w1_l", [P, E * F], F32R)
        w2 = sb("w2", [P, E * C])
        b2_hl = sb("b2_hl", [P, E * C], F32R)
        ones_r = sb("ones_r", [P, P], F32R)

        fm = sb("fm", [P, 2, HR * W])
        rows = sb("rows", [P, 2, 2, CR + 1, C])
        qf = sb("qf", [P, P])
        qft = sb("qft", [P, P])
        query = sb("query", [P, 2, QT_N, 2, C])
        o1 = sb("o1", [P, GROUPS, O1W])
        oa = sb("oa", [P, GROUPS, O1W])
        ob = sb("ob", [P, GROUPS, O1W])
        oht = sb("oht", [P, 2, P])
        st16 = sb("st16", [P, 8, GROUPS])
        base_xy = sb("base_xy", [P, GROUPS, NP_, 2])
        ca = oa[:].rearrange("p g (n k) -> p (g n) k", k=2)
        cb = ob[:].rearrange("p g (n k) -> p (g n) k", k=2)
        frac2 = sb("frac2", [P, GROUPS * NP_, 2, 2])
        idxf = o1[:].rearrange("p g n -> p (g n)")[:, 0:GROUPS * NP_].rearrange("p (g n) -> p g n", n=NP_)
        idx = sb("idx", [P, 2, GROUPS * NP_], U32)
        corner_w = sb("corner_w", [P, 2, GROUPS, NP_ * 4])
        table_base = sb("table_base", [P, 2])
        gath = sb("gath", [P, NG, NP_, 4 * C])

        shared = sb("shared", [P, 5 * 1024])
        prod = [shared[:, n * 1024:(n + 1) * 1024] for n in range(2)]
        samp_t = [shared[:, (2 + n) * 1024:(3 + n) * 1024] for n in range(2)]
        kq = shared[:, 4096:4608]
        av = shared[:, 4608:5120]
        probs = [shared[:, n * S:(n + 1) * S] for n in range(2)]
        probs_t = [shared[:, (2 + n) * S:(3 + n) * S] for n in range(2)]
        gated = [shared[:, n * 512:(n + 1) * 512] for n in range(2)]
        shared2 = sb("shared2", [P, 2 * S])
        q_t, k_t = shared2[:, 0:S], shared2[:, S:2 * S]
        hid = [shared2[:, n * CC * P:(n + 1) * CC * P] for n in range(3)]
        moe = shared2[:, S:2 * S].rearrange("p (h t c) -> p h t c", h=2, c=C)

        pt_sc = sb("pt_sc", [P, 4, NP_ * NH])
        pt_st = sb("pt_st", [P, 3, NH])
        pt_o = sb("pt_o", [P, C])
        h0 = sb("h0", [P, 2, ST_N, C])
        h1 = sb("h1", [P, ST_N, C])
        xn = sb("xn", [P, ST_N, C])
        xs = sb("xs", [P, ST_N, 2, C], F32R)
        xt = sb("xt", [P, S], F32R)
        v_sb = sb("v_sb", [P, ST_N, C])
        bn6 = sb("bn6", [P, ST_N, 6])
        mv = sb("mv", [P, ST_N, 2])
        ln9 = sb("ln9", [P, 8, ST_N])
        att = sb("att", [P, 4, ST_N])
        lg = sb("lg", [P, 6, ST_N, E])
        gs = sb("gs", [P, 8, ST_N])
        gate = sb("gate", [P, ST_N, E])
        out_sb = sb("out_sb", [P, ST_N, C])

        ps = ctx.enter_context(nc.psum_tensor("ps", [P, 8 * BANK], F32))

        def bank(n, a=0, b=BANK):
            return ps[:, n * BANK + a:n * BANK + b]

        consts_in = sig("consts_in", 0)
        setup = sig("setup", 0)
        ready = sig("ready", 0)
        fm_in = [sig(f"fm_in{n}", 16 * NCH) for n in range(2)]
        rows_ps = sig("rows_ps", 4 * NCH, 16)
        rows_sb = sig("rows_sb", 4 * NCH)
        carry = sig("carry", NCH)
        table_in = [sig(f"table_in{n}", 32 * NCH // 2, 16) for n in range(2)]
        qf_ps, qf_sb = sig("qf_ps", NCH, 16), sig("qf_sb", NCH)
        qft_ps, qft_sb = sig("qft_ps", NCH), sig("qft_sb", NCH)
        proj_ps, proj_sb = sig("proj_ps", NCH), sig("proj_sb", NCH)
        off_u = sig("off_u", 1)
        off_e = sig("off_e", 1)
        off_h, off_ht = sig("off_h", 1), sig("off_ht", 1, 16)
        off_hsb, off_raw = sig("off_hsb", 1), sig("off_raw", 1)
        off_rd = sig("off_rd", 1)
        idx_ok = sig("idx_ok", 1, 16)
        corner_ok = sig("corner_ok", 1)
        gath_in = [sig(f"gath_in{n}", 2 * 16 * NP_) for n in range(NG)]
        gath_rd = sig("gath_rd", 2 * QT_N, 3 * NG)
        wcorn = sig("wcorn", 4 * QT_N)
        samp_ps = sig("samp_ps", 4 * QT_N, 16)
        samp_sb = sig("samp_sb", 4 * QT_N)
        kv_ps = sig("kv_ps", 2 * QT_N, 16)
        sc_sub = sig("sc_sub", 2 * QT_N)
        sc_exp = sig("sc_exp", 2 * QT_N)
        kv_rd = sig("kv_rd", 4 * QT_N)
        tok = sig("tok", 2 * QT_N)
        txt_in = [sig(f"txt_in{n}", 16) for n in range(2)]
        ln_ab = sig("ln_ab", 6)
        ln_x = sig("ln_x", 6)
        ln_hi = sig("ln_hi", 4)
        ln_lo = sig("ln_lo", 4)
        xt_ps = sig("xt_ps", 4 * 3)
        xt_sb = sig("xt_sb", 4 * 3)
        q_ps, q_sb = sig("q_ps", 6), sig("q_sb", 6)
        k_ps, k_sb = sig("k_ps", 6), sig("k_sb", 6)
        v_ps, v_cp = sig("v_ps", 2), sig("v_cp", 4)
        s_ps = sig("s_ps", 2 * ST_N)
        s_max = sig("s_max", 2 * ST_N)
        s_exp = sig("s_exp", 2 * ST_N)
        PTB = sum((i + 4) // 4 for i in range(ST_N))
        p_ps, p_sb = sig("p_ps", 2 * PTB), sig("p_sb", 2 * PTB)
        o_ps, o_rd = sig("o_ps", 2 * ST_N), sig("o_rd", 2 * ST_N)
        gate_ps = sig("gate_ps", 2)
        gate_d = sig("gate_d", 2)
        gate_e = sig("gate_e", 2)
        z_ps, z_sb = sig("z_ps", 2 * NCC * E), sig("z_sb", 2 * NCC * E, 16)
        y_ps = sig("y_ps", 2 * NCC * 2 * CC)
        y_rd = sig("y_rd", 2 * NCC * 2 * CC, 16)
        out_ok = sig("out_ok", 2)
        stored = sig("stored", 32, 16)
        spare_rows = sig("spare_rows", 0)
        vec = ctx.enter_context(nc.semaphore("vec"))
        act_own = ctx.enter_context(nc.semaphore("act_own"))
        pool_gate = ctx.enter_context(nc.semaphore("pool_gate"))
        dve_gate = ctx.enter_context(nc.semaphore("dve_gate"))

        loads = [0]

        block = ctx.enter_context(nc.Block())

        def drive(eng, grid, work):
            grid(Pair(0), 0)
            with eng.Fori(0, PAIRS // 2 - 1) as j:
                work(Pair(0, eng, j), 0, True)
                work(Pair(1, eng, j), 1, True)
            work(Pair(PAIRS - 2), 0, True)
            work(Pair(PAIRS - 1), 1, False)

        x_v = x.rearrange("(n b) c (m r) w -> n (b c) m (r w)", b=2, r=HR)
        tab_v = [t.rearrange("(b y x) c -> b y x c", y=H, x=W) for t in tables]
        out_v = out.rearrange("b (t p) c -> b p t c", p=P)

        @block.sync
        def _(sp):
            def load(dst, src):
                loads[0] += 1
                sp.dma_start(dst, src).then_inc(consts_in.sem, 16)

            sp.wait_ge(*setup.rise(Pair(0), 1))
            load(const[:], w["const"])
            for b in range(2):
                r, c0 = slice(64 * b, 64 * b + 64), b * (C + O1W)
                load(w_proj[r, c0:c0 + C], w["Wq_t"])
                load(w_proj[r, c0 + C:c0 + C + O1W], w["W_o1"])
                load(w_kv[r, 0:C], w["Wk_t"])
                load(w_kv[r, C:2 * C], w["Wv_t"])
                load(fm[r, 0, 0:C], w["aWq"])
                load(fm[r, 0, 128:128 + C], w["aWk"])
                load(fm[r, 0, 256:256 + C], w["aWv"])
                load(fm[r, 1, 0:E], w["gate_w"])
                load(gath[r, 0:1].rearrange("p a b c -> p (a b c)").rearrange("p (e f) -> p e f", f=F),
                     w["w1"].rearrange("e c f -> c e f"))
            for g in range(8):
                load(w_o2[16 * g:16 * g + 16, 16 * g:16 * g + 16], w["W_o2"])
            for n, name in enumerate(("b_o1", "ln_g", "ln_b", "b_o2", "gate_b")):
                load(rows16[:, n, :], w[name].unsqueeze(0).to_broadcast([P, 16]))
            for n, name in enumerate(("abv", "gamma", "beta")):
                load(rows64[:, n, :], w[name].unsqueeze(0).to_broadcast([P, C]))
            load(bqk[0:C, 0:1], w["abq"].unsqueeze(1))
            load(bqk[0:C, 1:2], w["abk"].unsqueeze(1))
            load(b1[:], w["b1_t"])
            load(w2[:].rearrange("p (e c) -> p e c", c=C), w["w2"].rearrange("e f c -> f e c"))
            for r in (0, 32):
                load(xn[r:r + 1].rearrange("p t c -> p (t c)")[:, 0:C * 8],
                     w["b2"].rearrange("e c -> (e c)").unsqueeze(0)[:, 0:C * 8])
                load(out_sb[r:r + 1].rearrange("p t c -> p (t c)")[:, 0:C * 8],
                     w["b2"].rearrange("e c -> (e c)").unsqueeze(0)[:, C * 8:C * 16])

            def load_rows(pair, hc):
                if hc >= 2:
                    sp.wait_ge(*rows_ps.rise(pair, 2 * (hc - 1)))
                else:
                    sp.wait_ge(*rows_ps.rise(pair - 1, 4 * NCH - 2 * (1 - hc)))
                sp.dma_start(fm[:, hc % 2, :], x_v[pair.times(1), :, hc, :]).then_inc(fm_in[hc % 2].sem, 16)

            def write_table(pair, par, ch):
                sp.wait_ge(*rows_sb.rise(pair, 4 * (ch + 1)))
                sp.wait_ge(*carry.rise(pair, ch + 1))
                if ch == 0:
                    sp.wait_ge(*gath_rd.rise(pair - 2, 2 * QT_N))
                n = CR if ch else CR - 1
                first = 0 if ch else 1
                y0 = ch * CR + first - 1
                for b in range(2):
                    src = rows[:, ch % 2, b, first:first + n, :]
                    src = bass.AP(tensor=src.tensor, offset=src.offset,
                                  ap=[list(src.ap[0]), [C, n], [1, 2 * C]])
                    dst = tab_v[par][b, y0:y0 + n].rearrange("y x c -> x y c")
                    sp.dma_start(dst, src).then_inc(table_in[ch % 2].sem, 16)

            def grid(pair, par):
                for ch in range(NCH):
                    load_rows(pair, 2 * ch)
                    load_rows(pair, 2 * ch + 1)
                    if ch:
                        write_table(pair, par, ch - 1)
                write_table(pair, par, NCH - 1)

            def text(pair, b):
                sp.wait_ge(*stored.rise(pair - 1, 32))
                sp.dma_start(h0[:, b, QT_N, :], txt[pair.times(2, b)]).then_inc(txt_in[b].sem, 16)

            def store(pair, b):
                sp.wait_ge(*out_ok.rise(pair, b + 1))
                sp.dma_start(out_v[pair.times(2, b)], out_sb[:]).then_inc(stored.sem, 16)

            def work(pair, par, more):
                text(pair, 0)
                text(pair, 1)
                if more:
                    grid(pair + 1, 1 - par)
                store(pair, 0)
                store(pair, 1)

            for t in tab_v:
                for b in range(2):
                    sp.dma_start(t[b, H - 1, :, :], shared[:, 0:2 * C]).then_inc(spare_rows.sem, 16)
            sp.wait_ge(*ready.rise(Pair(0), 1))
            drive(sp, grid, work)
            sp.wait_ge(*stored.rise(Pair(PAIRS), 0))

        @block.gpsimd
        def _(pool):
            pool.wait_ge(*setup.rise(Pair(0), 2))
            pool.wait_ge(*spare_rows.rise(Pair(0), 64))

            def work(pair, par, more):
                pool.wait_ge(*idx_ok.rise(pair, 1))
                for n in range(2):
                    pool.wait_ge(*table_in[n].rise(pair, 32 * NCH // 2))
                for b in range(2):
                    for t in range(QT_N):
                        pool.wait_ge(*gath_rd.rise(pair, b * QT_N + t + 1 - NG))
                        pool.sem_inc(pool_gate, 1)
                        for p in range(NP_):
                            k = (t * 2 + b) * NP_ + p
                            pool.indirect_dma_start(
                                out=gath[:, t % NG, p, :], out_offset=None, in_=tables[par],
                                in_offset=bass.IndirectOffsetOnAxis(ap=idx[:, par, k:k + 1], axis=0),
                            ).then_inc(gath_in[t % NG].sem, 16)

            drive(pool, lambda pair, par: None, work)

        @block.tensor
        def _(pe):
            def grid_rows(pair, ch, half):
                slot = half
                pe.wait_ge(*fm_in[slot].rise(pair, 16 * (ch + 1)))
                for g in range(2):
                    n = 4 * ch + 2 * half + g
                    if n >= 2:
                        pe.wait_ge(*rows_sb.rise(pair, n - 1))
                    for r in range(4):
                        last = pe.transpose(bank(4 + g, r * P, r * P + P),
                                            fm[:, slot, (4 * g + r) * W:(4 * g + r + 1) * W], ident)
                    last.then_inc(rows_ps.sem, 1)

            def grid_sample(pair, t):
                pe.wait_ge(*rows_sb.rise(pair, 4 * (t + 1)))
                if t:
                    pe.wait_ge(*proj_sb.rise(pair, t))
                for i in range(4 * t, 4 * t + 4):
                    for k in range(2):
                        r = 1 + int(LOW[i]) + k - CR * t
                        assert 1 <= r <= CR
                        last = pe.matmul(bank(6, 0, P)[32 * (i % 4):32 * (i % 4) + 32],
                                         gridw[:, i, k, :], rows[:, t % 2, :, r, :],
                                         start=(k == 0), stop=(k == 1))
                last.then_inc(qf_ps.sem, 1)

            def grid_turn(pair, t):
                pe.wait_ge(*qf_sb.rise(pair, t + 1))
                if t:
                    pe.wait_ge(*qft_sb.rise(pair, t))
                pe.transpose(bank(6, 128, 256), qf[:], ident).then_inc(qft_ps.sem, 1)

            def grid_project(pair, t):
                pe.wait_ge(*qft_sb.rise(pair, t + 1))
                if t:
                    pe.wait_ge(*proj_sb.rise(pair, t))
                pe.matmul(bank(6, 256, 256 + 2 * (C + O1W)), qft[:], w_proj[:],
                          start=True, stop=True).then_inc(proj_ps.sem, 1)

            def grid_offsets(pair):
                pe.wait_ge(*off_h.rise(pair, 1))
                for n in range(2):
                    last = pe.transpose(bank(7, n * P, n * P + P),
                                        oa[:].rearrange("p g c -> p (g c)")[:, n * P:n * P + P], ident)
                last.then_inc(off_ht.sem, 1)
                pe.wait_ge(*off_hsb.rise(pair, 1))
                for n in range(2):
                    last = pe.matmul(bank(7, 256 + n * P, 256 + n * P + P), oht[:, n, :], w_o2[:],
                                     start=True, stop=True)
                last.then_inc(off_raw.sem, 1)

            def grid(pair, par):
                for t in range(NCH):
                    grid_rows(pair, t, 0)
                    grid_rows(pair, t, 1)
                    grid_sample(pair, t)
                    grid_turn(pair, t)
                    grid_project(pair, t)
                grid_offsets(pair)

            def tok_turn(pair, n):
                for h in range(2):
                    pe.wait_ge(*wcorn.rise(pair, 2 * n + h + 1))
                    if n:
                        pe.wait_ge(*samp_sb.rise(pair, 2 * (n - 1) + h + 1))
                    for p in range(4):
                        for dx in range(2):
                            last = pe.matmul(bank(h, p * P, p * P + P),
                                             prod[h][:, (p * 2 + dx) * P:(p * 2 + dx + 1) * P], ident,
                                             is_transpose=True, start=(dx == 0), stop=(dx == 1))
                    last.then_inc(samp_ps.sem, 1)

            def tok_kv(pair, n):
                for h in range(2):
                    pe.wait_ge(*samp_sb.rise(pair, 2 * n + h + 1))
                    if n:
                        pe.wait_ge(*kv_rd.rise(pair, 2 * (n - 1) + h + 1))
                    for p in range(4):
                        last = pe.matmul(bank(2 + h, p * P, p * P + P),
                                         samp_t[n % 2][:, (4 * h + p) * P:(4 * h + p + 1) * P], w_kv[:],
                                         start=True, stop=True)
                last.then_inc(kv_ps.sem, 1)

            def tokenize(pair, b, more):
                if b == 0:
                    pe.wait_ge(*y_rd.rise(pair - 1, 2 * NCC * 2 * CC))
                    pe.wait_ge(*z_sb.rise(pair - 1, 2 * NCC * E))
                else:
                    pe.wait_ge(*y_rd.rise(pair, NCC * 2 * CC))
                    pe.wait_ge(*z_sb.rise(pair, NCC * E))
                side = more and b == 0
                for t in range(QT_N):
                    n = b * QT_N + t
                    if side:
                        grid_rows(pair + 1, t, 0)
                    tok_turn(pair, n)
                    if side:
                        if t:
                            grid_turn(pair + 1, t - 1)
                        grid_rows(pair + 1, t, 1)
                        if t:
                            grid_project(pair + 1, t - 1)
                    tok_kv(pair, n)
                    if side:
                        grid_sample(pair + 1, t)
                if side:
                    grid_turn(pair + 1, NCH - 1)
                    grid_project(pair + 1, NCH - 1)

            def turn_tokens(pair, m, banks):
                pe.wait_ge(*ln_hi.rise(pair, m + 1))
                pe.wait_ge(*ln_lo.rise(pair, m + 1))
                for c in range(3):
                    for j in range(3):
                        t = 3 * c + j
                        last = pe.transpose(bank(banks[c], j * P, j * P + P),
                                            xs[:, t].rearrange("p h c -> p (h c)").bitcast(F32), ident)
                    last.then_inc(xt_ps.sem, 1)

            def split(dst, lhs, rhs, start=True, stop=True):
                for n in range(2):
                    a = lhs[n] if isinstance(lhs, tuple) else lhs
                    r = rhs[n] if isinstance(rhs, tuple) else rhs
                    last = pe.matmul(dst, a, r, start=start and n == 0, stop=stop and n == 1)
                return last

            def project_qkv(pair, b):
                CW = 3 * P
                for c in range(3):
                    pe.wait_ge(*xt_sb.rise(pair, 6 * b + c + 1))
                    split(bank(3 + c, 0, CW), (wa_h[:, 0:P], wa_l[:, 0:P]),
                          xt[:, c * CW:(c + 1) * CW]).then_inc(q_ps.sem, 1)
                for c in range(3):
                    split(bank((6, 7, 0)[c], 0, CW), (wa_h[:, P:2 * P], wa_l[:, P:2 * P]),
                          xt[:, c * CW:(c + 1) * CW]).then_inc(k_ps.sem, 1)
                for t in range(ST_N):
                    last = split(bank(1 + t // 8, (t % 8) * C, (t % 8) * C + C), xt[:, t * P:(t + 1) * P],
                                 (wa_h[:, 2 * P:2 * P + C], wa_l[:, 2 * P:2 * P + C]))
                last.then_inc(v_ps.sem, 1)

            def scores(pair, b, i):
                if i == 0:
                    pe.wait_ge(*q_sb.rise(pair, 3 * b + 3))
                    pe.wait_ge(*k_sb.rise(pair, 3 * b + 3))
                if i >= 2:
                    pe.wait_ge(*s_exp.rise(pair, ST_N * b + i - 1))
                n = (i + 1) * P
                for a in range(0, n, BANK):
                    m = min(n - a, BANK)
                    last = pe.matmul(bank(3 if i % 2 == 0 else 6, a, a + m), q_t[:, i * P:(i + 1) * P],
                                     k_t[:, a:a + m], start=True, stop=True)
                last.then_inc(s_ps.sem, 1)

            def first_bank(i):
                return sum((k + 4) // 4 for k in range(i))

            def attend(pair, b, i):
                pe.wait_ge(*s_exp.rise(pair, ST_N * b + i + 1))
                if i == 0:
                    pe.wait_ge(*v_cp.rise(pair, 2 * b + 2))
                for k in range(i + 1):
                    n = b * PTB + first_bank(i) + k // 4
                    if k % 4 == 0 and n - b * PTB >= 2:
                        pe.wait_ge(*p_sb.rise(pair, n - 1))
                    last = pe.transpose(bank(1 + n % 2, (k % 4) * P, (k % 4) * P + P),
                                        probs[i % 2][:, k * P:(k + 1) * P], ident)
                    if k % 4 == 3 or k == i:
                        last.then_inc(p_ps.sem, 1)

            def weigh(pair, b, i):
                if i:
                    pe.wait_ge(*o_rd.rise(pair, ST_N * b + i))
                for k in range(i + 1):
                    if k % 4 == 0:
                        pe.wait_ge(*p_sb.rise(pair, b * PTB + first_bank(i) + k // 4 + 1))
                    last = pe.matmul(bank(0, (i % 8) * C, (i % 8) * C + C),
                                     probs_t[i % 2][:, k * P:(k + 1) * P], v_sb[:, k, :],
                                     start=(k == 0), stop=(k == i))
                last.then_inc(o_ps.sem, 1)

            def experts(pair, b, side):
                turn_tokens(pair, 2 * b + 1, (5, 6, 7))
                pe.wait_ge(*xt_sb.rise(pair, 6 * b + 6))
                for t in range(ST_N):
                    last = split(bank(4, t * E, t * E + E), xt[:, t * P:(t + 1) * P], (wg_h[:], wg_l[:]))
                last.then_inc(gate_ps.sem, 1)
                if side:
                    grid_offsets(pair + 1)

                def layer1(n):
                    c, e = n // E, n % E
                    if n >= 2:
                        pe.wait_ge(*z_sb.rise(pair, b * NCC * E + n - 1))
                    elif n == 1:
                        pe.wait_ge(*gate_d.rise(pair, b + 1))
                    split(bank(3 + n % 2, 0, CC * P), (w1_h[:, e * F:(e + 1) * F], w1_l[:, e * F:(e + 1) * F]),
                          xt[:, c * CC * P:(c + 1) * CC * P]).then_inc(z_ps.sem, 1)

                def layer2(n):
                    c, e = n // E, n % E
                    half = e // EH
                    for j in range(CC):
                        if e % EH == 0:
                            u = b * NCC * 2 * CC + (c * 2 + half) * CC + j
                            if c or half:
                                pe.wait_ge(*y_rd.rise(pair, u - CC + 1))
                            pe.matmul(bank(j), ones_r[:], b2_hl[:, half * BANK:(half + 1) * BANK],
                                      start=True, stop=False, skip_group_check=True)
                        if j == 0:
                            pe.wait_ge(*z_sb.rise(pair, b * NCC * E + n + 1))
                        last = pe.matmul(bank(j, (e % EH) * C, (e % EH + 1) * C), hid[n % 3][:, j * P:(j + 1) * P],
                                         w2[:, e * C:(e + 1) * C], start=False, stop=(e % EH == EH - 1),
                                         skip_group_check=True)
                        if e % EH == EH - 1:
                            last.then_inc(y_ps.sem, 1)

                layer1(0)
                layer1(1)
                for n in range(2, NCC * E):
                    layer2(n - 2)
                    layer1(n)
                layer2(NCC * E - 2)
                layer2(NCC * E - 1)

            def work(pair, par, more):
                for b in range(2):
                    tokenize(pair, b, more)
                    turn_tokens(pair, 2 * b, (0, 1, 2))
                    project_qkv(pair, b)
                    scores(pair, b, 0)
                    for i in range(ST_N):
                        if i + 1 < ST_N:
                            scores(pair, b, i + 1)
                        attend(pair, b, i)
                        if i:
                            weigh(pair, b, i - 1)
                    weigh(pair, b, ST_N - 1)
                    experts(pair, b, more and b == 0)

            pe.wait_ge(*consts_in.rise(Pair(0), 16 * loads[0]))
            pe.wait_ge(*setup.rise(Pair(0), 3))
            pe.wait_ge(*ready.rise(Pair(0), 1))
            drive(pe, grid, work)

        @block.scalar
        def _(act):
            def copy(dst, src):
                return act.activation(dst, src, ACT.Copy)

            def grid_rows(pair, ch, half):
                for g in range(2):
                    n = 4 * ch + 2 * half + g
                    if half == 0 and g == 0:
                        if ch >= 2:
                            act.wait_ge(*qf_ps.rise(pair, ch - 1))
                            act.wait_ge(*table_in[ch % 2].rise(pair, 32 * (ch // 2)))
                        else:
                            act.wait_ge(*qf_ps.rise(pair - 1, NCH - 1 + ch))
                            act.wait_ge(*table_in[ch % 2].rise(pair - 1, 32 * NCH // 2))
                        if ch:
                            act.wait_ge(*rows_sb.rise(pair, 4 * ch))
                            c = copy(rows[:, ch % 2, :, 0, :], rows[:, 1 - ch % 2, :, CR, :])
                            c.then_inc(carry.sem, 1)
                    act.wait_ge(*rows_ps.rise(pair, n + 1))
                    r0 = 1 + HR * half + 4 * g
                    copy(rows[:, ch % 2, :, r0:r0 + 4, :].rearrange("p b r c -> p r b c"),
                         bank(4 + g).rearrange("p (r b c) -> p r b c", r=4, b=2)).then_inc(rows_sb.sem, 1)
                if ch == 0 and half == 1:
                    act.sem_inc(carry.sem, 1)

            def grid_feature(pair, t):
                act.wait_ge(*qf_ps.rise(pair, t + 1))
                if t:
                    act.wait_ge(*qft_ps.rise(pair, t))
                copy(qf[:], bank(6, 0, P)).then_inc(qf_sb.sem, 1)

            def grid_turn(pair, t):
                act.wait_ge(*qft_ps.rise(pair, t + 1))
                if t:
                    act.wait_ge(*proj_ps.rise(pair, t))
                copy(qft[:], bank(6, 128, 256)).then_inc(qft_sb.sem, 1)

            def grid_project(pair, par, t):
                act.wait_ge(*proj_ps.rise(pair, t + 1))
                src = bank(6, 256, 256 + 2 * (C + O1W)).rearrange("p (b c) -> p b c", b=2)
                if t == 0:
                    act.wait_ge(*idx_ok.rise(pair - 1, 1))
                copy(query[:, par, t], src[:, :, 0:C])
                copy(o1[:, 2 * t:2 * t + 2], src[:, :, C:C + O1W]).then_inc(proj_sb.sem, 1)

            def grid_gelu(pair):
                act.wait_ge(*off_u.rise(pair, 1))
                act.activation(ob[:], ob[:], ACT.Exp, scale=-2.0 * (2.0 / np.pi) ** 0.5).then_inc(off_e.sem, 1)

            def grid_offsets(pair):
                act.wait_ge(*off_ht.rise(pair, 1))
                copy(oht[:].rearrange("p a b -> p (a b)"), bank(7, 0, 2 * P)).then_inc(off_hsb.sem, 1)

            def grid(pair, par):
                for t in range(NCH):
                    grid_rows(pair, t, 0)
                    grid_rows(pair, t, 1)
                    grid_feature(pair, t)
                    grid_turn(pair, t)
                    grid_project(pair, par, t)
                grid_gelu(pair)
                grid_offsets(pair)

            def tok_copy(pair, n):
                for h in range(2):
                    act.wait_ge(*samp_ps.rise(pair, 2 * n + h + 1))
                    if h == 0:
                        if n >= 2:
                            act.wait_ge(*kv_ps.rise(pair, n - 1))
                        else:
                            act.wait_ge(*kv_ps.rise(pair - 1, 2 * QT_N))
                    copy(samp_t[n % 2][:, h * BANK:(h + 1) * BANK], bank(h)).then_inc(samp_sb.sem, 1)

            def tok_exp(pair, n):
                act.wait_ge(*sc_sub.rise(pair, n + 1))
                act.activation(pt_sc[:, 2 + n % 2], pt_sc[:, 1], ACT.Exp, scale=QK_SCALE).then_inc(sc_exp.sem, 1)

            def tokenize(pair, par, b, more):
                side = more and b == 0
                for t in range(QT_N):
                    n = b * QT_N + t
                    if side:
                        grid_rows(pair + 1, t, 0)
                    tok_copy(pair, n)
                    if side:
                        if t:
                            grid_turn(pair + 1, t - 1)
                        grid_rows(pair + 1, t, 1)
                        if t:
                            grid_project(pair + 1, 1 - par, t - 1)
                        grid_feature(pair + 1, t)
                    tok_exp(pair, n)
                if side:
                    grid_turn(pair + 1, NCH - 1)
                    grid_project(pair + 1, 1 - par, NCH - 1)

            def normalize(pair, m, src, dst):
                act.wait_ge(*ln_ab.rise(pair, m + 1))
                for t in range(ST_N):
                    last = act.activation(dst[:, t, :], src[:, t, :], ACT.Identity,
                                          scale=ln9[:, 6, t:t + 1], bias=ln9[:, 7, t:t + 1])
                last.then_inc(ln_x.sem, 1)

            def halves(pair, b, k):
                m = 2 * b + k
                act.wait_ge(*ln_x.rise(pair, 3 * b + k + 1))
                act.activation(xs[:, :, 0, :], xn[:], ACT.Copy).then_inc(ln_hi.sem, 1)
                for c in range(3):
                    act.wait_ge(*xt_ps.rise(pair, 3 * m + c + 1))
                    copy(xt[:, c * 3 * P:(c + 1) * 3 * P], bank((0, 5)[k] + c, 0, 3 * P)).then_inc(xt_sb.sem, 1)

            def copy_qkv(pair, b):
                CW = 3 * P
                for c in range(3):
                    act.wait_ge(*q_ps.rise(pair, 3 * b + c + 1))
                    act.activation(q_t[:, c * CW:(c + 1) * CW], bank(3 + c, 0, CW), ACT.Identity,
                                   bias=bqk[:, 0:1]).then_inc(q_sb.sem, 1)
                for c in range(3):
                    act.wait_ge(*k_ps.rise(pair, 3 * b + c + 1))
                    act.activation(k_t[:, c * CW:(c + 1) * CW], bank((6, 7, 0)[c], 0, CW), ACT.Identity,
                                   bias=bqk[:, 1:2]).then_inc(k_sb.sem, 1)
                act.wait_ge(*v_ps.rise(pair, b + 1))
                vf = v_sb[:].rearrange("p t c -> p (t c)")
                copy(vf[:, 0:BANK], bank(1)).then_inc(v_cp.sem, 1)
                copy(vf[:, BANK:BANK + C], bank(2, 0, C)).then_inc(v_cp.sem, 1)

            def soft(pair, b, i):
                act.wait_ge(*s_max.rise(pair, ST_N * b + i + 1))
                n = (i + 1) * P
                act.activation(probs[i % 2][:, 0:n], bank(3 if i % 2 == 0 else 6, 0, n), ACT.Exp,
                               bias=att[:, 1, i:i + 1], scale=ATT_SCALE,
                               accum_out=att[:, 2, i:i + 1]).then_inc(s_exp.sem, 1)

            def turned(pair, b, i):
                for k in range(0, i + 1, 4):
                    n = b * PTB + sum((q + 4) // 4 for q in range(i)) + k // 4
                    m = min(4, i + 1 - k) * P
                    act.wait_ge(*p_ps.rise(pair, n + 1))
                    if k == 0 and i >= 2:
                        act.wait_ge(*o_ps.rise(pair, ST_N * b + i - 1))
                    copy(probs_t[i % 2][:, k * P:k * P + m], bank(1 + n % 2, 0, m)).then_inc(p_sb.sem, 1)

            def experts(pair, b, side):
                if side:
                    grid_offsets(pair + 1)
                act.wait_ge(*gate_d.rise(pair, b + 1))
                act.activation(gs[:, 3, :], gs[:, 2, :], ACT.Exp).then_inc(gate_e.sem, 1)
                for n in range(NCC * E):
                    u = b * NCC * E + n
                    act.wait_ge(*z_ps.rise(pair, u + 1))
                    if n % EH == 3 and n > EH:
                        act.wait_ge(*y_ps.rise(pair, b * NCC * 2 * CC + (n // EH) * CC))
                    act.activation(hid[n % 3], bank(3 + n % 2, 0, CC * P), ACT.Relu,
                                   bias=b1[:, n % E:n % E + 1]).then_inc(z_sb.sem, 1)

            def work(pair, par, more):
                for b in range(2):
                    tokenize(pair, par, b, more)
                    normalize(pair, 3 * b, h0[:, b], xn)
                    halves(pair, b, 0)
                    copy_qkv(pair, b)
                    if more and b == 0:
                        grid_gelu(pair + 1)
                    soft(pair, b, 0)
                    for i in range(ST_N):
                        if i + 1 < ST_N:
                            soft(pair, b, i + 1)
                        turned(pair, b, i)
                    normalize(pair, 3 * b + 1, h1, xn)
                    halves(pair, b, 1)
                    experts(pair, b, more and b == 0)
                    normalize(pair, 3 * b + 2, xn, out_sb)

            act.wait_ge(*consts_in.rise(Pair(0), 16 * loads[0]))
            act.wait_ge(*setup.rise(Pair(0), 1))
            copy(wa_h[:], fm[:, 0, 0:NATT])
            copy(wg_h[:], fm[:, 1, 0:E])
            copy(b2_hl[:, 0:BANK], xn[:].rearrange("p t c -> p (t c)")[:, 0:BANK])
            copy(b2_hl[:, BANK:2 * BANK], out_sb[:].rearrange("p t c -> p (t c)")[:, 0:BANK])
            copy(w1_h[:], gath[:, 0].rearrange("p a b -> p (a b)")).then_inc(act_own, 1)
            act.wait_ge(*setup.rise(Pair(0), 3))
            act.sem_inc(ready.sem, 1)
            drive(act, grid, work)

        @block.vector
        def _(dve):
            steps = [0]
            base = [None]
            head = [0]

            def step(ins):
                steps[0] += 1
                ins.then_inc(vec, 1)

            def settle():
                dve.wait_ge(vec, steps[0] if base[0] is None else base[0].times(STEPS[1], head[0] + steps[0]))

            def own(ins):
                step(ins)
                settle()

            def tt(o, a, b, op):
                return dve.tensor_tensor(o, a, b, op)

            def ts(o, a, s1, op1, s2=None, op2=None):
                if op2 is None:
                    return dve.tensor_scalar(o, a, s1, None, op1)
                return dve.tensor_scalar(o, a, s1, s2, op1, op2)

            def stt(o, a, s, b, op0, op1):
                return dve.scalar_tensor_tensor(out=o, in0=a, scalar=s, in1=b, op0=op0, op1=op1)

            def red(o, a, op=ALU.add):
                return dve.tensor_reduce(o, a, X_AXIS, op)

            def rsqrt(r, v, t, h):
                step(ts(t.bitcast(I32), v.bitcast(I32), 1, ALU.logical_shift_right))
                own(ts(h, v, -0.5, ALU.mult))
                own(ts(r.bitcast(I32), t.bitcast(I32), -1.0, ALU.mult, RSQRT_SEED, ALU.add))
                for _ in range(3):
                    own(tt(t, r, r, ALU.mult))
                    own(tt(t, t, h, ALU.mult))
                    own(stt(r, t, 1.5, r, ALU.add, ALU.mult))

            def bc16(v):
                return v.unsqueeze(2).to_broadcast([P, GROUPS, O1W])

            def row16(v):
                return v.unsqueeze(1).to_broadcast([P, GROUPS, O1W])

            def off_hidden(pair):
                dve.wait_ge(*proj_sb.rise(pair, NCH))
                dve.wait_ge(*off_ht.rise(pair - 1, 1))
                own(tt(oa[:], o1[:], row16(bo1), ALU.add))
                own(red(st16[:, 0], oa[:]))
                own(stt(oa[:], bc16(st16[:, 0]), -1.0 / O1W, oa[:], ALU.mult, ALU.add))
                own(tt(ob[:], oa[:], oa[:], ALU.mult))
                own(red(st16[:, 0], ob[:]))
                own(ts(st16[:, 1], st16[:, 0], 1.0 / O1W, ALU.mult, EPS, ALU.add))
                rsqrt(st16[:, 2], st16[:, 1], st16[:, 3], st16[:, 4])
                own(tt(oa[:], oa[:], bc16(st16[:, 2]), ALU.mult))
                own(tt(oa[:], oa[:], row16(lng), ALU.mult))
                own(tt(oa[:], oa[:], row16(lnb), ALU.add))
                own(tt(ob[:], oa[:], oa[:], ALU.mult))
                own(ts(ob[:], ob[:], 0.044715, ALU.mult, 1.0, ALU.add))
                own(tt(ob[:], ob[:], oa[:], ALU.mult))
                ts(ob[:], ob[:], -50.0, ALU.max).then_inc(off_u.sem, 1)

            def off_gelu(pair):
                dve.wait_ge(*off_e.rise(pair, 1))
                own(ts(ob[:], ob[:], 1.0, ALU.add))
                own(dve.reciprocal(ob[:], ob[:]))
                tt(oa[:], oa[:], ob[:], ALU.mult).then_inc(off_h.sem, 1)

            def off_points(pair, par):
                dve.wait_ge(*off_raw.rise(pair, 1))
                xy = base_xy[:].rearrange("p g n k -> p (g n k)")
                caf, cbf = (v.rearrange("p n k -> p (n k)") for v in (ca, cb))
                stt(caf, bank(7, 256, 512), 4.0, xy, ALU.mult, ALU.add).then_inc(off_rd.sem, 1)
                dve.wait_ge(*off_rd.rise(pair, 1))
                own(ts(caf, caf, 0.0, ALU.max, float(W - 1), ALU.min))
                own(ts(cbf, caf, RNE, ALU.add, RNE, ALU.subtract))
                f1 = frac2[:].rearrange("p n k s -> p (n k) s")
                own(tt(f1[:, :, 0], cbf, caf, ALU.is_gt))
                own(stt(cbf, f1[:, :, 0], -1.0, cbf, ALU.mult, ALU.add))
                own(ts(cbf, cbf, float(W - 2), ALU.min))
                own(stt(f1[:, :, 1], cbf, -1.0, caf, ALU.mult, ALU.add))
                step(ts(f1[:, :, 0], f1[:, :, 1], -1.0, ALU.mult, 1.0, ALU.add))
                idf = idxf.rearrange("p g n -> p (g n)")
                own(stt(idf, cb[:, :, 1], float(W), cb[:, :, 0], ALU.mult, ALU.add))
                base_t = table_base[:].unsqueeze(1).unsqueeze(3).to_broadcast([P, QT_N, 2, NP_])
                tt(idx[:, par].rearrange("p (t b n) -> p t b n", t=QT_N, b=2),
                        idxf.rearrange("p (t b) n -> p t b n", b=2), base_t, ALU.add).then_inc(idx_ok.sem, 1)
                cw = corner_w[:, par].rearrange("p g (n x y) -> p (g n) x y", x=2, y=2)
                n = GROUPS * NP_
                tt(cw, frac2[:, :, 0, :].unsqueeze(3).to_broadcast([P, n, 2, 2]),
                        frac2[:, :, 1, :].unsqueeze(2).to_broadcast([P, n, 2, 2]), ALU.mult).then_inc(corner_ok.sem, 1)

            def tok_weigh(pair, par, b, t):
                n = b * QT_N + t
                dve.wait_ge(*gath_in[t % NG].rise(pair, 16 * NP_ * (b + 1)))
                if t == 0 and b == 0:
                    dve.wait_ge(*corner_ok.rise(pair, 1))
                for h in range(2):
                    if n:
                        dve.wait_ge(*samp_ps.rise(pair, 2 * (n - 1) + h + 1))
                    else:
                        dve.wait_ge(*samp_ps.rise(pair - 1, 4 * QT_N))
                    g = gath[:, t % NG, 4 * h:4 * h + 4, :].rearrange("p n (k c) -> p (n k) c", c=C)
                    cw = corner_w[:, par, 2 * t + b, 16 * h:16 * h + 16]
                    ins = tt(prod[h].rearrange("p (n c) -> p n c", c=C), g,
                             cw.unsqueeze(2).to_broadcast([P, 16, C]), ALU.mult)
                    ins.then_inc(wcorn.sem, 1)
                dve.wait_ge(*wcorn.rise(pair, 2 * n + 2))
                dve.sem_inc(gath_rd.sem, 1)

            def tok_scores(pair, par, b, t):
                n = b * QT_N + t
                dve.wait_ge(*kv_ps.rise(pair, n + 1))
                kv = ps[:, 2 * BANK:4 * BANK].rearrange("p (n c) -> p n c", c=2 * C)
                q = query[:, par, t, b, :].unsqueeze(1).to_broadcast([P, NP_, C])
                own(tt(kq.rearrange("p (n c) -> p n c", c=C), kv[:, :, 0:C], q, ALU.mult))
                own(red(pt_sc[:, 0], kq.rearrange("p (m d) -> p m d", d=DH)))
                sc = pt_sc[:, 0].rearrange("p (n h) -> p n h", h=NH)
                own(red(pt_st[:, 0], sc.rearrange("p n h -> p h n"), ALU.max))
                if n:
                    dve.wait_ge(*sc_exp.rise(pair, n))
                tt(pt_sc[:, 1].rearrange("p (n h) -> p n h", h=NH), sc,
                   pt_st[:, 0].unsqueeze(1).to_broadcast([P, NP_, NH]), ALU.subtract).then_inc(sc_sub.sem, 1)

            def tok_values(pair, b, t):
                n = b * QT_N + t
                dve.wait_ge(*sc_exp.rise(pair, n + 1))
                ex = pt_sc[:, 2 + n % 2]
                step(red(pt_st[:, 1], ex.rearrange("p (n h) -> p h n", h=NH)))
                for h in range(2):
                    kv = bank(2 + h).rearrange("p (n c) -> p n c", c=2 * C)[:, :, C:2 * C]
                    e = ex[:, 32 * h:32 * h + 32]
                    tt(av[:, 256 * h:256 * h + 256].rearrange("p (m d) -> p m d", d=DH),
                       kv.rearrange("p n (h d) -> p n h d", d=DH),
                       e.rearrange("p (n h) -> p n h", h=NH).unsqueeze(3).to_broadcast([P, 4, NH, DH]),
                       ALU.mult).then_inc(kv_rd.sem, 1)
                settle()
                step(dve.reciprocal(pt_st[:, 2], pt_st[:, 1]))
                dve.wait_ge(*kv_rd.rise(pair, 2 * n + 2))
                own(red(pt_o[:], av.rearrange("p (n c) -> p c n", c=C)))
                tt(h0[:, b, t].rearrange("p (h d) -> p h d", d=DH), pt_o[:].rearrange("p (h d) -> p h d", d=DH),
                   pt_st[:, 2].unsqueeze(2).to_broadcast([P, NH, DH]), ALU.mult).then_inc(tok.sem, 1)

            def tokenize(pair, par, b):
                tok_weigh(pair, par, b, 0)
                for t in range(QT_N):
                    tok_scores(pair, par, b, t)
                    if t + 1 < QT_N:
                        tok_weigh(pair, par, b, t + 1)
                    tok_values(pair, b, t)

            def norm(pair, m, src, low):
                for t in range(ST_N):
                    step(dve.bn_stats(bn6[:, t, :], src[:, t, :]))
                settle()
                dve.sem_inc(dve_gate, 1)
                for t in range(ST_N):
                    step(dve.bn_aggr(mv[:, t, :], bn6[:, t, :]))
                settle()
                own(ts(ln9[:, 0], mv[:, :, 1], EPS, ALU.add))
                rsqrt(ln9[:, 6], ln9[:, 0], ln9[:, 1], ln9[:, 2])
                stt(ln9[:, 7], mv[:, :, 0], -1.0, ln9[:, 6], ALU.mult, ALU.mult).then_inc(ln_ab.sem, 1)
                if low is not None:
                    dve.wait_ge(*ln_hi.rise(pair, low + 1))
                    tt(xs[:, :, 1, :], xn[:], xs[:, :, 0, :].bitcast(F32), ALU.subtract).then_inc(ln_lo.sem, 1)

            def shift(pair, b, i):
                dve.wait_ge(*s_ps.rise(pair, ST_N * b + i + 1))
                n = i * P
                s = bank(3 if i % 2 == 0 else 6, 0, n + P)
                own(tt(s[:, n:n + P], s[:, n:n + P], mask, ALU.add))
                own(red(att[:, 0, i:i + 1], s, ALU.max))
                ts(att[:, 1, i:i + 1], att[:, 0, i:i + 1], -ATT_SCALE, ALU.mult).then_inc(s_max.sem, 1)

            def gather_heads(pair, b, i):
                dve.wait_ge(*s_exp.rise(pair, ST_N * b + i + 1))
                own(dve.reciprocal(att[:, 3, i:i + 1], att[:, 2, i:i + 1]))
                dve.wait_ge(*o_ps.rise(pair, ST_N * b + i + 1))
                ins = stt(h1[:, i, :], bank(0, (i % 8) * C, (i % 8) * C + C), att[:, 3, i:i + 1],
                          h0[:, b, i, :], ALU.mult, ALU.add)
                ins.then_inc(o_rd.sem, 1)

            def top2(pair, b):
                dve.wait_ge(*gate_ps.rise(pair, b + 1))
                rank = const[:, RANK:RANK + E].unsqueeze(1).to_broadcast([P, ST_N, E])

                def bc(v):
                    return v.unsqueeze(2).to_broadcast([P, ST_N, E])

                own(tt(lg[:, 0], bank(4, 0, ST_N * E).rearrange("p (t e) -> p t e", e=E),
                       gateb.unsqueeze(1).to_broadcast([P, ST_N, E]), ALU.add))
                for n in range(2):
                    own(red(gs[:, n], lg[:, n], ALU.max))
                    own(tt(lg[:, 4], lg[:, n], bc(gs[:, n]), ALU.is_equal))
                    own(tt(lg[:, 4], lg[:, 4], rank, ALU.mult))
                    own(red(gs[:, 5], lg[:, 4], ALU.max))
                    own(tt(lg[:, 2 + n], lg[:, 4], bc(gs[:, 5]), ALU.is_equal))
                    if n == 0:
                        own(stt(lg[:, 1], lg[:, 2], MASKED, lg[:, 0], ALU.mult, ALU.add))
                tt(gs[:, 2], gs[:, 1], gs[:, 0], ALU.subtract).then_inc(gate_d.sem, 1)

            def gates(pair, b):
                dve.wait_ge(*gate_e.rise(pair, b + 1))
                def bc(v):
                    return v.unsqueeze(2).to_broadcast([P, ST_N, E])
                own(ts(gs[:, 4], gs[:, 3], 1.0, ALU.add))
                own(dve.reciprocal(gs[:, 5], gs[:, 4]))
                own(tt(gs[:, 6], gs[:, 3], gs[:, 5], ALU.mult))
                step(tt(lg[:, 2], lg[:, 2], bc(gs[:, 5]), ALU.mult))
                own(tt(lg[:, 3], lg[:, 3], bc(gs[:, 6]), ALU.mult))
                own(tt(gate[:], lg[:, 2], lg[:, 3], ALU.add))

            def combine(pair, b):
                order = [(c * CC + j, half, j) for c in range(NCC) for half in range(2) for j in range(CC)]
                u0 = b * len(order)

                def add_up(n):
                    t, half, _ = order[n]
                    dve.wait_ge(*y_rd.rise(pair, u0 + n + 1))
                    step(red(moe[:, half, t, :], gated[n % 2].rearrange("p (e c) -> p c e", c=C)))

                for n, (t, half, j) in enumerate(order):
                    dve.wait_ge(*y_ps.rise(pair, u0 + n + 1))
                    settle()
                    tt(gated[n % 2].rearrange("p (e c) -> p e c", c=C),
                       bank(j).rearrange("p (e c) -> p e c", c=C),
                       gate[:, t, half * EH:(half + 1) * EH].unsqueeze(2).to_broadcast([P, EH, C]),
                       ALU.mult).then_inc(y_rd.sem, 1)
                    if n:
                        add_up(n - 1)
                add_up(len(order) - 1)
                settle()
                own(tt(xn[:], moe[:, 0], xn[:], ALU.add))
                own(tt(xn[:], moe[:, 1], xn[:], ALU.add))

            def finish(pair, b):
                def row(v):
                    return v.unsqueeze(1).to_broadcast([P, ST_N, C])
                dve.wait_ge(*ln_x.rise(pair, 3 * b + 3))
                own(tt(out_sb[:], out_sb[:], row(gamma), ALU.mult))
                own(tt(out_sb[:], out_sb[:], row(beta), ALU.add))
                tt(out_sb[:], out_sb[:], h1[:], ALU.add).then_inc(out_ok.sem, 1)

            def work(pair, par, more):
                for b in range(2):
                    tokenize(pair, par, b)
                    dve.wait_ge(*txt_in[b].rise(pair, 16))
                    dve.wait_ge(*tok.rise(pair, QT_N * (b + 1)))
                    norm(pair, 3 * b, h0[:, b], 2 * b)
                    own(tt(h0[:, b], h0[:, b], bv.unsqueeze(1).to_broadcast([P, ST_N, C]), ALU.add))
                    side = more and b == 0
                    if side:
                        off_hidden(pair + 1)
                    shift(pair, b, 0)
                    for i in range(ST_N):
                        if i + 1 < ST_N:
                            shift(pair, b, i + 1)
                        if i:
                            gather_heads(pair, b, i - 1)
                        if side and i == 2:
                            off_gelu(pair + 1)
                    gather_heads(pair, b, ST_N - 1)
                    dve.wait_ge(*o_rd.rise(pair, ST_N * (b + 1)))
                    norm(pair, 3 * b + 1, h1, 2 * b + 1)
                    top2(pair, b)
                    gates(pair, b)
                    if side:
                        off_points(pair + 1, 1 - par)
                    combine(pair, b)
                    dve.wait_ge(*stored.rise(pair, 16 * b))
                    norm(pair, 3 * b + 2, xn, None)
                    finish(pair, b)

            for v in (w_proj, w_o2, bqk, xn, out_sb):
                step(dve.memset(v[:], 0.0))
            step(dve.memset(fm[:], 0.0))
            step(dve.memset(shared[:, 0:P], 0.0))
            settle()
            step(dve.memset(shared[0:1, 0:P], 1.0))
            step(dve.memset(shared[32:33, 0:P], 1.0))
            for b in range(2):
                step(dve.memset(table_base[:, b:b + 1], float(b * H * W)))
            settle()
            for s in signals:
                if s.spare:
                    dve.sem_inc(s.sem, s.spare)
            dve.sem_inc(setup.sem, 1)
            dve.wait_ge(*consts_in.rise(Pair(0), 16 * loads[0]))
            dve.wait_ge(act_own, 1)
            step(dve.tensor_copy(ones_r[:], shared[:, 0:P]))
            step(tt(wa_l[:], fm[:, 0, 0:NATT], wa_h[:].bitcast(F32), ALU.subtract))
            step(tt(wg_l[:], fm[:, 1, 0:E], wg_h[:].bitcast(F32), ALU.subtract))
            step(tt(w1_l[:], gath[:, 0].rearrange("p a b -> p (a b)"), w1_h[:].bitcast(F32), ALU.subtract))
            for n, v in enumerate((xn, out_sb)):
                r = slice(32, 33)
                step(tt(b2_hl[r, n * BANK:(n + 1) * BANK], v[r].rearrange("p t c -> p (t c)")[:, 0:BANK],
                        b2_hl[r, n * BANK:(n + 1) * BANK].bitcast(F32), ALU.subtract))
            step(dve.memset(base_xy[:], 0.0))
            settle()
            bxy = base_xy[:].rearrange("p (t b) n k -> p t (b n) k", b=2)
            own(stt(base_xy[:].rearrange("p g n k -> p g (n k)"), bo2.unsqueeze(1).to_broadcast([P, GROUPS, 16]), 4.0,
                    base_xy[:].rearrange("p g n k -> p g (n k)"), ALU.mult, ALU.add))
            own(ts(bxy[:, :, :, 0], bxy[:, :, :, 0], const[:, GX:GX + 1], ALU.add))
            own(tt(bxy[:, :, :, 1], bxy[:, :, :, 1],
                   const[:, GY:GY + QT_N].unsqueeze(2).to_broadcast([P, QT_N, 2 * NP_]), ALU.add))
            dve.wait_ge(*spare_rows.rise(Pair(0), 64))
            dve.sem_inc(setup.sem, 2)

            start = steps[0]
            grid_steps, work_steps, last_steps = STEPS
            off_hidden(Pair(0))
            off_gelu(Pair(0))
            off_points(Pair(0), 0)
            assert steps[0] == start + grid_steps, (steps[0] - start)
            head[0] = steps[0]

            def stretch(pair, par, more):
                steps[0] = 0
                base[0] = pair
                work(pair, par, more)
                assert steps[0] == (work_steps if more else last_steps), (more, steps[0])

            with dve.Fori(0, PAIRS // 2 - 1) as j:
                stretch(Pair(0, dve, j), 0, True)
                stretch(Pair(1, dve, j), 1, True)
            stretch(Pair(PAIRS - 2), 0, True)
            stretch(Pair(PAIRS - 1), 1, False)


STEPS = (34, 452, 418)


def kernel(**inputs):
    import concourse.bacc as bacc
    from concourse.bass_utils import run_bass_kernel_spmd as run

    a = {k: np.ascontiguousarray(v) for k, v in inputs.items()}
    arrays = {
        "x": a["x"], "txt": a["txt"], "const": constants(),
        "Wq_t": a["L0_tok_W_q"].T, "Wk_t": a["L0_tok_W_k"].T, "Wv_t": a["L0_tok_W_v"].T,
        "W_o1": a["L0_tok_W_o1"], "b_o1": a["L0_tok_b_o1"], "ln_g": a["L0_tok_ln_g"], "ln_b": a["L0_tok_ln_b"],
        "W_o2": a["L0_tok_W_o2"], "b_o2": a["L0_tok_b_o2"],
        "aWq": a["L0_attn_Wq"], "abq": a["L0_attn_bq"], "aWk": a["L0_attn_Wk"], "abk": a["L0_attn_bk"],
        "aWv": a["L0_attn_Wv"], "abv": a["L0_attn_bv"],
        "gate_w": a["L0_ffn_gate_w"], "gate_b": a["L0_ffn_gate_b"], "w1": a["L0_ffn_w1"],
        "b1_t": a["L0_ffn_b1"].T, "w2": a["L0_ffn_w2"], "b2": a["L0_ffn_b2"],
        "gamma": a["L0_ffn_gamma"], "beta": a["L0_ffn_beta"],
    }
    arrays = {f"in_{k}": np.ascontiguousarray(v) for k, v in arrays.items()}
    nc = bacc.Bacc("TRN2", target_bir_lowering=False, num_devices=1)
    nc.disable_value_cache = True
    w = {k[3:]: nc.dram_tensor(k, v.shape, mybir.dt.from_np(v.dtype), kind="ExternalInput").ap()
         for k, v in arrays.items()}
    out = nc.dram_tensor("out_0", (B, S, C), F32, kind="ExternalOutput").ap()
    tables = [nc.dram_tensor(f"table{n}", (2 * H * W, 2 * C), F32, kind="Internal").ap() for n in range(2)]
    build(nc, w["x"], w["txt"], w, out, tables)
    r = run(nc, [arrays], core_ids=[0])
    return r.results[0]["out_0"]
```

```python
from contextlib import ExitStack

import concourse.bass as bass
from concourse import mybir
import numpy as np

F32 = mybir.dt.float32
F32R = mybir.dt.float32r
I32 = mybir.dt.int32
U32 = mybir.dt.uint32
ALU = mybir.AluOpType
ACT = mybir.ActivationFunctionType
X_AXIS = mybir.AxisListType.X

P = 128
B, C, H, W = 32, 64, 128, 128
TXT = 128
PAIRS = B // 2
GRID = 32
NQ = GRID * GRID
QT_N = NQ // P
S = NQ + TXT
ST_N = S // P
NP_, NH, DH = 8, 8, 8
F, E = 128, 16
O1W = C // 4
GROUPS = 2 * QT_N
NCH = QT_N
CR = H // NCH
HR = CR // 2
NG = 4
EPS = 1e-5
RNE = 8388608.0
RSQRT_SEED = float(0x5F3759DF)
MASKED = -1.0e30
LOWEST = -3.4e38
QK_SCALE = DH ** -0.5
ATT_SCALE = C ** -0.5
CC = 2
CHUNKS = [list(range(t, min(t + CC, ST_N))) for t in range(0, ST_N, CC)]
NZ = len(CHUNKS) * E
NY = 2 * ST_N
EH = E // 2
BANK = 512


def grid_coordinates():
    step = np.arange(GRID, dtype=np.float32) / np.float32(GRID - 1)
    ref = np.float32(-1.0) * (np.float32(1.0) - step) + np.float32(1.0) * step
    pix = (ref + np.float32(1.0)) * np.float32(0.5) * np.float32(W - 1)
    low = np.clip(np.floor(pix), 0, W - 2).astype(np.int64)
    return pix.astype(np.float32), low, np.clip(pix - low, 0, 1).astype(np.float32)


IDENT, ZERO, MASK, GX, GY, RANK, GRIDW = 0, 128, 512, 640, 641, 649, 665
NCONST = GRIDW + GRID * 2 * GRID


def constants():
    pix, low, frac = grid_coordinates()
    c = np.zeros((P, NCONST), np.float32)
    c[:, IDENT:IDENT + P] = np.eye(P, dtype=np.float32)
    c[:, MASK:MASK + P] = np.where(np.arange(P)[None, :] > np.arange(P)[:, None], np.float32(MASKED), np.float32(0))
    c[:, GX] = pix[np.arange(P) % GRID]
    for t in range(QT_N):
        c[:, GY + t] = pix[4 * t + np.arange(P) // GRID]
    c[:, RANK:RANK + E] = E - np.arange(E)
    m = c[:, GRIDW:].reshape(P, GRID, 2, GRID)
    for i in range(GRID):
        for k, wy in ((0, np.float32(1) - frac[i]), (1, frac[i])):
            for j in range(GRID):
                m[low[j], i, k, j] += wy * (np.float32(1) - frac[j])
                m[low[j] + 1, i, k, j] += wy * frac[j]
    return c


def key_chunks(i):
    return (i + 4) // 4


def first_chunk(i):
    return sum(key_chunks(k) for k in range(i))


KEY_CHUNKS = first_chunk(ST_N)

def layer2_count(c, half, j):
    return 2 * CHUNKS[c][0] + half * len(CHUNKS[c]) + j + 1


def token_stages():
    order = []
    for t in range(QT_N + 1):
        for h in range(2):
            if t < QT_N:
                order += [("weigh", (t, h), 2), ("turn", (t, h), 2), ("turned", (t, h), 2)]
            if t and h == 0:
                order += [("scores", (t - 1,), 2), ("point_exp", (t - 1,), 1)]
            elif t:
                order += [("values", (t - 1,), 2)]
        if t < QT_N:
            order += [("key_values", (t, 0), 1), ("key_values", (t, 1), 1)]
    return order


def block_stages():
    order = [("norm", (0,), 25), ("normalize", (0,), 15), ("high", (0,), 5), ("low", (0,), 8),
             ("turn_tokens", (0,), 4), ("copy_tokens", (0,), 4), ("project_q", (), 3), ("copy_q", (), 3),
             ("project_k", (), 3), ("copy_k", (), 3), ("project_v", (), 3), ("copy_v", (), 3)]

    def score(i):
        o = []
        for c in range(key_chunks(i)):
            o += [("score", (i, c), 2), ("score_max", (i, c), 2)]
        return o + [("soft", (i,), 2)]

    order += score(0)
    waiting = []
    for i in range(ST_N):
        if i + 1 < ST_N:
            order += score(i + 1)
        for c in range(key_chunks(i)):
            order += [("turn_probs", (i, c), 2), ("copy_probs", (i, c), 2)] + waiting
            waiting = [("attend", (i, c), 1)] + ([("heads", (i,), 1)] if c == key_chunks(i) - 1 else [])
    order += waiting
    order += [("norm", (1,), 25), ("normalize", (1,), 15), ("high", (1,), 5), ("low", (1,), 8),
              ("turn_tokens", (1,), 4), ("copy_tokens", (1,), 4), ("gate_logits", (), 3), ("top2", (), 15),
              ("gate_exp", (), 1), ("gates", (), 6), ("turn_gates", (), 1), ("copy_gates", (), 1),
              ("gate_bias", (), 2), ("add_bias", (), 2)]
    late = []
    for n in range(NZ + 2):
        if n < NZ:
            order += [("layer1", (n,), 1), ("relu", (n,), 1)]
        order += late
        late = []
        if n >= 2:
            order += [("layer2", (n - 2,), 1)]
            c, e = (n - 2) // E, (n - 2) % E
            if e % EH == EH - 1:
                late = [("gated", (c, e // EH, j), 1) for j in range(len(CHUNKS[c]))]
                if e == E - 1:
                    late += [("add_up", (c, j), 1) for j in range(len(CHUNKS[c]))]
    order += late
    return order + [("residual", (), 3), ("norm", (2,), 25), ("normalize", (2,), 15), ("finish", (), 8),
                    ("store", (), 1)]


def grid_stages(chunks):
    order = []
    for ch in chunks:
        if ch == chunks[0]:
            order += [("load", (2 * ch,), 1), ("load", (2 * ch + 1,), 6)]
        for half in range(2):
            for g in range(2):
                order += [("rows", (ch, half, g), 1), ("copy_rows", (ch, half, g), 1)]
            if ch != chunks[-1]:
                order += [("load", (2 * ch + 2 + half,), 0)]
        order += [("table", (ch,), 0), ("sample", (ch,), 2), ("feature", (ch,), 1),
                  ("turn_feature", (ch,), 1), ("feature_t", (ch,), 1), ("query", (ch,), 1), ("copy_query", (ch,), 1)]
    if chunks[-1] == NCH - 1:
        order += [("off_hidden", (), 12), ("off_exp", (), 2), ("off_gelu", (), 2), ("off_turn", (), 1),
                  ("off_copy", (), 1), ("off_layer2", (), 1), ("off_points", (), 8)]
    return order


GRID_FIRST = 5


def merge(*threads):
    placed = []
    for name, stages, begin, end in threads:
        total, at = sum(s[2] for s in stages), 0
        for stage, args, share in stages:
            placed.append((begin + (end - begin) * at / total, len(placed), name, stage, args))
            at += share
    return [p[2:] for p in sorted(placed)]


def slot_order(slot, first, last):
    threads = [("tokens", [("text", (), 0)] + token_stages(), 0.0, 0.96)]
    if slot or not first:
        threads.append(("block", block_stages(), 0.0, 1.0))
    if not last:
        chunks = range(GRID_FIRST) if slot == 0 else range(GRID_FIRST, NCH)
        threads.append(("grid", grid_stages(chunks), 0.02, 0.9 if slot == 0 else 0.8))
    return merge(*threads)


class Pair:

    def __init__(self, off, eng=None, turn=None):
        self.off, self.eng, self.turn, self.products = off, eng, turn, {}

    def __add__(self, n):
        p = Pair(self.off + n, self.eng, self.turn)
        p.products = self.products
        return p

    def __sub__(self, n):
        return self + -n

    def times(self, per, k=0):
        if self.turn is None:
            return self.off * per + k
        if per not in self.products:
            self.products[per] = self.eng.snap(self.turn * (2 * per))
        return self.products[per] + (self.off * per + k)


class Signal:

    def __init__(self, sem, per, spare=0):
        self.sem, self.per, self.spare = sem, per, spare

    def rise(self, pair, k):
        assert pair.off * self.per + k + self.spare > 0, "a wait's value has to stay positive"
        return self.sem, pair.times(self.per, k + self.spare)


def build(nc, x, txt, w, out, tables):
    _, LOW, _ = grid_coordinates()
    ctx = ExitStack()
    with ctx:
        def sb(name, shape, dt=F32):
            return ctx.enter_context(nc.sbuf_tensor(name, shape, dt))

        signals = []

        def sig(name, per, spare=0):
            s = Signal(ctx.enter_context(nc.semaphore(name)), per, spare)
            signals.append(s)
            return s

        const = sb("const", [P, NCONST])
        ident = const[:, IDENT:IDENT + P]
        zero = const[:, ZERO:ZERO + 1]
        gridw = const[:, GRIDW:].rearrange("p (i k j) -> p i k j", i=GRID, k=2)
        w_proj = sb("w_proj", [P, 2 * (C + O1W)])
        w_o2 = sb("w_o2", [P, P])
        w_kv = sb("w_kv", [P, 2 * C])
        rows16 = sb("rows16", [P, 5, 16])
        bo1, lng, lnb, bo2, gateb = (rows16[:, n, :] for n in range(5))
        rows64 = sb("rows64", [P, 3, C])
        bv, gamma, beta = (rows64[:, n, :] for n in range(3))
        bqk = sb("bqk", [P, 2])
        b1 = sb("b1", [P, E])
        NATT = 2 * P + C
        wa_h = sb("wa_h", [P, NATT], F32R)
        wa_l = sb("wa_l", [P, NATT], F32R)
        wg_h = sb("wg_h", [P, E], F32R)
        wg_l = sb("wg_l", [P, E], F32R)
        w1_h = sb("w1_h", [P, E * F], F32R)
        w1_l = sb("w1_l", [P, E * F], F32R)
        w2 = sb("w2", [P, E * C])
        b2_diag = sb("b2_diag", [P, QT_N * C])

        fm = sb("fm", [P, 2, HR * W])
        rows = sb("rows", [P, 2, 2, CR + 1, C])
        qf = sb("qf", [P, P])
        qft = sb("qft", [P, P])
        query = sb("query", [P, 2, QT_N, 2, C])
        o1 = sb("o1", [P, GROUPS, O1W])
        oa = sb("oa", [P, GROUPS, O1W])
        ob = sb("ob", [P, GROUPS, O1W])
        oht = sb("oht", [P, 2, P])
        st16 = sb("st16", [P, 8, GROUPS])
        base_xy = sb("base_xy", [P, GROUPS, NP_, 2])
        ca = oa[:].rearrange("p g (n k) -> p (g n) k", k=2)
        cb = ob[:].rearrange("p g (n k) -> p (g n) k", k=2)
        frac2 = sb("frac2", [P, GROUPS * NP_, 2, 2])
        idxf = o1[:].rearrange("p g n -> p (g n)")[:, 0:GROUPS * NP_].rearrange("p (g n) -> p g n", n=NP_)
        idx = sb("idx", [P, 2, GROUPS * NP_], U32)
        corner_w = sb("corner_w", [P, 2, GROUPS, NP_ * 4])
        table_base = sb("table_base", [P, 2])
        gath = sb("gath", [P, NG, NP_, 4 * C])

        prod = [sb(f"prod{n}", [P, 1024]) for n in range(2)]
        samp_t = [sb(f"samp_t{n}", [P, 1024]) for n in range(2)]
        kq = sb("kq", [P, 512])
        av = sb("av", [P, 512])
        shared = sb("shared", [P, 2 * S])
        probs = [shared[:, n * S:(n + 1) * S] for n in range(2)]
        gated = [shared[:, n * 1024:(n + 1) * 1024] for n in range(2)]
        probs_t = [sb(f"probs_t{n}", [P, BANK]) for n in range(3)]
        shared2 = sb("shared2", [P, 2 * S])
        q_t, k_t = shared2[:, 0:S], shared2[:, S:2 * S]
        hid = [shared2[:, n * CC * P:(n + 1) * CC * P] for n in range(4)]
        moe = shared2[:, S:S + ST_N * C].rearrange("p (t c) -> p t c", c=C)

        pt_sc = sb("pt_sc", [P, 4, NP_ * NH])
        pt_st = sb("pt_st", [P, 3, NH])
        pt_o = sb("pt_o", [P, C])
        h0 = sb("h0", [P, 2, ST_N, C])
        h1 = sb("h1", [P, ST_N, C])
        xn = sb("xn", [P, ST_N, C])
        xs = sb("xs", [P, ST_N, 2, C], F32R)
        xt = sb("xt", [P, S], F32R)
        v_sb = sb("v_sb", [P, ST_N, C])
        bn6 = sb("bn6", [P, ST_N, 6])
        mv = sb("mv", [P, ST_N, 2])
        ln9 = sb("ln9", [P, 8, ST_N])
        att = sb("att", [P, 4, ST_N])
        att_m = sb("att_m", [P, KEY_CHUNKS])
        lg = sb("lg", [P, 6, ST_N, E])
        gs = sb("gs", [P, 8, ST_N])
        gate = sb("gate", [P, 2 * QT_N, E])
        gate_t = sb("gate_t", [P, 2, P])
        out_sb = sb("out_sb", [P, ST_N, C])

        ps = ctx.enter_context(nc.psum_tensor("ps", [P, 8 * BANK], F32))

        def bank(n, a=0, b=BANK):
            return ps[:, n * BANK + a:n * BANK + b]

        consts_in = sig("consts_in", 0)
        setup = sig("setup", 0)
        ready = sig("ready", 0)
        fm_in = [sig(f"fm_in{n}", 16 * NCH) for n in range(2)]
        rows_ps = sig("rows_ps", 4 * NCH, 16)
        rows_sb = sig("rows_sb", 4 * NCH)
        carry = sig("carry", NCH)
        table_in = [sig(f"table_in{n}", 32 * NCH // 2, 16) for n in range(2)]
        qf_ps, qf_sb = sig("qf_ps", NCH, 16), sig("qf_sb", NCH)
        qft_ps, qft_sb = sig("qft_ps", NCH), sig("qft_sb", NCH)
        proj_ps, proj_sb = sig("proj_ps", NCH), sig("proj_sb", NCH, 16)
        off_u = sig("off_u", 1)
        off_e = sig("off_e", 1)
        off_h, off_ht = sig("off_h", 1), sig("off_ht", 1, 16)
        off_hsb, off_raw = sig("off_hsb", 1), sig("off_raw", 1)
        off_rd = sig("off_rd", 1, 2)
        idx_ok = sig("idx_ok", 1, 16)
        corner_ok = sig("corner_ok", 1)
        gath_in = [sig(f"gath_in{n}", 2 * QT_N // NG * 16 * NP_) for n in range(NG)]
        gath_rd = sig("gath_rd", 2 * QT_N, 24)
        wcorn = sig("wcorn", 4 * QT_N)
        samp_ps = sig("samp_ps", 4 * QT_N, 16)
        samp_sb = sig("samp_sb", 4 * QT_N, 16)
        kv_ps = sig("kv_ps", 2 * QT_N, 16)
        sc_sub = sig("sc_sub", 2 * QT_N)
        sc_exp = sig("sc_exp", 2 * QT_N, 16)
        kv_rd = sig("kv_rd", 4 * QT_N, 16)
        tok = sig("tok", 2 * QT_N, 24)
        txt_in = [sig(f"txt_in{n}", 16) for n in range(2)]
        ln_ab = sig("ln_ab", 6)
        ln_x = sig("ln_x", 6)
        ln_hi = sig("ln_hi", 4)
        ln_lo = sig("ln_lo", 4)
        xt_ps = sig("xt_ps", 4 * 3)
        xt_sb = sig("xt_sb", 4 * 3)
        q_ps, q_sb = sig("q_ps", 6), sig("q_sb", 6)
        k_ps, k_sb = sig("k_ps", 6), sig("k_sb", 6)
        v_ps, v_cp = sig("v_ps", 2), sig("v_cp", 4)
        s_ps = sig("s_ps", 2 * KEY_CHUNKS)
        s_rd = sig("s_rd", 2 * KEY_CHUNKS)
        s_max = sig("s_max", 2 * ST_N)
        s_exp = sig("s_exp", 2 * ST_N)
        p_ps, p_sb = sig("p_ps", 2 * KEY_CHUNKS), sig("p_sb", 2 * KEY_CHUNKS)
        o_part = sig("o_part", 2 * KEY_CHUNKS)
        o_rd = sig("o_rd", 2 * ST_N)
        gate_ps = sig("gate_ps", 2)
        gate_d = sig("gate_d", 2)
        gate_e = sig("gate_e", 2)
        gate_ok = sig("gate_ok", 2)
        gate_turn, gate_tsb = sig("gate_turn", 2), sig("gate_tsb", 2)
        bias_ps, bias_rd = sig("bias_ps", 2), sig("bias_rd", 4)
        z_ps, z_sb = sig("z_ps", 2 * NZ), sig("z_sb", 2 * NZ, 16)
        y_ps, y_rd = sig("y_ps", 2 * NY), sig("y_rd", 2 * NY, 16)
        out_ok = sig("out_ok", 2)
        stored = sig("stored", 32, 48)
        spare_rows = sig("spare_rows", 0)
        vec = ctx.enter_context(nc.semaphore("vec"))
        act_own = ctx.enter_context(nc.semaphore("act_own"))
        pool_gate = ctx.enter_context(nc.semaphore("pool_gate"))
        dve_gate = ctx.enter_context(nc.semaphore("dve_gate"))

        loads = [0]

        block = ctx.enter_context(nc.Block())

        def follow(stages, pair, par, slot, first, last):
            who = {"tokens": (pair, par, slot), "grid": (pair + 1, 1 - par, None),
                   "block": (pair, par, 0) if slot else (pair - 1, 1 - par, 1)}
            for thread, stage, args in slot_order(slot, first, last):
                if stage in stages:
                    stages[stage](*who[thread], *args)

        def drive(eng, stages, stretch):
            stretch(0, None)
            for stage, args, _ in grid_stages(range(NCH)):
                if stage in stages:
                    stages[stage](Pair(0), 0, None, *args)
            stretch(1, None)
            for slot in range(2):
                follow(stages, Pair(0), 0, slot, True, False)
            with eng.Fori(0, PAIRS // 2 - 1) as j:
                for par in (1, 0):
                    pair = Pair(2 - par, eng, j)
                    stretch(2, pair)
                    for slot in range(2):
                        follow(stages, pair, par, slot, False, False)
            stretch(3, None)
            for slot in range(2):
                follow(stages, Pair(PAIRS - 1), 1, slot, False, True)
            stretch(4, None)
            for stage, args, _ in block_stages():
                if stage in stages:
                    stages[stage](Pair(PAIRS - 1), 1, 1, *args)
            stretch(5, None)

        def unseen(n, pair):
            pass

        x_v = x.rearrange("(n b) c (m r) w -> n (b c) m (r w)", b=2, r=HR)
        tab_v = [t.rearrange("(b y x) c -> b y x c", y=H, x=W) for t in tables]
        out_v = out.rearrange("b (t p) c -> b p t c", p=P)

        @block.sync
        def _(sp):
            def load(dst, src):
                loads[0] += 1
                sp.dma_start(dst, src).then_inc(consts_in.sem, 16)

            sp.wait_ge(*setup.rise(Pair(0), 1))
            load(const[:], w["const"])
            for b in range(2):
                r, c0 = slice(64 * b, 64 * b + 64), b * (C + O1W)
                load(w_proj[r, c0:c0 + C], w["Wq_t"])
                load(w_proj[r, c0 + C:c0 + C + O1W], w["W_o1"])
                load(w_kv[r, 0:C], w["Wk_t"])
                load(w_kv[r, C:2 * C], w["Wv_t"])
                load(fm[r, 0, 0:C], w["aWq"])
                load(fm[r, 0, 128:128 + C], w["aWk"])
                load(fm[r, 0, 256:256 + C], w["aWv"])
                load(fm[r, 1, 0:E], w["gate_w"])
                load(gath[r, 0:1].rearrange("p a b c -> p (a b c)").rearrange("p (e f) -> p e f", f=F),
                     w["w1"].rearrange("e c f -> c e f"))
            for g in range(8):
                load(w_o2[16 * g:16 * g + 16, 16 * g:16 * g + 16], w["W_o2"])
            for n, name in enumerate(("b_o1", "ln_g", "ln_b", "b_o2", "gate_b")):
                load(rows16[:, n, :], w[name].unsqueeze(0).to_broadcast([P, 16]))
            for n, name in enumerate(("abv", "gamma", "beta")):
                load(rows64[:, n, :], w[name].unsqueeze(0).to_broadcast([P, C]))
            load(bqk[0:C, 0:1], w["abq"].unsqueeze(1))
            load(bqk[0:C, 1:2], w["abk"].unsqueeze(1))
            load(b1[:], w["b1_t"])
            load(w2[:].rearrange("p (e c) -> p e c", c=C), w["w2"].rearrange("e f c -> f e c"))
            for t in range(QT_N):
                load(b2_diag[t * E:(t + 1) * E, t * C:(t + 1) * C], w["b2"])

            def load_rows(pair, par, _, hc):
                if hc >= 2:
                    sp.wait_ge(*rows_ps.rise(pair, 2 * (hc - 1)))
                else:
                    sp.wait_ge(*rows_ps.rise(pair - 1, 4 * NCH - 2 * (1 - hc)))
                sp.dma_start(fm[:, hc % 2, :], x_v[pair.times(1), :, hc, :]).then_inc(fm_in[hc % 2].sem, 16)

            def write_table(pair, par, _, ch):
                sp.wait_ge(*rows_sb.rise(pair, 4 * (ch + 1)))
                sp.wait_ge(*carry.rise(pair, ch + 1))
                if ch == 0:
                    sp.wait_ge(*gath_rd.rise(pair - 2, 2 * QT_N))
                n = CR if ch else CR - 1
                first = 0 if ch else 1
                y0 = ch * CR + first - 1
                for b in range(2):
                    src = rows[:, ch % 2, b, first:first + n, :]
                    src = bass.AP(tensor=src.tensor, offset=src.offset,
                                  ap=[list(src.ap[0]), [C, n], [1, 2 * C]])
                    dst = tab_v[par][b, y0:y0 + n].rearrange("y x c -> x y c")
                    sp.dma_start(dst, src).then_inc(table_in[ch % 2].sem, 16)

            def text(pair, par, b):
                sp.wait_ge(*stored.rise(pair - 1, 16 * (b + 1)))
                sp.dma_start(h0[:, b, QT_N, :], txt[pair.times(2, b)]).then_inc(txt_in[b].sem, 16)

            def store(pair, par, b):
                sp.wait_ge(*out_ok.rise(pair, b + 1))
                sp.dma_start(out_v[pair.times(2, b)], out_sb[:]).then_inc(stored.sem, 16)

            for t in tab_v:
                for b in range(2):
                    sp.dma_start(t[b, H - 1, :, :], shared[:, 0:2 * C]).then_inc(spare_rows.sem, 16)
            sp.wait_ge(*ready.rise(Pair(0), 1))
            drive(sp, {"load": load_rows, "table": write_table, "text": text, "store": store}, unseen)
            sp.wait_ge(*stored.rise(Pair(PAIRS), 0))

        @block.gpsimd
        def _(pool):
            pool.wait_ge(*setup.rise(Pair(0), 2))
            pool.wait_ge(*spare_rows.rise(Pair(0), 64))

            def gather(pair, par):
                pool.wait_ge(*idx_ok.rise(pair, 1))
                for n in range(2):
                    pool.wait_ge(*table_in[n].rise(pair, 32 * NCH // 2))
                for b in range(2):
                    for t in range(QT_N):
                        n = b * QT_N + t
                        pool.wait_ge(*gath_rd.rise(pair, n + 1 - NG))
                        pool.sem_inc(pool_gate, 1)
                        for p in range(NP_):
                            k = (t * 2 + b) * NP_ + p
                            pool.indirect_dma_start(
                                out=gath[:, n % NG, p, :], out_offset=None, in_=tables[par],
                                in_offset=bass.IndirectOffsetOnAxis(ap=idx[:, par, k:k + 1], axis=0),
                            ).then_inc(gath_in[n % NG].sem, 16)

            with pool.Fori(0, PAIRS // 2) as j:
                gather(Pair(0, pool, j), 0)
                gather(Pair(1, pool, j), 1)

        @block.tensor
        def _(pe):
            def rows_turn(pair, par, _, ch, half, g):
                n = 4 * ch + 2 * half + g
                if g == 0:
                    pe.wait_ge(*fm_in[half].rise(pair, 16 * (ch + 1)))
                if half or g:
                    pe.wait_ge(*rows_sb.rise(pair, n))
                elif ch:
                    pe.wait_ge(*proj_sb.rise(pair, ch))
                else:
                    pe.wait_ge(*off_rd.rise(pair - 1, 1))
                for r in range(4):
                    last = pe.transpose(bank(3, r * P, r * P + P),
                                        fm[:, half, (4 * g + r) * W:(4 * g + r + 1) * W], ident)
                last.then_inc(rows_ps.sem, 1)

            def sample(pair, par, _, t):
                pe.wait_ge(*rows_sb.rise(pair, 4 * (t + 1)))
                for i in range(4 * t, 4 * t + 4):
                    for k in range(2):
                        r = 1 + int(LOW[i]) + k - CR * t
                        assert 1 <= r <= CR
                        last = pe.matmul(bank(3, 0, P)[32 * (i % 4):32 * (i % 4) + 32],
                                         gridw[:, i, k, :], rows[:, t % 2, :, r, :],
                                         start=(k == 0), stop=(k == 1))
                last.then_inc(qf_ps.sem, 1)

            def turn_feature(pair, par, _, t):
                pe.wait_ge(*qf_sb.rise(pair, t + 1))
                pe.transpose(bank(3, 128, 256), qf[:], ident).then_inc(qft_ps.sem, 1)

            def queries(pair, par, _, t):
                pe.wait_ge(*qft_sb.rise(pair, t + 1))
                pe.matmul(bank(3, 256, 256 + 2 * (C + O1W)), qft[:], w_proj[:],
                          start=True, stop=True).then_inc(proj_ps.sem, 1)

            def off_turn(pair, par, _):
                pe.wait_ge(*off_h.rise(pair, 1))
                pe.wait_ge(*proj_sb.rise(pair, NCH))
                for n in range(2):
                    last = pe.transpose(bank(3, n * P, n * P + P),
                                        oa[:].rearrange("p g c -> p (g c)")[:, n * P:n * P + P], ident)
                last.then_inc(off_ht.sem, 1)

            def off_layer2(pair, par, _):
                pe.wait_ge(*off_hsb.rise(pair, 1))
                for n in range(2):
                    last = pe.matmul(bank(3, 256 + n * P, 256 + n * P + P), oht[:, n, :], w_o2[:],
                                     start=True, stop=True)
                last.then_inc(off_raw.sem, 1)

            def turn(pair, par, b, t, h):
                m = 2 * (b * QT_N + t) + h
                pe.wait_ge(*wcorn.rise(pair, m + 1))
                if m:
                    pe.wait_ge(*samp_sb.rise(pair, m))
                else:
                    pe.wait_ge(*samp_sb.rise(pair - 1, 4 * QT_N))
                for p in range(4):
                    for dx in range(2):
                        last = pe.matmul(bank(0, p * P, p * P + P),
                                         prod[h][:, (p * 2 + dx) * P:(p * 2 + dx + 1) * P], ident,
                                         is_transpose=True, start=(dx == 0), stop=(dx == 1))
                last.then_inc(samp_ps.sem, 1)

            def key_values(pair, par, b, t, h):
                n = b * QT_N + t
                pe.wait_ge(*samp_sb.rise(pair, 2 * n + h + 1))
                if n:
                    pe.wait_ge(*kv_rd.rise(pair, 2 * (n - 1) + h + 1))
                else:
                    pe.wait_ge(*kv_rd.rise(pair - 1, 4 * QT_N - 1 + h))
                for p in range(4):
                    last = pe.matmul(bank(1 + h, p * P, p * P + P),
                                     samp_t[n % 2][:, (4 * h + p) * P:(4 * h + p + 1) * P], w_kv[:],
                                     start=True, stop=True)
                if h:
                    last.then_inc(kv_ps.sem, 1)

            def turn_tokens(pair, par, b, k):
                m = 2 * b + k
                pe.wait_ge(*ln_hi.rise(pair, m + 1))
                pe.wait_ge(*ln_lo.rise(pair, m + 1))
                if k:
                    pe.wait_ge(*s_rd.rise(pair, KEY_CHUNKS * (b + 1)))
                    pe.wait_ge(*p_sb.rise(pair, KEY_CHUNKS * (b + 1)))
                else:
                    before = (pair, 1) if b else (pair - 1, 2)
                    pe.wait_ge(*z_sb.rise(before[0], NZ * before[1]))
                    pe.wait_ge(*y_rd.rise(before[0], NY * before[1]))
                for c in range(3):
                    for j in range(3):
                        t = 3 * c + j
                        last = pe.transpose(bank(4 + c, j * P, j * P + P),
                                            xs[:, t].rearrange("p h c -> p (h c)").bitcast(F32), ident)
                    last.then_inc(xt_ps.sem, 1)

            def split(dst, lhs, rhs):
                for n in range(2):
                    a = lhs[n] if isinstance(lhs, tuple) else lhs
                    r = rhs[n] if isinstance(rhs, tuple) else rhs
                    last = pe.matmul(dst, a, r, start=n == 0, stop=n == 1)
                return last

            CW = 3 * P

            def project_q(pair, par, b):
                for c in range(3):
                    pe.wait_ge(*xt_sb.rise(pair, 6 * b + c + 1))
                    split(bank((7, 4, 5)[c], 0, CW), (wa_h[:, 0:P], wa_l[:, 0:P]),
                          xt[:, c * CW:(c + 1) * CW]).then_inc(q_ps.sem, 1)

            def project_k(pair, par, b):
                for c in range(3):
                    if c:
                        pe.wait_ge(*q_sb.rise(pair, 3 * b + c))
                    split(bank((6, 7, 4)[c], 0, CW), (wa_h[:, P:2 * P], wa_l[:, P:2 * P]),
                          xt[:, c * CW:(c + 1) * CW]).then_inc(k_ps.sem, 1)

            def project_v(pair, par, b):
                pe.wait_ge(*q_sb.rise(pair, 3 * b + 3))
                for t in range(ST_N):
                    if t == 8:
                        pe.wait_ge(*k_sb.rise(pair, 3 * b + 1))
                    last = split(bank(5 + t // 8, (t % 8) * C, (t % 8) * C + C), xt[:, t * P:(t + 1) * P],
                                 (wa_h[:, 2 * P:2 * P + C], wa_l[:, 2 * P:2 * P + C]))
                last.then_inc(v_ps.sem, 1)

            def score(pair, par, b, i, c):
                n = first_chunk(i) + c
                if n == 0:
                    pe.wait_ge(*q_sb.rise(pair, 3 * b + 3))
                    pe.wait_ge(*k_sb.rise(pair, 3 * b + 3))
                elif n == 1:
                    pe.wait_ge(*v_cp.rise(pair, 2 * b + 2))
                else:
                    pe.wait_ge(*s_rd.rise(pair, KEY_CHUNKS * b + n - 1))
                a = c * BANK
                m = min((i + 1) * P - a, BANK)
                pe.matmul(bank(4 + n % 2, 0, m), q_t[:, i * P:(i + 1) * P], k_t[:, a:a + m],
                          start=True, stop=True).then_inc(s_ps.sem, 1)

            def turn_probs(pair, par, b, i, c):
                n = KEY_CHUNKS * b + first_chunk(i) + c
                if c == 0:
                    pe.wait_ge(*s_exp.rise(pair, ST_N * b + i + 1))
                if i:
                    pe.wait_ge(*p_sb.rise(pair, n))
                else:
                    pe.wait_ge(*v_cp.rise(pair, 2 * b + 2))
                for k in range(4 * c, min(4 * c + 4, i + 1)):
                    last = pe.transpose(bank(6, (k % 4) * P, (k % 4) * P + P),
                                        probs[i % 2][:, k * P:(k + 1) * P], ident)
                last.then_inc(p_ps.sem, 1)

            def attend(pair, par, b, i, c):
                n = KEY_CHUNKS * b + first_chunk(i) + c
                pe.wait_ge(*p_sb.rise(pair, n + 1))
                if i and c == 0:
                    pe.wait_ge(*o_rd.rise(pair, ST_N * b + i))
                for k in range(4 * c, min(4 * c + 4, i + 1)):
                    last = pe.matmul(bank(7, (i % 8) * C, (i % 8) * C + C),
                                     probs_t[n % 3][:, (k % 4) * P:(k % 4) * P + P], v_sb[:, k, :],
                                     start=(k == 0), stop=(k == i))
                last.then_inc(o_part.sem, 1)

            def gate_logits(pair, par, b):
                pe.wait_ge(*xt_sb.rise(pair, 6 * b + 6))
                pe.wait_ge(*o_rd.rise(pair, ST_N * (b + 1)))
                for t in range(ST_N):
                    last = split(bank(7, t * E, t * E + E), xt[:, t * P:(t + 1) * P], (wg_h[:], wg_l[:]))
                last.then_inc(gate_ps.sem, 1)

            def turn_gates(pair, par, b):
                pe.wait_ge(*gate_ok.rise(pair, b + 1))
                for n in range(2):
                    last = pe.transpose(bank(6, n * P, n * P + P),
                                        gate[:, n * QT_N:(n + 1) * QT_N, :].rearrange("p t e -> p (t e)"), ident)
                last.then_inc(gate_turn.sem, 1)

            def gate_bias(pair, par, b):
                pe.wait_ge(*gate_tsb.rise(pair, b + 1))
                pe.matmul(bank(7), gate_t[:, 0, :], b2_diag[:], start=True, stop=True)
                pe.matmul(bank(6, 256, 256 + C), gate_t[:, 1, :], b2_diag[:, 0:C],
                          start=True, stop=True).then_inc(bias_ps.sem, 1)

            def layer1(pair, par, b, n):
                c, e = n // E, n % E
                if n >= 2:
                    pe.wait_ge(*z_sb.rise(pair, b * NZ + n - 1))
                a, m = CHUNKS[c][0] * P, len(CHUNKS[c]) * P
                split(bank(4 + n % 2, 0, m), (w1_h[:, e * F:(e + 1) * F], w1_l[:, e * F:(e + 1) * F]),
                      xt[:, a:a + m]).then_inc(z_ps.sem, 1)

            def layer2(pair, par, b, n):
                c, e = n // E, n % E
                pe.wait_ge(*z_sb.rise(pair, b * NZ + n + 1))
                for j, t in enumerate(CHUNKS[c]):
                    if e % EH == 0:
                        if e:
                            pe.wait_ge(*y_rd.rise(pair, b * NY + layer2_count(c, 0, j)))
                        elif c:
                            pe.wait_ge(*y_rd.rise(pair, b * NY + layer2_count(c - 1, 1, j)))
                        else:
                            pe.wait_ge(*bias_rd.rise(pair, 2 * b + 2))
                    last = pe.matmul(bank(6 + j, (e % EH) * C, (e % EH + 1) * C), hid[n % 4][:, j * P:(j + 1) * P],
                                     w2[:, e * C:(e + 1) * C], start=True, stop=True)
                    if e % EH == EH - 1:
                        last.then_inc(y_ps.sem, 1)

            pe.wait_ge(*consts_in.rise(Pair(0), 16 * loads[0]))
            pe.wait_ge(*setup.rise(Pair(0), 3))
            pe.wait_ge(*ready.rise(Pair(0), 1))
            drive(pe, {"rows": rows_turn, "sample": sample, "turn_feature": turn_feature, "query": queries,
                       "off_turn": off_turn, "off_layer2": off_layer2, "turn": turn, "key_values": key_values,
                       "turn_tokens": turn_tokens, "project_q": project_q,
                       "project_k": project_k, "project_v": project_v, "score": score, "turn_probs": turn_probs,
                       "attend": attend, "gate_logits": gate_logits, "turn_gates": turn_gates,
                       "gate_bias": gate_bias, "layer1": layer1, "layer2": layer2}, unseen)

        @block.scalar
        def _(act):
            def copy(dst, src):
                return act.activation(dst, src, ACT.Copy)

            def copy_rows(pair, par, _, ch, half, g):
                n = 4 * ch + 2 * half + g
                if half == 0 and g == 0:
                    if ch >= 2:
                        act.wait_ge(*qf_ps.rise(pair, ch - 1))
                        act.wait_ge(*table_in[ch % 2].rise(pair, 32 * (ch // 2)))
                    else:
                        act.wait_ge(*qf_ps.rise(pair - 1, NCH - 1 + ch))
                        act.wait_ge(*table_in[ch % 2].rise(pair - 1, 32 * NCH // 2))
                    if ch:
                        act.wait_ge(*rows_sb.rise(pair, 4 * ch))
                        c = copy(rows[:, ch % 2, :, 0, :], rows[:, 1 - ch % 2, :, CR, :])
                        c.then_inc(carry.sem, 1)
                act.wait_ge(*rows_ps.rise(pair, n + 1))
                r0 = 1 + HR * half + 4 * g
                copy(rows[:, ch % 2, :, r0:r0 + 4, :].rearrange("p b r c -> p r b c"),
                     bank(3).rearrange("p (r b c) -> p r b c", r=4, b=2)).then_inc(rows_sb.sem, 1)
                if n == 3:
                    act.sem_inc(carry.sem, 1)

            def feature(pair, par, _, t):
                act.wait_ge(*qf_ps.rise(pair, t + 1))
                copy(qf[:], bank(3, 0, P)).then_inc(qf_sb.sem, 1)

            def feature_t(pair, par, _, t):
                act.wait_ge(*qft_ps.rise(pair, t + 1))
                copy(qft[:], bank(3, 128, 256)).then_inc(qft_sb.sem, 1)

            def copy_query(pair, par, _, t):
                act.wait_ge(*proj_ps.rise(pair, t + 1))
                src = bank(3, 256, 256 + 2 * (C + O1W)).rearrange("p (b c) -> p b c", b=2)
                if t == 0:
                    act.wait_ge(*tok.rise(pair - 2, 2 * QT_N))
                    act.wait_ge(*idx_ok.rise(pair - 1, 1))
                copy(query[:, par, t], src[:, :, 0:C])
                copy(o1[:, 2 * t:2 * t + 2], src[:, :, C:C + O1W]).then_inc(proj_sb.sem, 1)

            def off_exp(pair, par, _):
                act.wait_ge(*off_u.rise(pair, 1))
                act.activation(ob[:], ob[:], ACT.Exp, scale=-2.0 * (2.0 / np.pi) ** 0.5).then_inc(off_e.sem, 1)

            def off_copy(pair, par, _):
                act.wait_ge(*off_ht.rise(pair, 1))
                copy(oht[:].rearrange("p a b -> p (a b)"), bank(3, 0, 2 * P)).then_inc(off_hsb.sem, 1)

            def turned(pair, par, b, t, h):
                n = b * QT_N + t
                act.wait_ge(*samp_ps.rise(pair, 2 * n + h + 1))
                if h == 0:
                    if n >= 2:
                        act.wait_ge(*kv_ps.rise(pair, n - 1))
                    else:
                        act.wait_ge(*kv_ps.rise(pair - 1, 2 * QT_N - 1 + n))
                copy(samp_t[n % 2][:, h * BANK:(h + 1) * BANK], bank(0)).then_inc(samp_sb.sem, 1)

            def point_exp(pair, par, b, t):
                n = b * QT_N + t
                act.wait_ge(*sc_sub.rise(pair, n + 1))
                act.activation(pt_sc[:, 2 + n % 2], pt_sc[:, 1], ACT.Exp, scale=QK_SCALE).then_inc(sc_exp.sem, 1)

            def normalize(pair, par, b, k):
                src, dst = ((h0[:, b], xn), (h1, xn), (xn, out_sb))[k]
                act.wait_ge(*ln_ab.rise(pair, 3 * b + k + 1))
                for t in range(ST_N):
                    last = act.activation(dst[:, t, :], src[:, t, :], ACT.Identity,
                                          scale=ln9[:, 6, t:t + 1], bias=ln9[:, 7, t:t + 1])
                last.then_inc(ln_x.sem, 1)

            def high(pair, par, b, k):
                act.wait_ge(*ln_x.rise(pair, 3 * b + k + 1))
                act.activation(xs[:, :, 0, :], xn[:], ACT.Copy).then_inc(ln_hi.sem, 1)

            def copy_tokens(pair, par, b, k):
                for c in range(3):
                    act.wait_ge(*xt_ps.rise(pair, 3 * (2 * b + k) + c + 1))
                    copy(xt[:, c * 3 * P:(c + 1) * 3 * P], bank(4 + c, 0, 3 * P)).then_inc(xt_sb.sem, 1)

            CW = 3 * P

            def copy_q(pair, par, b):
                for c in range(3):
                    act.wait_ge(*q_ps.rise(pair, 3 * b + c + 1))
                    act.activation(q_t[:, c * CW:(c + 1) * CW], bank((7, 4, 5)[c], 0, CW), ACT.Identity,
                                   bias=bqk[:, 0:1]).then_inc(q_sb.sem, 1)

            def copy_k(pair, par, b):
                for c in range(3):
                    act.wait_ge(*k_ps.rise(pair, 3 * b + c + 1))
                    act.activation(k_t[:, c * CW:(c + 1) * CW], bank((6, 7, 4)[c], 0, CW), ACT.Identity,
                                   bias=bqk[:, 1:2]).then_inc(k_sb.sem, 1)

            def copy_v(pair, par, b):
                act.wait_ge(*v_ps.rise(pair, b + 1))
                vf = v_sb[:].rearrange("p t c -> p (t c)")
                copy(vf[:, 0:BANK], bank(5)).then_inc(v_cp.sem, 1)
                copy(vf[:, BANK:BANK + C], bank(6, 0, C)).then_inc(v_cp.sem, 1)

            def soft(pair, par, b, i):
                act.wait_ge(*s_max.rise(pair, ST_N * b + i + 1))
                n = (i + 1) * P
                act.activation(probs[i % 2][:, 0:n], probs[i % 2][:, 0:n], ACT.Exp,
                               bias=att[:, 1, i:i + 1], scale=ATT_SCALE,
                               accum_out=att[:, 2, i:i + 1]).then_inc(s_exp.sem, 1)

            def copy_probs(pair, par, b, i, c):
                n = first_chunk(i) + c
                m = min(4, i + 1 - 4 * c) * P
                act.wait_ge(*p_ps.rise(pair, KEY_CHUNKS * b + n + 1))
                if n >= 3:
                    act.wait_ge(*o_part.rise(pair, KEY_CHUNKS * b + n - 2))
                copy(probs_t[(KEY_CHUNKS * b + n) % 3][:, 0:m], bank(6, 0, m)).then_inc(p_sb.sem, 1)

            def gate_exp(pair, par, b):
                act.wait_ge(*gate_d.rise(pair, b + 1))
                act.activation(gs[:, 3, :], gs[:, 2, :], ACT.Exp).then_inc(gate_e.sem, 1)

            def copy_gates(pair, par, b):
                act.wait_ge(*gate_turn.rise(pair, b + 1))
                copy(gate_t[:].rearrange("p a b -> p (a b)"), bank(6, 0, 2 * P)).then_inc(gate_tsb.sem, 1)

            def relu(pair, par, b, n):
                c, e = n // E, n % E
                m = len(CHUNKS[c]) * P
                act.wait_ge(*z_ps.rise(pair, b * NZ + n + 1))
                act.activation(hid[n % 4][:, 0:m], bank(4 + n % 2, 0, m), ACT.Relu,
                               bias=b1[:, e:e + 1]).then_inc(z_sb.sem, 1)

            act.wait_ge(*consts_in.rise(Pair(0), 16 * loads[0]))
            act.wait_ge(*setup.rise(Pair(0), 1))
            copy(wa_h[:], fm[:, 0, 0:NATT])
            copy(wg_h[:], fm[:, 1, 0:E])
            copy(w1_h[:], gath[:, 0].rearrange("p a b -> p (a b)")).then_inc(act_own, 1)
            act.wait_ge(*setup.rise(Pair(0), 3))
            act.sem_inc(ready.sem, 1)
            drive(act, {"copy_rows": copy_rows, "feature": feature, "feature_t": feature_t,
                        "copy_query": copy_query, "off_exp": off_exp, "off_copy": off_copy,
                        "turned": turned, "point_exp": point_exp, "normalize": normalize, "high": high,
                        "copy_tokens": copy_tokens, "copy_q": copy_q, "copy_k": copy_k, "copy_v": copy_v, "soft": soft,
                        "copy_probs": copy_probs, "gate_exp": gate_exp, "copy_gates": copy_gates,
                        "relu": relu}, unseen)

        @block.vector
        def _(dve):
            steps = [0]
            before = [None]

            def step(ins):
                steps[0] += 1
                ins.then_inc(vec, 1)

            def settle():
                if before[0] is None:
                    dve.wait_ge(vec, steps[0])
                else:
                    pair, head = before[0]
                    dve.wait_ge(vec, pair.times(STEPS[2], head + steps[0]))

            def own(ins):
                step(ins)
                settle()

            def tt(o, a, b, op):
                return dve.tensor_tensor(o, a, b, op)

            def ts(o, a, s1, op1, s2=None, op2=None):
                if op2 is None:
                    return dve.tensor_scalar(o, a, s1, None, op1)
                return dve.tensor_scalar(o, a, s1, s2, op1, op2)

            def stt(o, a, s, b, op0, op1):
                return dve.scalar_tensor_tensor(out=o, in0=a, scalar=s, in1=b, op0=op0, op1=op1)

            def red(o, a, op=ALU.add):
                return dve.tensor_reduce(o, a, X_AXIS, op)

            def rsqrt(r, v, t, h):
                step(ts(t.bitcast(I32), v.bitcast(I32), 1, ALU.logical_shift_right))
                own(ts(h, v, -0.5, ALU.mult))
                own(ts(r.bitcast(I32), t.bitcast(I32), -1.0, ALU.mult, RSQRT_SEED, ALU.add))
                for _ in range(3):
                    own(tt(t, r, r, ALU.mult))
                    own(tt(t, t, h, ALU.mult))
                    own(stt(r, t, 1.5, r, ALU.add, ALU.mult))

            def bc16(v):
                return v.unsqueeze(2).to_broadcast([P, GROUPS, O1W])

            def row16(v):
                return v.unsqueeze(1).to_broadcast([P, GROUPS, O1W])

            def off_hidden(pair, par, _):
                dve.wait_ge(*proj_sb.rise(pair, NCH))
                dve.wait_ge(*off_ht.rise(pair - 1, 1))
                own(tt(oa[:], o1[:], row16(bo1), ALU.add))
                own(red(st16[:, 0], oa[:]))
                own(stt(oa[:], bc16(st16[:, 0]), -1.0 / O1W, oa[:], ALU.mult, ALU.add))
                own(tt(ob[:], oa[:], oa[:], ALU.mult))
                own(red(st16[:, 0], ob[:]))
                own(ts(st16[:, 1], st16[:, 0], 1.0 / O1W, ALU.mult, EPS, ALU.add))
                rsqrt(st16[:, 2], st16[:, 1], st16[:, 3], st16[:, 4])
                own(tt(oa[:], oa[:], bc16(st16[:, 2]), ALU.mult))
                own(tt(oa[:], oa[:], row16(lng), ALU.mult))
                own(tt(oa[:], oa[:], row16(lnb), ALU.add))
                own(tt(ob[:], oa[:], oa[:], ALU.mult))
                own(ts(ob[:], ob[:], 0.044715, ALU.mult, 1.0, ALU.add))
                own(tt(ob[:], ob[:], oa[:], ALU.mult))
                ts(ob[:], ob[:], -50.0, ALU.max).then_inc(off_u.sem, 1)

            def off_gelu(pair, par, _):
                dve.wait_ge(*off_e.rise(pair, 1))
                own(ts(ob[:], ob[:], 1.0, ALU.add))
                own(dve.reciprocal(ob[:], ob[:]))
                tt(oa[:], oa[:], ob[:], ALU.mult).then_inc(off_h.sem, 1)

            def off_points(pair, par, _):
                dve.wait_ge(*off_raw.rise(pair, 1))
                xy = base_xy[:].rearrange("p g n k -> p (g n k)")
                caf, cbf = (v.rearrange("p n k -> p (n k)") for v in (ca, cb))
                stt(caf, bank(3, 256, 512), 4.0, xy, ALU.mult, ALU.add).then_inc(off_rd.sem, 1)
                dve.wait_ge(*off_rd.rise(pair, 1))
                own(ts(caf, caf, 0.0, ALU.max, float(W - 1), ALU.min))
                own(ts(cbf, caf, RNE, ALU.add, RNE, ALU.subtract))
                f1 = frac2[:].rearrange("p n k s -> p (n k) s")
                own(tt(f1[:, :, 0], cbf, caf, ALU.is_gt))
                own(stt(cbf, f1[:, :, 0], -1.0, cbf, ALU.mult, ALU.add))
                own(ts(cbf, cbf, float(W - 2), ALU.min))
                own(stt(f1[:, :, 1], cbf, -1.0, caf, ALU.mult, ALU.add))
                step(ts(f1[:, :, 0], f1[:, :, 1], -1.0, ALU.mult, 1.0, ALU.add))
                idf = idxf.rearrange("p g n -> p (g n)")
                own(stt(idf, cb[:, :, 1], float(W), cb[:, :, 0], ALU.mult, ALU.add))
                base_t = table_base[:].unsqueeze(1).unsqueeze(3).to_broadcast([P, QT_N, 2, NP_])
                tt(idx[:, par].rearrange("p (t b n) -> p t b n", t=QT_N, b=2),
                        idxf.rearrange("p (t b) n -> p t b n", b=2), base_t, ALU.add).then_inc(idx_ok.sem, 1)
                cw = corner_w[:, par].rearrange("p g (n x y) -> p (g n) x y", x=2, y=2)
                n = GROUPS * NP_
                tt(cw, frac2[:, :, 0, :].unsqueeze(3).to_broadcast([P, n, 2, 2]),
                        frac2[:, :, 1, :].unsqueeze(2).to_broadcast([P, n, 2, 2]), ALU.mult).then_inc(corner_ok.sem, 1)

            def weigh(pair, par, b, t, h):
                n = b * QT_N + t
                m = 2 * n + h
                if h == 0:
                    dve.wait_ge(*gath_in[n % NG].rise(pair, 16 * NP_ * (n // NG + 1)))
                    if n == 0:
                        dve.wait_ge(*corner_ok.rise(pair, 1))
                if m >= 2:
                    dve.wait_ge(*samp_ps.rise(pair, m - 1))
                else:
                    dve.wait_ge(*samp_ps.rise(pair - 1, 4 * QT_N - 1 + m))
                g = gath[:, n % NG, 4 * h:4 * h + 4, :].rearrange("p n (k c) -> p (n k) c", c=C)
                cw = corner_w[:, par, 2 * t + b, 16 * h:16 * h + 16]
                tt(prod[h][:].rearrange("p (n c) -> p n c", c=C), g,
                   cw.unsqueeze(2).to_broadcast([P, 16, C]), ALU.mult).then_inc(wcorn.sem, 1)
                if h:
                    dve.wait_ge(*wcorn.rise(pair, m + 1))
                    dve.sem_inc(gath_rd.sem, 1)

            def scores(pair, par, b, t):
                n = b * QT_N + t
                dve.wait_ge(*kv_ps.rise(pair, n + 1))
                kv = ps[:, BANK:3 * BANK].rearrange("p (n c) -> p n c", c=2 * C)
                q = query[:, par, t, b, :].unsqueeze(1).to_broadcast([P, NP_, C])
                own(tt(kq[:].rearrange("p (n c) -> p n c", c=C), kv[:, :, 0:C], q, ALU.mult))
                own(red(pt_sc[:, 0], kq[:].rearrange("p (m d) -> p m d", d=DH)))
                sc = pt_sc[:, 0].rearrange("p (n h) -> p n h", h=NH)
                own(red(pt_st[:, 0], sc.rearrange("p n h -> p h n"), ALU.max))
                if n:
                    dve.wait_ge(*sc_exp.rise(pair, n))
                else:
                    dve.wait_ge(*sc_exp.rise(pair - 1, 2 * QT_N))
                tt(pt_sc[:, 1].rearrange("p (n h) -> p n h", h=NH), sc,
                   pt_st[:, 0].unsqueeze(1).to_broadcast([P, NP_, NH]), ALU.subtract).then_inc(sc_sub.sem, 1)

            def values(pair, par, b, t):
                n = b * QT_N + t
                dve.wait_ge(*sc_exp.rise(pair, n + 1))
                ex = pt_sc[:, 2 + n % 2]
                step(red(pt_st[:, 1], ex.rearrange("p (n h) -> p h n", h=NH)))
                for h in range(2):
                    kv = bank(1 + h).rearrange("p (n c) -> p n c", c=2 * C)[:, :, C:2 * C]
                    e = ex[:, 32 * h:32 * h + 32]
                    tt(av[:, 256 * h:256 * h + 256].rearrange("p (m d) -> p m d", d=DH),
                       kv.rearrange("p n (h d) -> p n h d", d=DH),
                       e.rearrange("p (n h) -> p n h", h=NH).unsqueeze(3).to_broadcast([P, 4, NH, DH]),
                       ALU.mult).then_inc(kv_rd.sem, 1)
                settle()
                step(dve.reciprocal(pt_st[:, 2], pt_st[:, 1]))
                dve.wait_ge(*kv_rd.rise(pair, 2 * n + 2))
                own(red(pt_o[:], av[:].rearrange("p (n c) -> p c n", c=C)))
                tt(h0[:, b, t].rearrange("p (h d) -> p h d", d=DH), pt_o[:].rearrange("p (h d) -> p h d", d=DH),
                   pt_st[:, 2].unsqueeze(2).to_broadcast([P, NH, DH]), ALU.mult).then_inc(tok.sem, 1)

            def norm(pair, par, b, k):
                src = (h0[:, b], h1, xn)[k]
                if k == 0:
                    dve.wait_ge(*txt_in[b].rise(pair, 16))
                    dve.wait_ge(*tok.rise(pair, QT_N * (b + 1)))
                elif k == 1:
                    dve.wait_ge(*o_rd.rise(pair, ST_N * (b + 1)))
                else:
                    dve.wait_ge(*stored.rise(pair, 16 * b))
                for t in range(ST_N):
                    step(dve.bn_stats(bn6[:, t, :], src[:, t, :]))
                settle()
                dve.sem_inc(dve_gate, 1)
                for t in range(ST_N):
                    step(dve.bn_aggr(mv[:, t, :], bn6[:, t, :]))
                settle()
                own(ts(ln9[:, 0], mv[:, :, 1], EPS, ALU.add))
                rsqrt(ln9[:, 6], ln9[:, 0], ln9[:, 1], ln9[:, 2])
                stt(ln9[:, 7], mv[:, :, 0], -1.0, ln9[:, 6], ALU.mult, ALU.mult).then_inc(ln_ab.sem, 1)

            def low(pair, par, b, k):
                dve.wait_ge(*ln_hi.rise(pair, 2 * b + k + 1))
                tt(xs[:, :, 1, :], xn[:], xs[:, :, 0, :].bitcast(F32), ALU.subtract).then_inc(ln_lo.sem, 1)
                if k == 0:
                    own(tt(h0[:, b], h0[:, b], bv.unsqueeze(1).to_broadcast([P, ST_N, C]), ALU.add))

            def score_max(pair, par, b, i, c):
                n = first_chunk(i) + c
                dve.wait_ge(*s_ps.rise(pair, KEY_CHUNKS * b + n + 1))
                a = c * BANK
                m = min((i + 1) * P - a, BANK)
                if c == 0 and i >= 2:
                    dve.wait_ge(*p_ps.rise(pair, KEY_CHUNKS * b + first_chunk(i - 1)))
                end = c == key_chunks(i) - 1
                plus = const[:, MASK + P - m:MASK + P] if end else zero.to_broadcast([P, m])
                one = end and c == 0
                most = att[:, 0, i:i + 1] if one else att_m[:, n:n + 1]
                dve.sem_inc(dve_gate, 1)
                dve.tensor_tensor_reduce(out=probs[i % 2][:, a:a + m], in0=bank(4 + n % 2, 0, m), in1=plus,
                                         scale=1.0, scalar=LOWEST, op0=ALU.add, op1=ALU.max,
                                         accum_out=most).then_inc(s_rd.sem, 1)
                if end:
                    dve.wait_ge(*s_rd.rise(pair, KEY_CHUNKS * b + n + 1))
                    if c:
                        own(red(att[:, 0, i:i + 1], att_m[:, n - c:n + 1], ALU.max))
                    ts(att[:, 1, i:i + 1], att[:, 0, i:i + 1], -ATT_SCALE, ALU.mult).then_inc(s_max.sem, 1)

            def heads(pair, par, b, i):
                dve.wait_ge(*s_exp.rise(pair, ST_N * b + i + 1))
                own(dve.reciprocal(att[:, 3, i:i + 1], att[:, 2, i:i + 1]))
                dve.wait_ge(*o_part.rise(pair, KEY_CHUNKS * b + first_chunk(i + 1)))
                stt(h1[:, i, :], bank(7, (i % 8) * C, (i % 8) * C + C), att[:, 3, i:i + 1],
                    h0[:, b, i, :], ALU.mult, ALU.add).then_inc(o_rd.sem, 1)

            def bc_e(v):
                return v.unsqueeze(2).to_broadcast([P, ST_N, E])

            def top2(pair, par, b):
                dve.wait_ge(*gate_ps.rise(pair, b + 1))
                rank = const[:, RANK:RANK + E].unsqueeze(1).to_broadcast([P, ST_N, E])
                own(tt(lg[:, 0], bank(7, 0, ST_N * E).rearrange("p (t e) -> p t e", e=E),
                       gateb.unsqueeze(1).to_broadcast([P, ST_N, E]), ALU.add))
                for n in range(2):
                    own(red(gs[:, n], lg[:, n], ALU.max))
                    own(tt(lg[:, 4], lg[:, n], bc_e(gs[:, n]), ALU.is_equal))
                    own(tt(lg[:, 4], lg[:, 4], rank, ALU.mult))
                    own(red(gs[:, 5], lg[:, 4], ALU.max))
                    own(tt(lg[:, 2 + n], lg[:, 4], bc_e(gs[:, 5]), ALU.is_equal))
                    if n == 0:
                        own(stt(lg[:, 1], lg[:, 2], MASKED, lg[:, 0], ALU.mult, ALU.add))
                tt(gs[:, 2], gs[:, 1], gs[:, 0], ALU.subtract).then_inc(gate_d.sem, 1)

            def gates(pair, par, b):
                dve.wait_ge(*gate_e.rise(pair, b + 1))
                own(ts(gs[:, 4], gs[:, 3], 1.0, ALU.add))
                own(dve.reciprocal(gs[:, 5], gs[:, 4]))
                own(tt(gs[:, 6], gs[:, 3], gs[:, 5], ALU.mult))
                step(tt(lg[:, 2], lg[:, 2], bc_e(gs[:, 5]), ALU.mult))
                own(tt(lg[:, 3], lg[:, 3], bc_e(gs[:, 6]), ALU.mult))
                tt(gate[:, 0:ST_N], lg[:, 2], lg[:, 3], ALU.add).then_inc(gate_ok.sem, 1)

            def add_bias(pair, par, b):
                dve.wait_ge(*bias_ps.rise(pair, b + 1))
                step(tt(xn[:, 0:QT_N], bank(7).rearrange("p (t c) -> p t c", c=C), xn[:, 0:QT_N], ALU.add))
                tt(xn[:, QT_N], bank(6, 256, 256 + C), xn[:, QT_N], ALU.add).then_inc(bias_rd.sem, 1)
                settle()
                dve.sem_inc(bias_rd.sem, 1)

            def gated_out(pair, par, b, c, half, j):
                t = CHUNKS[c][j]
                dve.wait_ge(*y_ps.rise(pair, b * NY + layer2_count(c, half, j)))
                settle()
                tt(gated[j][:, half * BANK:(half + 1) * BANK].rearrange("p (e c) -> p e c", c=C),
                   bank(6 + j).rearrange("p (e c) -> p e c", c=C),
                   gate[:, t, half * EH:(half + 1) * EH].unsqueeze(2).to_broadcast([P, EH, C]),
                   ALU.mult).then_inc(y_rd.sem, 1)

            def add_up(pair, par, b, c, j):
                dve.wait_ge(*y_rd.rise(pair, b * NY + layer2_count(c, 1, j)))
                step(red(moe[:, CHUNKS[c][j], :], gated[j].rearrange("p (e c) -> p c e", c=C)))

            def residual(pair, par, b):
                settle()
                own(tt(xn[:], moe, xn[:], ALU.add))

            def finish(pair, par, b):
                def row(v):
                    return v.unsqueeze(1).to_broadcast([P, ST_N, C])
                dve.wait_ge(*ln_x.rise(pair, 3 * b + 3))
                own(tt(out_sb[:], out_sb[:], row(gamma), ALU.mult))
                own(tt(out_sb[:], out_sb[:], row(beta), ALU.add))
                tt(out_sb[:], out_sb[:], h1[:], ALU.add).then_inc(out_ok.sem, 1)

            for v in (w_proj, w_o2, bqk, b2_diag, gate):
                step(dve.memset(v[:], 0.0))
            step(dve.memset(fm[:], 0.0))
            step(dve.memset(shared[:, 0:2 * C], 0.0))
            for b in range(2):
                step(dve.memset(table_base[:, b:b + 1], float(b * H * W)))
            settle()
            for s in signals:
                if s.spare:
                    dve.sem_inc(s.sem, s.spare)
            dve.sem_inc(setup.sem, 1)
            dve.wait_ge(*consts_in.rise(Pair(0), 16 * loads[0]))
            dve.wait_ge(act_own, 1)
            step(tt(wa_l[:], fm[:, 0, 0:NATT], wa_h[:].bitcast(F32), ALU.subtract))
            step(tt(wg_l[:], fm[:, 1, 0:E], wg_h[:].bitcast(F32), ALU.subtract))
            step(tt(w1_l[:], gath[:, 0].rearrange("p a b -> p (a b)"), w1_h[:].bitcast(F32), ALU.subtract))
            step(dve.memset(base_xy[:], 0.0))
            settle()
            bxy = base_xy[:].rearrange("p (t b) n k -> p t (b n) k", b=2)
            own(stt(base_xy[:].rearrange("p g n k -> p g (n k)"), bo2.unsqueeze(1).to_broadcast([P, GROUPS, 16]), 4.0,
                    base_xy[:].rearrange("p g n k -> p g (n k)"), ALU.mult, ALU.add))
            own(ts(bxy[:, :, :, 0], bxy[:, :, :, 0], const[:, GX:GX + 1], ALU.add))
            own(tt(bxy[:, :, :, 1], bxy[:, :, :, 1],
                   const[:, GY:GY + QT_N].unsqueeze(2).to_broadcast([P, QT_N, 2 * NP_]), ALU.add))
            dve.wait_ge(*spare_rows.rise(Pair(0), 64))
            dve.sem_inc(setup.sem, 2)

            done = [None, 0]

            def stretch(n, pair):
                last, count = done
                if last is not None:
                    assert steps[0] == count + STEPS[last], ("steps", last, steps[0] - count)
                if n == 2:
                    steps[0] = 0
                    before[0] = (pair, setup_steps + STEPS[0] + STEPS[1] - STEPS[2])
                    done[:] = [n, 0]
                elif n == 3:
                    before[0] = None
                    steps[0] = setup_steps + STEPS[0] + STEPS[1] + STEPS[2] * (PAIRS - 2)
                    done[:] = [n, steps[0]]
                else:
                    done[:] = [n, steps[0]]

            setup_steps = steps[0]
            drive(dve, {"off_hidden": off_hidden, "off_gelu": off_gelu, "off_points": off_points,
                        "weigh": weigh, "scores": scores, "values": values, "norm": norm, "low": low,
                        "score_max": score_max, "heads": heads, "top2": top2, "gates": gates,
                        "add_bias": add_bias, "gated": gated_out, "add_up": add_up, "residual": residual,
                        "finish": finish}, stretch)


STEPS = (34, 268, 406, 372, 138)


def kernel(**inputs):
    import concourse.bacc as bacc
    from concourse.bass_utils import run_bass_kernel_spmd as run

    a = {k: np.ascontiguousarray(v) for k, v in inputs.items()}
    arrays = {
        "x": a["x"], "txt": a["txt"], "const": constants(),
        "Wq_t": a["L0_tok_W_q"].T, "Wk_t": a["L0_tok_W_k"].T, "Wv_t": a["L0_tok_W_v"].T,
        "W_o1": a["L0_tok_W_o1"], "b_o1": a["L0_tok_b_o1"], "ln_g": a["L0_tok_ln_g"], "ln_b": a["L0_tok_ln_b"],
        "W_o2": a["L0_tok_W_o2"], "b_o2": a["L0_tok_b_o2"],
        "aWq": a["L0_attn_Wq"], "abq": a["L0_attn_bq"], "aWk": a["L0_attn_Wk"], "abk": a["L0_attn_bk"],
        "aWv": a["L0_attn_Wv"], "abv": a["L0_attn_bv"],
        "gate_w": a["L0_ffn_gate_w"], "gate_b": a["L0_ffn_gate_b"], "w1": a["L0_ffn_w1"],
        "b1_t": a["L0_ffn_b1"].T, "w2": a["L0_ffn_w2"], "b2": a["L0_ffn_b2"],
        "gamma": a["L0_ffn_gamma"], "beta": a["L0_ffn_beta"],
    }
    arrays = {f"in_{k}": np.ascontiguousarray(v) for k, v in arrays.items()}
    nc = bacc.Bacc("TRN2", target_bir_lowering=False, num_devices=1)
    nc.disable_value_cache = True
    w = {k[3:]: nc.dram_tensor(k, v.shape, mybir.dt.from_np(v.dtype), kind="ExternalInput").ap()
         for k, v in arrays.items()}
    out = nc.dram_tensor("out_0", (B, S, C), F32, kind="ExternalOutput").ap()
    tables = [nc.dram_tensor(f"table{n}", (2 * H * W, 2 * C), F32, kind="Internal").ap() for n in range(2)]
    build(nc, w["x"], w["txt"], w, out, tables)
    r = run(nc, [arrays], core_ids=[0])
    return r.results[0]["out_0"]
```

```python
from contextlib import ExitStack

import concourse.bass as bass
from concourse import mybir
import numpy as np

F32 = mybir.dt.float32
F32R = mybir.dt.float32r
I32 = mybir.dt.int32
U32 = mybir.dt.uint32
ALU = mybir.AluOpType
ACT = mybir.ActivationFunctionType
X_AXIS = mybir.AxisListType.X

P = 128
B, C, H, W = 32, 64, 128, 128
TXT = 128
PAIRS = B // 2
GRID = 32
NQ = GRID * GRID
QT_N = NQ // P
S = NQ + TXT
ST_N = S // P
NP_, NH, DH = 8, 8, 8
F, E = 128, 16
O1W = C // 4
GROUPS = 2 * QT_N
NCH = QT_N
CR = H // NCH
HR = CR // 2
NG = 4
EPS = 1e-5
RNE = 8388608.0
RSQRT_SEED = float(0x5F3759DF)
MASKED = -1.0e30
LOWEST = -3.4e38
QK_SCALE = DH ** -0.5
ATT_SCALE = C ** -0.5
CHUNKS = [(a, min(512, S - a)) for a in range(0, S, 512)]
NZ = len(CHUNKS) * E
NY = NZ // 2
NHID = 10
BANK = 512


def grid_coordinates():
    step = np.arange(GRID, dtype=np.float32) / np.float32(GRID - 1)
    ref = np.float32(-1.0) * (np.float32(1.0) - step) + np.float32(1.0) * step
    pix = (ref + np.float32(1.0)) * np.float32(0.5) * np.float32(W - 1)
    low = np.clip(np.floor(pix), 0, W - 2).astype(np.int64)
    return pix.astype(np.float32), low, np.clip(pix - low, 0, 1).astype(np.float32)


IDENT, ZERO, MASK, GX, GY, RANK, SELECT, HALVES, GRIDW = 0, 128, 512, 640, 641, 649, 665, 681, 745
NCONST = GRIDW + GRID * 2 * GRID


def constants():
    pix, low, frac = grid_coordinates()
    c = np.zeros((P, NCONST), np.float32)
    c[:, IDENT:IDENT + P] = np.eye(P, dtype=np.float32)
    c[:, MASK:MASK + P] = np.where(np.arange(P)[None, :] > np.arange(P)[:, None], np.float32(MASKED), np.float32(0))
    c[:, GX] = pix[np.arange(P) % GRID]
    for t in range(QT_N):
        c[:, GY + t] = pix[4 * t + np.arange(P) // GRID]
    c[:, RANK:RANK + E] = E - np.arange(E)
    c[:, SELECT:SELECT + E] = np.arange(P)[:, None] % E == np.arange(E)
    c[:, HALVES:HALVES + C] = np.arange(P)[:, None] % C == np.arange(C)
    m = c[:, GRIDW:].reshape(P, GRID, 2, GRID)
    for i in range(GRID):
        for k, wy in ((0, np.float32(1) - frac[i]), (1, frac[i])):
            for j in range(GRID):
                m[low[j], i, k, j] += wy * (np.float32(1) - frac[j])
                m[low[j] + 1, i, k, j] += wy * frac[j]
    return c


def key_chunks(i):
    return (i + 4) // 4


def first_chunk(i):
    return sum(key_chunks(k) for k in range(i))


KEY_CHUNKS = first_chunk(ST_N)

def token_stages():
    order = [("weigh", (0,))]
    for t in range(QT_N + 1):
        for h in range(2):
            if t < QT_N:
                order += [("turn", (t, h)), ("turned", (t, h))]
            if t and h == 0:
                order += [*[("scores", (t - 1,))] * 4, ("point_exp", (t - 1,))]
            elif t:
                order += [*[("values", (t - 1,))] * 3, ("stats", (0, t - 1))]
        if t < QT_N - 1:
            order += [("weigh", (t + 1,))]
        if t < QT_N:
            order += [("key_values", (t, 0)), ("key_values", (t, 1))]
    return order


def norm_stages(k):
    order = []
    for n in range(5):
        for lag, names in ((0, ("normalize",)), (1, ("high", "low")), (2, ("turn_tokens", "copy_tokens"))):
            if 0 <= n - lag < 3:
                order += [(name, (k, n - lag)) for name in names]
    return order


def block_stages():
    order = [("stats", (0, QT_N)), ("moments", (0,)), *[("scale", (0,))] * 13, *norm_stages(0),
             ("project_q", ()), ("copy_q", ()),
             ("project_k", ()), ("copy_k", ()), ("project_v", ()), ("copy_v", ())]

    def score(i):
        o = []
        for c in range(key_chunks(i)):
            o += [("score", (i, c)), ("score_max", (i, c))]
        return o + [("soft", (i,))]

    order += score(0)
    waiting = []
    for i in range(ST_N):
        if i + 1 < ST_N:
            order += score(i + 1)
        for c in range(key_chunks(i)):
            order += [("turn_probs", (i, c)), ("copy_probs", (i, c))] + waiting
            waiting = [("attend", (i, c))] + ([("heads", (i,)), ("stats", (1, i))] if c == key_chunks(i) - 1 else [])
    order += waiting
    order += [("moments", (1,)), *[("scale", (1,))] * 13, *norm_stages(1), ("gate_logits", ())]
    after = {1: [*[("top2", ())] * 3], 2: [*[("top2", ())] * 5], 3: [*[("top2", ())] * 5, ("gate_exp", ())],
             4: [*[("gates", ())] * 5, ("gate_high", ())],
             5: [("gate_low", ()), ("turn_gates", (0,)), ("copy_gates", (0,)), ("turn_gates", (1,)),
                 ("copy_gates", (1,))], 6: [("spread", (0,)), ("spread", (1,)), ("gated", (0,))]}
    for n in range(NZ):
        if n >= 2:
            after.setdefault(n + AHEAD, []).append(("spread", (n,)))
        if n >= 1:
            after.setdefault(n + AHEAD + LAG_G, []).append(("gated", (n,)))
        after.setdefault(n + AHEAD + LAG_Y + 1, []).append(("layer2", (n // 2, n % 2)))
        if n % E == E - 1:
            after.setdefault(n + AHEAD + LAG_Y + 1, []).append(("copy_y", (n // E,)))
    for n in range(max(after) + 1):
        if n < NZ:
            order += [("layer1", (n,)), ("relu", (n,))]
        order += after.get(n, [])
    return order + [("turn_back", ())]


def end_stages():
    return [("residual", ()), *[("stats", (2, t)) for t in range(ST_N)], ("moments", (2,)),
            *[("scale", (2,))] * 13, *[("normalize", (2, c)) for c in range(3)],
            *[("finish", ())] * 3, ("store", ())]


def grid_stages(chunks):
    order = []
    for ch in chunks:
        if ch == chunks[0]:
            order += [("load", (2 * ch,)), ("load", (2 * ch + 1,))]
        for half in range(2):
            for g in range(2):
                order += [("rows", (ch, half, g)), ("copy_rows", (ch, half, g))]
            if ch != chunks[-1]:
                order += [("load", (2 * ch + 2 + half,))]
        order += [("table", (ch,)), ("sample", (ch,)), ("feature", (ch,)),
                  ("turn_feature", (ch,)), ("feature_t", (ch,)), ("query", (ch,)), ("copy_query", (ch,))]
    if chunks[-1] == NCH - 1:
        order += [*[("off_hidden", ())] * 24, ("off_exp", ()), *[("off_gelu", ())] * 3, ("off_turn", ()),
                  ("off_copy", ()), ("off_layer2", ()), *[("off_points", ())] * 8]
    return order


SHARES = {"weigh": 2, "turn": 2, "turned": 2, "scores": 1, "point_exp": 1, "values": 1, "key_values": 1,
          "stats": 1, "moments": 5, "scale": 1, "normalize": 5, "high": 2, "low": 2, "turn_tokens": 1,
          "copy_tokens": 1, "project_q": 3, "copy_q": 3, "project_k": 3, "copy_k": 3, "project_v": 3,
          "copy_v": 3, "score": 2, "score_max": 2, "soft": 2, "turn_probs": 2, "copy_probs": 2, "attend": 1,
          "heads": 1, "gate_logits": 3, "top2": 2, "gate_exp": 1, "gates": 1, "gate_high": 1, "gate_low": 1,
          "turn_gates": 2, "copy_gates": 2, "spread": 1, "gated": 1, "layer2": 2, "copy_y": 1, "layer1": 1,
          "relu": 1, "turn_back": 2, "residual": 1, "finish": 1, "store": 1, "load": 1, "rows": 1,
          "copy_rows": 1, "table": 0, "sample": 2, "feature": 1, "turn_feature": 1, "feature_t": 1,
          "query": 1, "copy_query": 1, "off_hidden": 1, "off_exp": 2, "off_gelu": 1, "off_turn": 1,
          "off_copy": 1, "off_layer2": 1, "off_points": 1, "text": 0}
SMALL = 0.4
AHEAD = 5
LAG_G, LAG_Y = 1, 2
TOKENS_END = 0.98
END_AT = 0.02, 0.2
GRID_AT = (0.02, 0.98), (0.0, 0.85)
GRID_FIRST = 5


def share(stage, args):
    k = args[0] * 2 if stage == "layer2" else args[0] if stage in ("layer1", "relu", "spread", "gated") else 0
    return SHARES[stage] * (SMALL if k >= NZ - E else 1)


def merge(*threads):
    placed = []
    for name, stages, begin, end in threads:
        total, at = sum(share(*s) for s in stages), 0
        for stage, args in stages:
            placed.append((begin + (end - begin) * at / total, len(placed), name, stage, args))
            at += share(stage, args)
    return [p[2:] for p in sorted(placed)]


def slot_order(slot, first, last):
    threads = [("tokens", [("text", ())] + token_stages(), 0.0, TOKENS_END)]
    if slot or not first:
        threads.append(("block", block_stages(), 0.0, 1.0))
    if not first:
        threads.append(("end", end_stages(), *END_AT))
    if not last:
        chunks = range(GRID_FIRST) if slot == 0 else range(GRID_FIRST, NCH)
        threads.append(("grid", grid_stages(chunks), *GRID_AT[slot]))
    return merge(*threads)


class Pair:

    def __init__(self, off, eng=None, turn=None):
        self.off, self.eng, self.turn, self.products = off, eng, turn, {}

    def __add__(self, n):
        p = Pair(self.off + n, self.eng, self.turn)
        p.products = self.products
        return p

    def __sub__(self, n):
        return self + -n

    def times(self, per, k=0):
        if self.turn is None:
            return self.off * per + k
        if per not in self.products:
            self.products[per] = self.eng.snap(self.turn * (2 * per))
        return self.products[per] + (self.off * per + k)


class Signal:

    def __init__(self, sem, per, spare=0):
        self.sem, self.per, self.spare = sem, per, spare

    def rise(self, pair, k):
        assert pair.off * self.per + k + self.spare > 0, "a wait's value has to stay positive"
        return self.sem, pair.times(self.per, k + self.spare)


def build(nc, x, txt, w, out, tables):
    _, LOW, _ = grid_coordinates()
    ctx = ExitStack()
    with ctx:
        def sb(name, shape, dt=F32):
            return ctx.enter_context(nc.sbuf_tensor(name, shape, dt))

        signals = []

        def sig(name, per, spare=0):
            s = Signal(ctx.enter_context(nc.semaphore(name)), per, spare)
            signals.append(s)
            return s

        const = sb("const", [P, NCONST])
        ident = const[:, IDENT:IDENT + P]
        zero = const[:, ZERO:ZERO + 1]
        gridw = const[:, GRIDW:].rearrange("p (i k j) -> p i k j", i=GRID, k=2)
        w_proj = sb("w_proj", [P, 2 * (C + O1W)])
        w_o2 = sb("w_o2", [P, P])
        w_kv = sb("w_kv", [P, 2 * C])
        rows16 = sb("rows16", [P, 5, 16])
        bo1, lng, lnb, bo2, gateb = (rows16[:, n, :] for n in range(5))
        rows64 = sb("rows64", [P, 3, C])
        bv, gamma, beta = (rows64[:, n, :] for n in range(3))
        bqk = sb("bqk", [P, 2])
        b1 = sb("b1", [P, E])
        NATT = 2 * P + C
        wa_h = sb("wa_h", [P, NATT], F32R)
        wa_l = sb("wa_l", [P, NATT], F32R)
        wg_h = sb("wg_h", [P, E], F32R)
        wg_l = sb("wg_l", [P, E], F32R)
        w1_h = sb("w1_h", [P, E * F], F32R)
        w1_l = sb("w1_l", [P, E * F], F32R)
        w2 = sb("w2", [P, E * C])
        b2_h = sb("b2_h", [2 * E, P], F32R)
        b2_l = sb("b2_l", [2 * E, P], F32R)
        select = sb("select", [2 * E, E], F32R)

        fm = sb("fm", [P, 2, HR * W])
        rows = sb("rows", [P, 2, 2, CR + 1, C])
        qf = sb("qf", [P, P])
        qft = sb("qft", [P, P])
        query = sb("query", [P, 2, QT_N, 2, C])
        o1 = sb("o1", [P, GROUPS, O1W])
        oa = sb("oa", [P, GROUPS, O1W])
        ob = sb("ob", [P, GROUPS, O1W])
        oht = sb("oht", [P, 2, P])
        st16 = sb("st16", [P, 5, GROUPS])
        base_xy = sb("base_xy", [P, GROUPS, NP_, 2])
        ca = oa[:].rearrange("p g (n k) -> p (g n) k", k=2)
        cb = ob[:].rearrange("p g (n k) -> p (g n) k", k=2)
        frac2 = sb("frac2", [P, GROUPS * NP_, 2, 2])
        idxf = o1[:].rearrange("p g n -> p (g n)")[:, 0:GROUPS * NP_].rearrange("p (g n) -> p g n", n=NP_)
        idx = sb("idx", [P, 2, GROUPS * NP_], U32)
        corner_w = sb("corner_w", [P, 2, GROUPS, NP_ * 4])
        table_base = sb("table_base", [P, 2])
        gath = sb("gath", [P, NG, NP_, 4 * C])

        prod = [sb(f"prod{n}", [P, 1024]) for n in range(2)]
        samp_t = [sb(f"samp_t{n}", [P, 1024]) for n in range(2)]
        kq = sb("kq", [P, 512])
        av = sb("av", [P, 512])
        shared = sb("shared", [P, 2 * S])
        probs = [shared[:, n * S:(n + 1) * S] for n in range(2)]
        y_t = shared[:, 0:S]
        probs_t = [sb(f"probs_t{n}", [P, BANK]) for n in range(3)]
        shared2 = sb("shared2", [P, NHID * BANK])
        q_t, k_t = shared2[:, 0:S], shared2[:, S:2 * S]
        hid = [shared2[:, n * BANK:(n + 1) * BANK] for n in range(NHID)]

        pt_sc = sb("pt_sc", [P, 4, NP_ * NH])
        pt_st = sb("pt_st", [P, 3, NH])
        pt_o = sb("pt_o", [P, C])
        h0 = sb("h0", [P, 2, ST_N, C])
        h1 = sb("h1", [P, 2, ST_N, C])
        xn = sb("xn", [P, ST_N, C])
        xs = sb("xs", [P, ST_N, 2, C], F32R)
        xt = sb("xt", [P, S], F32R)
        v_sb = sb("v_sb", [P, ST_N, C])
        bn6 = sb("bn6", [P, ST_N, 6])
        mv = sb("mv", [P, ST_N, 2])
        ln9 = sb("ln9", [P, 5, ST_N])
        bn6_1 = sb("bn6_1", [P, ST_N, 6])
        bn6_e = sb("bn6_e", [P, ST_N, 6])
        mv_e = sb("mv_e", [P, ST_N, 2])
        ln9_e = sb("ln9_e", [P, 5, ST_N])
        att = sb("att", [P, 4, ST_N])
        att_m = sb("att_m", [P, KEY_CHUNKS])
        lg = sb("lg", [P, 5, ST_N, E])
        gs = sb("gs", [P, 8, ST_N])
        gate = sb("gate", [P, ST_N, E])
        gate_hl = sb("gate_hl", [P, ST_N, 2, E], F32R)
        gate_t = sb("gate_t", [2 * E, S], F32R)
        out_sb = sb("out_sb", [P, ST_N, C])

        ps = ctx.enter_context(nc.psum_tensor("ps", [P, 8 * BANK], F32))

        def bank(n, a=0, b=BANK):
            return ps[:, n * BANK + a:n * BANK + b]

        consts_in = sig("consts_in", 0)
        setup = sig("setup", 0)
        ready = sig("ready", 0)
        fm_in = [sig(f"fm_in{n}", 16 * NCH) for n in range(2)]
        rows_ps = sig("rows_ps", 4 * NCH, 16)
        rows_sb = sig("rows_sb", 4 * NCH)
        carry = sig("carry", NCH)
        table_in = [sig(f"table_in{n}", 32 * NCH // 2, 16) for n in range(2)]
        qf_ps, qf_sb = sig("qf_ps", NCH, 16), sig("qf_sb", NCH)
        qft_ps, qft_sb = sig("qft_ps", NCH), sig("qft_sb", NCH)
        proj_ps, proj_sb = sig("proj_ps", NCH), sig("proj_sb", NCH, 16)
        off_u = sig("off_u", 1)
        off_e = sig("off_e", 1)
        off_h, off_ht = sig("off_h", 1), sig("off_ht", 1, 16)
        off_hsb, off_raw = sig("off_hsb", 1), sig("off_raw", 1)
        off_rd = sig("off_rd", 1, 2)
        idx_ok = sig("idx_ok", 1, 16)
        corner_ok = sig("corner_ok", 1)
        gath_in = [sig(f"gath_in{n}", 2 * QT_N // NG * 16 * NP_) for n in range(NG)]
        wcorn = [sig(f"wcorn{n}", 2 * QT_N, 24) for n in range(2)]
        samp_ps = sig("samp_ps", 4 * QT_N, 16)
        samp_sb = sig("samp_sb", 4 * QT_N, 16)
        kv_ps = sig("kv_ps", 2 * QT_N, 16)
        sc_sub = sig("sc_sub", 2 * QT_N)
        sc_exp = sig("sc_exp", 2 * QT_N, 16)
        kv_rd = sig("kv_rd", 4 * QT_N, 16)
        tok = sig("tok", 2 * QT_N, 24)
        txt_in = [sig(f"txt_in{n}", 16) for n in range(2)]
        ln_ab, end_ab = sig("ln_ab", 4), sig("end_ab", 2)
        ln_x, end_x = sig("ln_x", 12, 16), sig("end_x", 6)
        ln_hi = sig("ln_hi", 12)
        ln_lo = sig("ln_lo", 12)
        xt_ps = sig("xt_ps", 4 * 3)
        xt_sb = sig("xt_sb", 4 * 3)
        q_ps, q_sb = sig("q_ps", 6), sig("q_sb", 6)
        k_ps, k_sb = sig("k_ps", 6), sig("k_sb", 6)
        v_ps, v_cp = sig("v_ps", 2), sig("v_cp", 4)
        s_ps = sig("s_ps", 2 * KEY_CHUNKS)
        s_rd = sig("s_rd", 2 * KEY_CHUNKS)
        s_max = sig("s_max", 2 * ST_N)
        s_exp = sig("s_exp", 2 * ST_N)
        p_ps, p_sb = sig("p_ps", 2 * KEY_CHUNKS), sig("p_sb", 2 * KEY_CHUNKS)
        o_part = sig("o_part", 2 * KEY_CHUNKS)
        o_rd = sig("o_rd", 2 * ST_N)
        gate_ps = sig("gate_ps", 2)
        gate_d = sig("gate_d", 2)
        gate_e = sig("gate_e", 2)
        gate_ok = sig("gate_ok", 2)
        gate_hi, gate_lo = sig("gate_hi", 2), sig("gate_lo", 2)
        gate_turn, gate_tsb = sig("gate_turn", 6), sig("gate_tsb", 6)
        z_ps, z_sb = sig("z_ps", 2 * NZ), sig("z_sb", 2 * NZ, 16)
        g_ps = sig("g_ps", 2 * NZ)
        h_ok = sig("h_ok", 2 * NZ, 16)
        y_ps, y_sb = sig("y_ps", 2 * NY), sig("y_sb", 2 * len(CHUNKS), 16)
        back_ps, back_rd = sig("back_ps", 2), sig("back_rd", 4, 16)
        out_ok = sig("out_ok", 2, 16)
        y_ok = sig("y_ok", 2)
        stored = sig("stored", 32, 48)
        spare_rows = sig("spare_rows", 0)
        vec = ctx.enter_context(nc.semaphore("vec"))
        act_own = ctx.enter_context(nc.semaphore("act_own"))
        pool_gate = ctx.enter_context(nc.semaphore("pool_gate"))
        dve_gate = ctx.enter_context(nc.semaphore("dve_gate"))

        loads = [0]

        block = ctx.enter_context(nc.Block())

        thread = [None]

        def follow(stages, pair, par, slot, first, last):
            who = {"tokens": (pair, par, slot), "grid": (pair + 1, 1 - par, None),
                   "block": (pair, par, 0) if slot else (pair - 1, 1 - par, 1),
                   "end": (pair - 1, 1 - par, slot)}
            for thread[0], stage, args in slot_order(slot, first, last):
                if stage in stages:
                    stages[stage](*who[thread[0]], *args)
            thread[0] = None

        def drive(eng, stages, stretch):
            stretch(0, None)
            for stage, args in grid_stages(range(NCH)):
                if stage in stages:
                    stages[stage](Pair(0), 0, None, *args)
            stretch(1, None)
            for slot in range(2):
                follow(stages, Pair(0), 0, slot, True, False)
            with eng.Fori(0, PAIRS // 2 - 1) as j:
                for par in (1, 0):
                    pair = Pair(2 - par, eng, j)
                    stretch(2, pair)
                    for slot in range(2):
                        follow(stages, pair, par, slot, False, False)
            stretch(3, None)
            for slot in range(2):
                follow(stages, Pair(PAIRS - 1), 1, slot, False, True)
            stretch(4, None)
            for thread[0], stage, args in merge(("block", block_stages(), 0.0, 1.0), ("end", end_stages(), *END_AT)):
                if stage in stages:
                    stages[stage](Pair(PAIRS - 1), 1, 1 if thread[0] == "block" else 0, *args)
            thread[0] = None
            for stage, args in end_stages():
                if stage in stages:
                    stages[stage](Pair(PAIRS - 1), 1, 1, *args)
            stretch(5, None)

        def unseen(n, pair):
            pass

        x_v = x.rearrange("(n b) c (m r) w -> n (b c) m (r w)", b=2, r=HR)
        tab_v = [t.rearrange("(b y x) c -> b y x c", y=H, x=W) for t in tables]
        out_v = out.rearrange("b (t p) c -> b p t c", p=P)

        @block.sync
        def _(sp):
            def load(dst, src):
                loads[0] += 1
                sp.dma_start(dst, src).then_inc(consts_in.sem, 16)

            sp.wait_ge(*setup.rise(Pair(0), 1))
            load(const[:], w["const"])
            for b in range(2):
                r, c0 = slice(64 * b, 64 * b + 64), b * (C + O1W)
                load(w_proj[r, c0:c0 + C], w["Wq_t"])
                load(w_proj[r, c0 + C:c0 + C + O1W], w["W_o1"])
                load(w_kv[r, 0:C], w["Wk_t"])
                load(w_kv[r, C:2 * C], w["Wv_t"])
                load(fm[r, 0, 0:C], w["aWq"])
                load(fm[r, 0, 128:128 + C], w["aWk"])
                load(fm[r, 0, 256:256 + C], w["aWv"])
                load(fm[r, 1, 0:E], w["gate_w"])
                load(gath[r, 0:1].rearrange("p a b c -> p (a b c)").rearrange("p (e f) -> p e f", f=F),
                     w["w1"].rearrange("e c f -> c e f"))
            for g in range(8):
                load(w_o2[16 * g:16 * g + 16, 16 * g:16 * g + 16], w["W_o2"])
            for n, name in enumerate(("b_o1", "ln_g", "ln_b", "b_o2", "gate_b")):
                load(rows16[:, n, :], w[name].unsqueeze(0).to_broadcast([P, 16]))
            for n, name in enumerate(("abv", "gamma", "beta")):
                load(rows64[:, n, :], w[name].unsqueeze(0).to_broadcast([P, C]))
            load(bqk[0:C, 0:1], w["abq"].unsqueeze(1))
            load(bqk[0:C, 1:2], w["abk"].unsqueeze(1))
            load(b1[:], w["b1_t"])
            load(w2[:].rearrange("p (e c) -> p e c", c=C), w["w2"].rearrange("e f c -> f e c"))
            for n in range(2):
                load(fm[n * E:(n + 1) * E, 1, E:E + C], w["b2"])

            def load_rows(pair, par, _, hc):
                if hc >= 2:
                    sp.wait_ge(*rows_ps.rise(pair, 2 * (hc - 1)))
                else:
                    sp.wait_ge(*rows_ps.rise(pair - 1, 4 * NCH - 2 * (1 - hc)))
                sp.dma_start(fm[:, hc % 2, :], x_v[pair.times(1), :, hc, :]).then_inc(fm_in[hc % 2].sem, 16)

            def write_table(pair, par, _, ch):
                sp.wait_ge(*rows_sb.rise(pair, 4 * (ch + 1)))
                sp.wait_ge(*carry.rise(pair, ch + 1))
                if ch == 0:
                    for n in range(2):
                        sp.wait_ge(*wcorn[n].rise(pair - 2, 2 * QT_N))
                n = CR if ch else CR - 1
                first = 0 if ch else 1
                y0 = ch * CR + first - 1
                for b in range(2):
                    src = rows[:, ch % 2, b, first:first + n, :]
                    src = bass.AP(tensor=src.tensor, offset=src.offset,
                                  ap=[list(src.ap[0]), [C, n], [1, 2 * C]])
                    dst = tab_v[par][b, y0:y0 + n].rearrange("y x c -> x y c")
                    sp.dma_start(dst, src).then_inc(table_in[ch % 2].sem, 16)

            def text(pair, par, b):
                sp.wait_ge(*ln_x.rise(pair - 1, 6 * b + 6))
                sp.dma_start(h0[:, b, QT_N, :], txt[pair.times(2, b)]).then_inc(txt_in[b].sem, 16)

            def store(pair, par, b):
                sp.wait_ge(*out_ok.rise(pair, b + 1))
                sp.dma_start(out_v[pair.times(2, b)], out_sb[:]).then_inc(stored.sem, 16)

            for t in tab_v:
                for b in range(2):
                    sp.dma_start(t[b, H - 1, :, :], shared[:, 0:2 * C]).then_inc(spare_rows.sem, 16)
            sp.wait_ge(*ready.rise(Pair(0), 1))
            drive(sp, {"load": load_rows, "table": write_table, "text": text, "store": store}, unseen)
            sp.wait_ge(*stored.rise(Pair(PAIRS), 0))

        @block.gpsimd
        def _(pool):
            pool.wait_ge(*setup.rise(Pair(0), 2))
            pool.wait_ge(*spare_rows.rise(Pair(0), 64))

            def weigh(pair, par, n):
                b, t = n // QT_N, n % QT_N
                if n == 0:
                    pool.wait_ge(*corner_ok.rise(pair, 1))
                pool.wait_ge(*gath_in[n % NG].rise(pair, 16 * NP_ * (n // NG + 1)))
                pool.wait_ge(*(samp_ps.rise(pair, 2 * n) if n else samp_ps.rise(pair - 1, 4 * QT_N)))
                pool.sem_inc(pool_gate, 1)
                g = gath[:, n % NG, 4:8, :].rearrange("p n (k c) -> p (n k) c", c=C)
                cw = corner_w[:, par, 2 * t + b, 16:32]
                pool.tensor_tensor(prod[1][:].rearrange("p (n c) -> p n c", c=C), g,
                                   cw.unsqueeze(2).to_broadcast([P, 16, C]), ALU.mult).then_inc(wcorn[1].sem, 1)

            def gather(pair, par):
                pool.wait_ge(*idx_ok.rise(pair, 1))
                for n in range(2):
                    pool.wait_ge(*table_in[n].rise(pair, 32 * NCH // 2))
                for b in range(2):
                    for t in range(QT_N):
                        n = b * QT_N + t
                        for h in range(2):
                            pool.wait_ge(*wcorn[h].rise(pair, n + 1 - NG))
                        pool.sem_inc(pool_gate, 1)
                        for p in range(NP_):
                            k = (t * 2 + b) * NP_ + p
                            pool.indirect_dma_start(
                                out=gath[:, n % NG, p, :], out_offset=None, in_=tables[par],
                                in_offset=bass.IndirectOffsetOnAxis(ap=idx[:, par, k:k + 1], axis=0),
                            ).then_inc(gath_in[n % NG].sem, 16)
                        if n:
                            weigh(pair, par, n - 1)
                weigh(pair, par, 2 * QT_N - 1)

            with pool.Fori(0, PAIRS // 2) as j:
                gather(Pair(0, pool, j), 0)
                gather(Pair(1, pool, j), 1)

        @block.tensor
        def _(pe):
            def rows_turn(pair, par, _, ch, half, g):
                n = 4 * ch + 2 * half + g
                if g == 0:
                    pe.wait_ge(*fm_in[half].rise(pair, 16 * (ch + 1)))
                if half or g:
                    pe.wait_ge(*rows_sb.rise(pair, n))
                elif ch:
                    pe.wait_ge(*proj_sb.rise(pair, ch))
                else:
                    pe.wait_ge(*off_rd.rise(pair - 1, 1))
                for r in range(4):
                    last = pe.transpose(bank(3, r * P, r * P + P),
                                        fm[:, half, (4 * g + r) * W:(4 * g + r + 1) * W], ident)
                last.then_inc(rows_ps.sem, 1)

            def sample(pair, par, _, t):
                pe.wait_ge(*rows_sb.rise(pair, 4 * (t + 1)))
                for i in range(4 * t, 4 * t + 4):
                    for k in range(2):
                        r = 1 + int(LOW[i]) + k - CR * t
                        assert 1 <= r <= CR
                        last = pe.matmul(bank(3, 0, P)[32 * (i % 4):32 * (i % 4) + 32],
                                         gridw[:, i, k, :], rows[:, t % 2, :, r, :],
                                         start=(k == 0), stop=(k == 1))
                last.then_inc(qf_ps.sem, 1)

            def turn_feature(pair, par, _, t):
                pe.wait_ge(*qf_sb.rise(pair, t + 1))
                pe.transpose(bank(3, 128, 256), qf[:], ident).then_inc(qft_ps.sem, 1)

            def queries(pair, par, _, t):
                pe.wait_ge(*qft_sb.rise(pair, t + 1))
                pe.matmul(bank(3, 256, 256 + 2 * (C + O1W)), qft[:], w_proj[:],
                          start=True, stop=True).then_inc(proj_ps.sem, 1)

            def off_turn(pair, par, _):
                pe.wait_ge(*off_h.rise(pair, 1))
                pe.wait_ge(*proj_sb.rise(pair, NCH))
                for n in range(2):
                    last = pe.transpose(bank(3, n * P, n * P + P),
                                        oa[:].rearrange("p g c -> p (g c)")[:, n * P:n * P + P], ident)
                last.then_inc(off_ht.sem, 1)

            def off_layer2(pair, par, _):
                pe.wait_ge(*off_hsb.rise(pair, 1))
                for n in range(2):
                    last = pe.matmul(bank(3, 256 + n * P, 256 + n * P + P), oht[:, n, :], w_o2[:],
                                     start=True, stop=True)
                last.then_inc(off_raw.sem, 1)

            def turn(pair, par, b, t, h):
                m = 2 * (b * QT_N + t) + h
                pe.wait_ge(*wcorn[h].rise(pair, b * QT_N + t + 1))
                if m:
                    pe.wait_ge(*samp_sb.rise(pair, m))
                else:
                    pe.wait_ge(*samp_sb.rise(pair - 1, 4 * QT_N))
                for p in range(4):
                    for dx in range(2):
                        last = pe.matmul(bank(0, p * P, p * P + P),
                                         prod[h][:, (p * 2 + dx) * P:(p * 2 + dx + 1) * P], ident,
                                         is_transpose=True, start=(dx == 0), stop=(dx == 1))
                last.then_inc(samp_ps.sem, 1)

            def key_values(pair, par, b, t, h):
                n = b * QT_N + t
                pe.wait_ge(*samp_sb.rise(pair, 2 * n + h + 1))
                if n:
                    pe.wait_ge(*kv_rd.rise(pair, 2 * (n - 1) + h + 1))
                else:
                    pe.wait_ge(*kv_rd.rise(pair - 1, 4 * QT_N - 1 + h))
                for p in range(4):
                    last = pe.matmul(bank(1 + h, p * P, p * P + P),
                                     samp_t[n % 2][:, (4 * h + p) * P:(4 * h + p + 1) * P], w_kv[:],
                                     start=True, stop=True)
                if h:
                    last.then_inc(kv_ps.sem, 1)

            def turn_tokens(pair, par, b, k, c):
                n = 3 * (2 * b + k) + c
                pe.wait_ge(*ln_lo.rise(pair, n + 1))
                if k:
                    pe.wait_ge(*s_rd.rise(pair, KEY_CHUNKS * (b + 1)))
                    pe.wait_ge(*p_sb.rise(pair, KEY_CHUNKS * (b + 1)))
                else:
                    before = (pair, 1) if b else (pair - 1, 2)
                    pe.wait_ge(*back_rd.rise(before[0], 2 * before[1]))
                    pe.wait_ge(*h_ok.rise(before[0], NZ * before[1]))
                    pe.wait_ge(*y_sb.rise(before[0], len(CHUNKS) * before[1]))
                for j in range(3):
                    last = pe.transpose(bank(4 + c, j * P, j * P + P),
                                        xs[:, 3 * c + j].rearrange("p h c -> p (h c)").bitcast(F32), ident)
                last.then_inc(xt_ps.sem, 1)

            def split(dst, lhs, rhs):
                for n in range(2):
                    a = lhs[n] if isinstance(lhs, tuple) else lhs
                    r = rhs[n] if isinstance(rhs, tuple) else rhs
                    last = pe.matmul(dst, a, r, start=n == 0, stop=n == 1)
                return last

            CW = 3 * P

            def project_q(pair, par, b):
                for c in range(3):
                    pe.wait_ge(*xt_sb.rise(pair, 6 * b + c + 1))
                    split(bank((7, 4, 5)[c], 0, CW), (wa_h[:, 0:P], wa_l[:, 0:P]),
                          xt[:, c * CW:(c + 1) * CW]).then_inc(q_ps.sem, 1)

            def project_k(pair, par, b):
                for c in range(3):
                    if c:
                        pe.wait_ge(*q_sb.rise(pair, 3 * b + c))
                    split(bank((6, 7, 4)[c], 0, CW), (wa_h[:, P:2 * P], wa_l[:, P:2 * P]),
                          xt[:, c * CW:(c + 1) * CW]).then_inc(k_ps.sem, 1)

            def project_v(pair, par, b):
                pe.wait_ge(*q_sb.rise(pair, 3 * b + 3))
                for t in range(ST_N):
                    if t == 8:
                        pe.wait_ge(*k_sb.rise(pair, 3 * b + 1))
                    last = split(bank(5 + t // 8, (t % 8) * C, (t % 8) * C + C), xt[:, t * P:(t + 1) * P],
                                 (wa_h[:, 2 * P:2 * P + C], wa_l[:, 2 * P:2 * P + C]))
                last.then_inc(v_ps.sem, 1)

            def score(pair, par, b, i, c):
                n = first_chunk(i) + c
                if n == 0:
                    pe.wait_ge(*q_sb.rise(pair, 3 * b + 3))
                    pe.wait_ge(*k_sb.rise(pair, 3 * b + 3))
                elif n == 1:
                    pe.wait_ge(*v_cp.rise(pair, 2 * b + 2))
                else:
                    pe.wait_ge(*s_rd.rise(pair, KEY_CHUNKS * b + n - 1))
                a = c * BANK
                m = min((i + 1) * P - a, BANK)
                pe.matmul(bank(4 + n % 2, 0, m), q_t[:, i * P:(i + 1) * P], k_t[:, a:a + m],
                          start=True, stop=True).then_inc(s_ps.sem, 1)

            def turn_probs(pair, par, b, i, c):
                n = KEY_CHUNKS * b + first_chunk(i) + c
                if c == 0:
                    pe.wait_ge(*s_exp.rise(pair, ST_N * b + i + 1))
                if i:
                    pe.wait_ge(*p_sb.rise(pair, n))
                else:
                    pe.wait_ge(*v_cp.rise(pair, 2 * b + 2))
                for k in range(4 * c, min(4 * c + 4, i + 1)):
                    last = pe.transpose(bank(6, (k % 4) * P, (k % 4) * P + P),
                                        probs[i % 2][:, k * P:(k + 1) * P], ident)
                last.then_inc(p_ps.sem, 1)

            def attend(pair, par, b, i, c):
                n = KEY_CHUNKS * b + first_chunk(i) + c
                pe.wait_ge(*p_sb.rise(pair, n + 1))
                if i and c == 0:
                    pe.wait_ge(*o_rd.rise(pair, ST_N * b + i))
                for k in range(4 * c, min(4 * c + 4, i + 1)):
                    last = pe.matmul(bank(7, (i % 8) * C, (i % 8) * C + C),
                                     probs_t[n % 3][:, (k % 4) * P:(k % 4) * P + P], v_sb[:, k, :],
                                     start=(k == 0), stop=(k == i))
                last.then_inc(o_part.sem, 1)

            def gate_logits(pair, par, b):
                pe.wait_ge(*xt_sb.rise(pair, 6 * b + 6))
                pe.wait_ge(*o_rd.rise(pair, ST_N * (b + 1)))
                for t in range(ST_N):
                    last = split(bank(7, t * E, t * E + E), xt[:, t * P:(t + 1) * P], (wg_h[:], wg_l[:]))
                last.then_inc(gate_ps.sem, 1)

            def turn_gates(pair, par, b, k):
                if k:
                    pe.wait_ge(*gate_tsb.rise(pair, 3 * b + 1))
                else:
                    pe.wait_ge(*gate_lo.rise(pair, b + 1))
                for t in range(QT_N, ST_N) if k else range(QT_N):
                    n = 6 + t % 8 // 4
                    last = pe.transpose(bank(n, t % 4 * P, t % 4 * P + P)[0:2 * E],
                                        gate_hl[:, t].rearrange("p h e -> p (h e)").bitcast(F32), ident)
                    if t % 4 == 3 or k:
                        last.then_inc(gate_turn.sem, 1)

            def layer1(pair, par, b, n):
                e, (a, m) = n % E, CHUNKS[n // E]
                if n:
                    pe.wait_ge(*z_sb.rise(pair, b * NZ + n))
                split(bank(4, 0, m), (w1_h[:, e * F:(e + 1) * F], w1_l[:, e * F:(e + 1) * F]),
                      xt[:, a:a + m]).then_inc(z_ps.sem, 1)

            def spread(pair, par, b, n):
                e, (a, m) = n % E, CHUNKS[n // E]
                if n >= 2:
                    pe.wait_ge(*h_ok.rise(pair, b * NZ + n - 1))
                elif n == 0:
                    pe.wait_ge(*gate_tsb.rise(pair, 3 * b + 3))
                pe.matmul(bank(5 + n % 2, 0, m), select[:, e:e + 1].to_broadcast([2 * E, P]), gate_t[:, a:a + m],
                          start=True, stop=True).then_inc(g_ps.sem, 1)

            def layer2(pair, par, b, k, part):
                c, e0 = 2 * k // E, 2 * k % E
                a, m = CHUNKS[c]
                if e0 == 0 and part == 0:
                    if c:
                        pe.wait_ge(*y_sb.rise(pair, len(CHUNKS) * b + c))
                    for n, v in enumerate((b2_h, b2_l)):
                        pe.matmul(bank(7, 0, m), v[:], gate_t[:, a:a + m],
                                  start=(n == 0), stop=False, skip_group_check=True)
                if part == 0:
                    pe.wait_ge(*h_ok.rise(pair, b * NZ + 2 * k + 2))
                x0, x1 = part * m // 2, (part + 1) * m // 2
                for half in range(2):
                    e = e0 + half
                    last = pe.matmul(bank(7, x0, x1)[C * half:C * half + C], w2[:, e * C:(e + 1) * C],
                                     hid[(2 * k + half) % NHID][:, x0:x1], start=False, stop=(e0 == E - 2),
                                     skip_group_check=True)
                if part:
                    last.then_inc(y_ps.sem, 1)

            def turn_back(pair, par, b):
                pe.wait_ge(*y_sb.rise(pair, len(CHUNKS) * (b + 1)))
                for t in range(ST_N):
                    last = pe.matmul(bank(4 + t // 8, t % 8 * C, t % 8 * C + C), y_t[:, t * P:(t + 1) * P],
                                     const[:, HALVES:HALVES + C], start=True, stop=True)
                last.then_inc(back_ps.sem, 1)

            pe.wait_ge(*consts_in.rise(Pair(0), 16 * loads[0]))
            pe.wait_ge(*setup.rise(Pair(0), 3))
            pe.wait_ge(*ready.rise(Pair(0), 1))
            drive(pe, {"rows": rows_turn, "sample": sample, "turn_feature": turn_feature, "query": queries,
                       "off_turn": off_turn, "off_layer2": off_layer2, "turn": turn, "key_values": key_values,
                       "turn_tokens": turn_tokens, "project_q": project_q,
                       "project_k": project_k, "project_v": project_v, "score": score, "turn_probs": turn_probs,
                       "attend": attend, "gate_logits": gate_logits, "turn_gates": turn_gates,
                       "layer1": layer1, "spread": spread, "layer2": layer2, "turn_back": turn_back}, unseen)

        @block.scalar
        def _(act):
            def copy(dst, src):
                return act.activation(dst, src, ACT.Copy)

            def copy_rows(pair, par, _, ch, half, g):
                n = 4 * ch + 2 * half + g
                if half == 0 and g == 0:
                    if ch >= 2:
                        act.wait_ge(*qf_ps.rise(pair, ch - 1))
                        act.wait_ge(*table_in[ch % 2].rise(pair, 32 * (ch // 2)))
                    else:
                        act.wait_ge(*qf_ps.rise(pair - 1, NCH - 1 + ch))
                        act.wait_ge(*table_in[ch % 2].rise(pair - 1, 32 * NCH // 2))
                    if ch:
                        act.wait_ge(*rows_sb.rise(pair, 4 * ch))
                        c = copy(rows[:, ch % 2, :, 0, :], rows[:, 1 - ch % 2, :, CR, :])
                        c.then_inc(carry.sem, 1)
                act.wait_ge(*rows_ps.rise(pair, n + 1))
                r0 = 1 + HR * half + 4 * g
                copy(rows[:, ch % 2, :, r0:r0 + 4, :].rearrange("p b r c -> p r b c"),
                     bank(3).rearrange("p (r b c) -> p r b c", r=4, b=2)).then_inc(rows_sb.sem, 1)
                if n == 3:
                    act.sem_inc(carry.sem, 1)

            def feature(pair, par, _, t):
                act.wait_ge(*qf_ps.rise(pair, t + 1))
                copy(qf[:], bank(3, 0, P)).then_inc(qf_sb.sem, 1)

            def feature_t(pair, par, _, t):
                act.wait_ge(*qft_ps.rise(pair, t + 1))
                copy(qft[:], bank(3, 128, 256)).then_inc(qft_sb.sem, 1)

            def copy_query(pair, par, _, t):
                act.wait_ge(*proj_ps.rise(pair, t + 1))
                src = bank(3, 256, 256 + 2 * (C + O1W)).rearrange("p (b c) -> p b c", b=2)
                if t == 0:
                    act.wait_ge(*tok.rise(pair - 2, 2 * QT_N))
                    act.wait_ge(*idx_ok.rise(pair - 1, 1))
                copy(query[:, par, t], src[:, :, 0:C])
                copy(o1[:, 2 * t:2 * t + 2], src[:, :, C:C + O1W]).then_inc(proj_sb.sem, 1)

            def off_exp(pair, par, _):
                act.wait_ge(*off_u.rise(pair, 1))
                act.activation(ob[:], ob[:], ACT.Exp, scale=-2.0 * (2.0 / np.pi) ** 0.5).then_inc(off_e.sem, 1)

            def off_copy(pair, par, _):
                act.wait_ge(*off_ht.rise(pair, 1))
                copy(oht[:].rearrange("p a b -> p (a b)"), bank(3, 0, 2 * P)).then_inc(off_hsb.sem, 1)

            def turned(pair, par, b, t, h):
                n = b * QT_N + t
                act.wait_ge(*samp_ps.rise(pair, 2 * n + h + 1))
                if h == 0:
                    if n >= 2:
                        act.wait_ge(*kv_ps.rise(pair, n - 1))
                    else:
                        act.wait_ge(*kv_ps.rise(pair - 1, 2 * QT_N - 1 + n))
                copy(samp_t[n % 2][:, h * BANK:(h + 1) * BANK], bank(0)).then_inc(samp_sb.sem, 1)

            def point_exp(pair, par, b, t):
                n = b * QT_N + t
                act.wait_ge(*sc_sub.rise(pair, n + 1))
                act.activation(pt_sc[:, 2 + n % 2], pt_sc[:, 1], ACT.Exp, scale=QK_SCALE).then_inc(sc_exp.sem, 1)

            def normalize(pair, par, b, k, c):
                if k == 2:
                    act.wait_ge(*end_ab.rise(pair, b + 1))
                else:
                    act.wait_ge(*ln_ab.rise(pair, 2 * b + k + 1))
                src, dst, ab = ((h0[:, b], xn, ln9), (h1[:, b], xn, ln9), (out_sb, out_sb, ln9_e))[k]
                for t in range(3 * c, 3 * c + 3):
                    last = act.activation(dst[:, t, :], src[:, t, :], ACT.Identity,
                                          scale=ab[:, 3, t:t + 1], bias=ab[:, 4, t:t + 1])
                last.then_inc(end_x.sem if k == 2 else ln_x.sem, 1)

            def high(pair, par, b, k, c):
                act.wait_ge(*ln_x.rise(pair, 3 * (2 * b + k) + c + 1))
                act.activation(xs[:, 3 * c:3 * c + 3, 0, :], xn[:, 3 * c:3 * c + 3], ACT.Copy).then_inc(ln_hi.sem, 1)

            def copy_tokens(pair, par, b, k, c):
                act.wait_ge(*xt_ps.rise(pair, 3 * (2 * b + k) + c + 1))
                copy(xt[:, c * 3 * P:(c + 1) * 3 * P], bank(4 + c, 0, 3 * P)).then_inc(xt_sb.sem, 1)

            CW = 3 * P

            def copy_q(pair, par, b):
                for c in range(3):
                    act.wait_ge(*q_ps.rise(pair, 3 * b + c + 1))
                    act.activation(q_t[:, c * CW:(c + 1) * CW], bank((7, 4, 5)[c], 0, CW), ACT.Identity,
                                   bias=bqk[:, 0:1]).then_inc(q_sb.sem, 1)

            def copy_k(pair, par, b):
                for c in range(3):
                    act.wait_ge(*k_ps.rise(pair, 3 * b + c + 1))
                    act.activation(k_t[:, c * CW:(c + 1) * CW], bank((6, 7, 4)[c], 0, CW), ACT.Identity,
                                   bias=bqk[:, 1:2]).then_inc(k_sb.sem, 1)

            def copy_v(pair, par, b):
                act.wait_ge(*v_ps.rise(pair, b + 1))
                vf = v_sb[:].rearrange("p t c -> p (t c)")
                copy(vf[:, 0:BANK], bank(5)).then_inc(v_cp.sem, 1)
                copy(vf[:, BANK:BANK + C], bank(6, 0, C)).then_inc(v_cp.sem, 1)

            def soft(pair, par, b, i):
                act.wait_ge(*s_max.rise(pair, ST_N * b + i + 1))
                n = (i + 1) * P
                act.activation(probs[i % 2][:, 0:n], probs[i % 2][:, 0:n], ACT.Exp,
                               bias=att[:, 1, i:i + 1], scale=ATT_SCALE,
                               accum_out=att[:, 2, i:i + 1]).then_inc(s_exp.sem, 1)

            def copy_probs(pair, par, b, i, c):
                n = first_chunk(i) + c
                m = min(4, i + 1 - 4 * c) * P
                act.wait_ge(*p_ps.rise(pair, KEY_CHUNKS * b + n + 1))
                if n >= 3:
                    act.wait_ge(*o_part.rise(pair, KEY_CHUNKS * b + n - 2))
                copy(probs_t[(KEY_CHUNKS * b + n) % 3][:, 0:m], bank(6, 0, m)).then_inc(p_sb.sem, 1)

            def gate_exp(pair, par, b):
                act.wait_ge(*gate_d.rise(pair, b + 1))
                act.activation(gs[:, 3, :], gs[:, 2, :], ACT.Exp).then_inc(gate_e.sem, 1)

            def gate_high(pair, par, b):
                act.wait_ge(*gate_ok.rise(pair, b + 1))
                act.activation(gate_hl[:, :, 0, :], gate[:], ACT.Copy).then_inc(gate_hi.sem, 1)

            def copy_gates(pair, par, b, k):
                for n in (2,) if k else range(2):
                    act.wait_ge(*gate_turn.rise(pair, 3 * b + n + 1))
                    m = P if k else BANK
                    copy(gate_t[:, n * BANK:n * BANK + m], bank(6 + n % 2, 0, m)[0:2 * E]).then_inc(gate_tsb.sem, 1)

            def relu(pair, par, b, n):
                e, m = n % E, CHUNKS[n // E][1]
                act.wait_ge(*z_ps.rise(pair, b * NZ + n + 1))
                if n >= NHID and n % 2 == 0:
                    act.wait_ge(*y_ps.rise(pair, b * NY + (n - NHID) // 2 + 1))
                act.activation(hid[n % NHID][:, 0:m], bank(4, 0, m), ACT.Relu,
                               bias=b1[:, e:e + 1]).then_inc(z_sb.sem, 1)

            def copy_y(pair, par, b, c):
                a, m = CHUNKS[c]
                act.wait_ge(*y_ps.rise(pair, b * NY + (c + 1) * E // 2))
                copy(y_t[:, a:a + m], bank(7, 0, m)).then_inc(y_sb.sem, 1)

            act.wait_ge(*consts_in.rise(Pair(0), 16 * loads[0]))
            act.wait_ge(*setup.rise(Pair(0), 1))
            copy(wa_h[:], fm[:, 0, 0:NATT])
            copy(wg_h[:], fm[:, 1, 0:E])
            copy(b2_h[:], fm[0:2 * E, 1, E:E + P])
            copy(select[:], const[0:2 * E, SELECT:SELECT + E])
            copy(w1_h[:], gath[:, 0].rearrange("p a b -> p (a b)")).then_inc(act_own, 1)
            act.wait_ge(*setup.rise(Pair(0), 3))
            act.sem_inc(ready.sem, 1)
            drive(act, {"copy_rows": copy_rows, "feature": feature, "feature_t": feature_t,
                        "copy_query": copy_query, "off_exp": off_exp, "off_copy": off_copy,
                        "turned": turned, "point_exp": point_exp, "normalize": normalize, "high": high,
                        "copy_tokens": copy_tokens, "copy_q": copy_q, "copy_k": copy_k, "copy_v": copy_v, "soft": soft,
                        "copy_probs": copy_probs, "gate_exp": gate_exp, "gate_high": gate_high, "copy_gates": copy_gates,
                        "relu": relu, "copy_y": copy_y}, unseen)

        @block.vector
        def _(dve):
            steps = [0]
            start = [0]
            marks = {}
            before = [None]

            def step(ins):
                steps[0] += 1
                marks[thread[0]] = steps[0]
                ins.then_inc(vec, 1)

            def settle():
                n = marks.get(thread[0], start[0])
                if before[0] is None:
                    dve.wait_ge(vec, n)
                else:
                    pair, head = before[0]
                    dve.wait_ge(vec, pair.times(STEPS[2], head + n))

            def own(ins):
                step(ins)
                settle()

            def parts(stage):
                begun = {}

                def go(pair, par, b, *args):
                    key = (b, *args)
                    if key not in begun:
                        begun[key] = stage(pair, par, b, *args)
                    if next(begun[key], "end") == "end":
                        del begun[key]
                go.begun = begun
                staged.append(go)
                return go

            staged = []

            def tt(o, a, b, op):
                return dve.tensor_tensor(o, a, b, op)

            def ts(o, a, s1, op1, s2=None, op2=None):
                if op2 is None:
                    return dve.tensor_scalar(o, a, s1, None, op1)
                return dve.tensor_scalar(o, a, s1, s2, op1, op2)

            def stt(o, a, s, b, op0, op1):
                return dve.scalar_tensor_tensor(out=o, in0=a, scalar=s, in1=b, op0=op0, op1=op1)

            def red(o, a, op=ALU.add):
                return dve.tensor_reduce(o, a, X_AXIS, op)

            def rsqrt(r, v, t, h):
                step(ts(t.bitcast(I32), v.bitcast(I32), 1, ALU.logical_shift_right))
                step(ts(h, v, -0.5, ALU.mult))
                yield
                settle()
                step(ts(r.bitcast(I32), t.bitcast(I32), -1.0, ALU.mult, RSQRT_SEED, ALU.add))
                yield
                settle()
                for _ in range(3):
                    step(tt(t, r, r, ALU.mult))
                    yield
                    settle()
                    step(tt(t, t, h, ALU.mult))
                    yield
                    settle()
                    step(stt(r, t, 1.5, r, ALU.add, ALU.mult))
                    yield
                    settle()

            def bc16(v):
                return v.unsqueeze(2).to_broadcast([P, GROUPS, O1W])

            def row16(v):
                return v.unsqueeze(1).to_broadcast([P, GROUPS, O1W])

            def off_hidden(pair, par, _):
                dve.wait_ge(*proj_sb.rise(pair, NCH))
                dve.wait_ge(*off_ht.rise(pair - 1, 1))
                step(tt(oa[:], o1[:], row16(bo1), ALU.add))
                yield
                settle()
                step(red(st16[:, 0], oa[:]))
                yield
                settle()
                step(stt(oa[:], bc16(st16[:, 0]), -1.0 / O1W, oa[:], ALU.mult, ALU.add))
                yield
                settle()
                step(tt(ob[:], oa[:], oa[:], ALU.mult))
                yield
                settle()
                step(red(st16[:, 0], ob[:]))
                yield
                settle()
                step(ts(st16[:, 1], st16[:, 0], 1.0 / O1W, ALU.mult, EPS, ALU.add))
                yield
                settle()
                yield from rsqrt(st16[:, 2], st16[:, 1], st16[:, 3], st16[:, 4])
                step(tt(oa[:], oa[:], bc16(st16[:, 2]), ALU.mult))
                yield
                settle()
                step(tt(oa[:], oa[:], row16(lng), ALU.mult))
                yield
                settle()
                step(tt(oa[:], oa[:], row16(lnb), ALU.add))
                yield
                settle()
                step(tt(ob[:], oa[:], oa[:], ALU.mult))
                yield
                settle()
                step(ts(ob[:], ob[:], 0.044715, ALU.mult, 1.0, ALU.add))
                yield
                settle()
                step(tt(ob[:], ob[:], oa[:], ALU.mult))
                yield
                settle()
                ts(ob[:], ob[:], -50.0, ALU.max).then_inc(off_u.sem, 1)

            def off_gelu(pair, par, _):
                dve.wait_ge(*off_e.rise(pair, 1))
                step(ts(ob[:], ob[:], 1.0, ALU.add))
                yield
                settle()
                step(dve.reciprocal(ob[:], ob[:]))
                yield
                settle()
                tt(oa[:], oa[:], ob[:], ALU.mult).then_inc(off_h.sem, 1)

            def off_points(pair, par, _):
                dve.wait_ge(*off_raw.rise(pair, 1))
                xy = base_xy[:].rearrange("p g n k -> p (g n k)")
                caf, cbf = (v.rearrange("p n k -> p (n k)") for v in (ca, cb))
                stt(caf, bank(3, 256, 512), 4.0, xy, ALU.mult, ALU.add).then_inc(off_rd.sem, 1)
                dve.wait_ge(*off_rd.rise(pair, 1))
                step(ts(caf, caf, 0.0, ALU.max, float(W - 1), ALU.min))
                yield
                settle()
                step(ts(cbf, caf, RNE, ALU.add, RNE, ALU.subtract))
                yield
                settle()
                f1 = frac2[:].rearrange("p n k s -> p (n k) s")
                step(tt(f1[:, :, 0], cbf, caf, ALU.is_gt))
                yield
                settle()
                step(stt(cbf, f1[:, :, 0], -1.0, cbf, ALU.mult, ALU.add))
                yield
                settle()
                step(ts(cbf, cbf, float(W - 2), ALU.min))
                yield
                settle()
                step(stt(f1[:, :, 1], cbf, -1.0, caf, ALU.mult, ALU.add))
                yield
                settle()
                step(ts(f1[:, :, 0], f1[:, :, 1], -1.0, ALU.mult, 1.0, ALU.add))
                idf = idxf.rearrange("p g n -> p (g n)")
                step(stt(idf, cb[:, :, 1], float(W), cb[:, :, 0], ALU.mult, ALU.add))
                yield
                settle()
                base_t = table_base[:].unsqueeze(1).unsqueeze(3).to_broadcast([P, QT_N, 2, NP_])
                tt(idx[:, par].rearrange("p (t b n) -> p t b n", t=QT_N, b=2),
                        idxf.rearrange("p (t b) n -> p t b n", b=2), base_t, ALU.add).then_inc(idx_ok.sem, 1)
                dve.wait_ge(*wcorn[1].rise(pair - 2, 2 * QT_N))
                cw = corner_w[:, par].rearrange("p g (n x y) -> p (g n) x y", x=2, y=2)
                n = GROUPS * NP_
                tt(cw, frac2[:, :, 0, :].unsqueeze(3).to_broadcast([P, n, 2, 2]),
                        frac2[:, :, 1, :].unsqueeze(2).to_broadcast([P, n, 2, 2]), ALU.mult).then_inc(corner_ok.sem, 1)

            def weigh(pair, par, b, t):
                n = b * QT_N + t
                dve.wait_ge(*gath_in[n % NG].rise(pair, 16 * NP_ * (n // NG + 1)))
                if n == 0:
                    dve.wait_ge(*corner_ok.rise(pair, 1))
                    dve.wait_ge(*samp_ps.rise(pair - 1, 4 * QT_N - 1))
                else:
                    dve.wait_ge(*samp_ps.rise(pair, 2 * n - 1))
                g = gath[:, n % NG, 0:4, :].rearrange("p n (k c) -> p (n k) c", c=C)
                cw = corner_w[:, par, 2 * t + b, 0:16]
                tt(prod[0][:].rearrange("p (n c) -> p n c", c=C), g,
                   cw.unsqueeze(2).to_broadcast([P, 16, C]), ALU.mult).then_inc(wcorn[0].sem, 1)

            def scores(pair, par, b, t):
                n = b * QT_N + t
                dve.wait_ge(*kv_ps.rise(pair, n + 1))
                kv = ps[:, BANK:3 * BANK].rearrange("p (n c) -> p n c", c=2 * C)
                q = query[:, par, t, b, :].unsqueeze(1).to_broadcast([P, NP_, C])
                step(tt(kq[:].rearrange("p (n c) -> p n c", c=C), kv[:, :, 0:C], q, ALU.mult))
                yield
                settle()
                step(red(pt_sc[:, 0], kq[:].rearrange("p (m d) -> p m d", d=DH)))
                yield
                settle()
                sc = pt_sc[:, 0].rearrange("p (n h) -> p n h", h=NH)
                step(red(pt_st[:, 0], sc.rearrange("p n h -> p h n"), ALU.max))
                yield
                settle()
                if n:
                    dve.wait_ge(*sc_exp.rise(pair, n))
                else:
                    dve.wait_ge(*sc_exp.rise(pair - 1, 2 * QT_N))
                tt(pt_sc[:, 1].rearrange("p (n h) -> p n h", h=NH), sc,
                   pt_st[:, 0].unsqueeze(1).to_broadcast([P, NP_, NH]), ALU.subtract).then_inc(sc_sub.sem, 1)

            def values(pair, par, b, t):
                n = b * QT_N + t
                dve.wait_ge(*sc_exp.rise(pair, n + 1))
                ex = pt_sc[:, 2 + n % 2]
                step(red(pt_st[:, 1], ex.rearrange("p (n h) -> p h n", h=NH)))
                for h in range(2):
                    kv = bank(1 + h).rearrange("p (n c) -> p n c", c=2 * C)[:, :, C:2 * C]
                    e = ex[:, 32 * h:32 * h + 32]
                    tt(av[:, 256 * h:256 * h + 256].rearrange("p (m d) -> p m d", d=DH),
                       kv.rearrange("p n (h d) -> p n h d", d=DH),
                       e.rearrange("p (n h) -> p n h", h=NH).unsqueeze(3).to_broadcast([P, 4, NH, DH]),
                       ALU.mult).then_inc(kv_rd.sem, 1)
                settle()
                step(dve.reciprocal(pt_st[:, 2], pt_st[:, 1]))
                yield
                dve.wait_ge(*kv_rd.rise(pair, 2 * n + 2))
                step(red(pt_o[:], av[:].rearrange("p (n c) -> p c n", c=C)))
                yield
                settle()
                tt(h0[:, b, t].rearrange("p (h d) -> p h d", d=DH), pt_o[:].rearrange("p (h d) -> p h d", d=DH),
                   pt_st[:, 2].unsqueeze(2).to_broadcast([P, NH, DH]), ALU.mult).then_inc(tok.sem, 1)

            def stats(pair, par, b, k, t):
                if k == 0 and t < QT_N:
                    dve.wait_ge(*tok.rise(pair, QT_N * b + t + 1))
                elif k == 0:
                    dve.wait_ge(*txt_in[b].rise(pair, 16))
                elif k == 1:
                    dve.wait_ge(*o_rd.rise(pair, ST_N * b + t + 1))
                elif t == 0:
                    dve.wait_ge(*y_ok.rise(pair, b + 1))
                bn = (bn6, bn6_1, bn6_e)[k]
                step(dve.bn_stats(bn[:, t, :], (h0[:, b], h1[:, b], out_sb)[k][:, t, :]))

            def moments(pair, par, b, k):
                settle()
                dve.sem_inc(dve_gate, 1)
                for t in range(ST_N):
                    step(dve.bn_aggr((mv_e if k == 2 else mv)[:, t, :], (bn6, bn6_1, bn6_e)[k][:, t, :]))

            def scale(pair, par, b, k):
                settle()
                ab, m = (ln9_e, mv_e) if k == 2 else (ln9, mv)
                step(ts(ab[:, 0], m[:, :, 1], EPS, ALU.add))
                yield
                settle()
                yield from rsqrt(ab[:, 3], ab[:, 0], ab[:, 1], ab[:, 2])
                stt(ab[:, 4], m[:, :, 0], -1.0, ab[:, 3], ALU.mult, ALU.mult).then_inc(
                    end_ab.sem if k == 2 else ln_ab.sem, 1)

            def low(pair, par, b, k, c):
                dve.wait_ge(*ln_hi.rise(pair, 3 * (2 * b + k) + c + 1))
                t = slice(3 * c, 3 * c + 3)
                tt(xs[:, t, 1, :], xn[:, t], xs[:, t, 0, :].bitcast(F32), ALU.subtract).then_inc(ln_lo.sem, 1)
                if k == 0 and c == 2:
                    step(tt(h0[:, b], h0[:, b], bv.unsqueeze(1).to_broadcast([P, ST_N, C]), ALU.add))

            def score_max(pair, par, b, i, c):
                n = first_chunk(i) + c
                dve.wait_ge(*s_ps.rise(pair, KEY_CHUNKS * b + n + 1))
                a = c * BANK
                m = min((i + 1) * P - a, BANK)
                if c == 0 and i >= 2:
                    dve.wait_ge(*p_ps.rise(pair, KEY_CHUNKS * b + first_chunk(i - 1)))
                end = c == key_chunks(i) - 1
                plus = const[:, MASK + P - m:MASK + P] if end else zero.to_broadcast([P, m])
                one = end and c == 0
                most = att[:, 0, i:i + 1] if one else att_m[:, n:n + 1]
                dve.sem_inc(dve_gate, 1)
                dve.tensor_tensor_reduce(out=probs[i % 2][:, a:a + m], in0=bank(4 + n % 2, 0, m), in1=plus,
                                         scale=1.0, scalar=LOWEST, op0=ALU.add, op1=ALU.max,
                                         accum_out=most).then_inc(s_rd.sem, 1)
                if end:
                    dve.wait_ge(*s_rd.rise(pair, KEY_CHUNKS * b + n + 1))
                    if c:
                        own(red(att[:, 0, i:i + 1], att_m[:, n - c:n + 1], ALU.max))
                    ts(att[:, 1, i:i + 1], att[:, 0, i:i + 1], -ATT_SCALE, ALU.mult).then_inc(s_max.sem, 1)

            def heads(pair, par, b, i):
                dve.wait_ge(*s_exp.rise(pair, ST_N * b + i + 1))
                own(dve.reciprocal(att[:, 3, i:i + 1], att[:, 2, i:i + 1]))
                dve.wait_ge(*o_part.rise(pair, KEY_CHUNKS * b + first_chunk(i + 1)))
                if i == 0:
                    dve.wait_ge(*out_ok.rise(pair - 1, b + 1))
                stt(h1[:, b, i, :], bank(7, (i % 8) * C, (i % 8) * C + C), att[:, 3, i:i + 1],
                    h0[:, b, i, :], ALU.mult, ALU.add).then_inc(o_rd.sem, 1)

            def bc_e(v):
                return v.unsqueeze(2).to_broadcast([P, ST_N, E])

            def top2(pair, par, b):
                dve.wait_ge(*gate_ps.rise(pair, b + 1))
                rank = const[:, RANK:RANK + E].unsqueeze(1).to_broadcast([P, ST_N, E])
                step(tt(lg[:, 0], bank(7, 0, ST_N * E).rearrange("p (t e) -> p t e", e=E),
                        gateb.unsqueeze(1).to_broadcast([P, ST_N, E]), ALU.add))
                yield
                settle()
                for n in range(2):
                    step(red(gs[:, n], lg[:, n], ALU.max))
                    yield
                    settle()
                    step(tt(lg[:, 4], lg[:, n], bc_e(gs[:, n]), ALU.is_equal))
                    yield
                    settle()
                    step(tt(lg[:, 4], lg[:, 4], rank, ALU.mult))
                    yield
                    settle()
                    step(red(gs[:, 5], lg[:, 4], ALU.max))
                    yield
                    settle()
                    step(tt(lg[:, 2 + n], lg[:, 4], bc_e(gs[:, 5]), ALU.is_equal))
                    yield
                    settle()
                    if n == 0:
                        step(stt(lg[:, 1], lg[:, 2], MASKED, lg[:, 0], ALU.mult, ALU.add))
                        yield
                        settle()
                tt(gs[:, 2], gs[:, 1], gs[:, 0], ALU.subtract).then_inc(gate_d.sem, 1)

            def gates(pair, par, b):
                dve.wait_ge(*gate_e.rise(pair, b + 1))
                step(ts(gs[:, 4], gs[:, 3], 1.0, ALU.add))
                yield
                settle()
                step(dve.reciprocal(gs[:, 5], gs[:, 4]))
                yield
                settle()
                step(tt(gs[:, 6], gs[:, 3], gs[:, 5], ALU.mult))
                yield
                settle()
                step(tt(lg[:, 2], lg[:, 2], bc_e(gs[:, 5]), ALU.mult))
                step(tt(lg[:, 3], lg[:, 3], bc_e(gs[:, 6]), ALU.mult))
                yield
                settle()
                tt(gate[:], lg[:, 2], lg[:, 3], ALU.add).then_inc(gate_ok.sem, 1)

            def gate_low(pair, par, b):
                dve.wait_ge(*gate_hi.rise(pair, b + 1))
                tt(gate_hl[:, :, 1, :], gate[:], gate_hl[:, :, 0, :].bitcast(F32),
                   ALU.subtract).then_inc(gate_lo.sem, 1)

            def gated(pair, par, b, n):
                m = CHUNKS[n // E][1]
                dve.wait_ge(*z_sb.rise(pair, b * NZ + n + 1))
                dve.wait_ge(*g_ps.rise(pair, b * NZ + n + 1))
                h = hid[n % NHID][:, 0:m]
                tt(h, h, bank(5 + n % 2, 0, m), ALU.mult).then_inc(h_ok.sem, 1)

            def residual(pair, par, b):
                dve.wait_ge(*stored.rise(pair, 16 * b))
                dve.wait_ge(*back_ps.rise(pair, b + 1))
                for n, (t, m) in enumerate(((0, QT_N), (QT_N, 1))):
                    tt(out_sb[:, t:t + m], bank(4 + n, 0, m * C).rearrange("p (t c) -> p t c", c=C),
                       xn[:, t:t + m], ALU.add).then_inc(back_rd.sem, 1)
                dve.wait_ge(*back_rd.rise(pair, 2 * b + 2))
                dve.sem_inc(y_ok.sem, 1)

            def finish(pair, par, b):
                def row(v):
                    return v.unsqueeze(1).to_broadcast([P, ST_N, C])
                dve.wait_ge(*end_x.rise(pair, 3 * b + 3))
                step(tt(out_sb[:], out_sb[:], row(gamma), ALU.mult))
                yield
                settle()
                step(tt(out_sb[:], out_sb[:], row(beta), ALU.add))
                yield
                settle()
                tt(out_sb[:], out_sb[:], h1[:, b], ALU.add).then_inc(out_ok.sem, 1)

            for v in (w_proj, w_o2, bqk):
                step(dve.memset(v[:], 0.0))
            step(dve.memset(fm[:], 0.0))
            step(dve.memset(shared[:, 0:2 * C], 0.0))
            for b in range(2):
                step(dve.memset(table_base[:, b:b + 1], float(b * H * W)))
            settle()
            for s in signals:
                if s.spare:
                    dve.sem_inc(s.sem, s.spare)
            dve.sem_inc(setup.sem, 1)
            dve.wait_ge(*consts_in.rise(Pair(0), 16 * loads[0]))
            dve.wait_ge(act_own, 1)
            step(tt(wa_l[:], fm[:, 0, 0:NATT], wa_h[:].bitcast(F32), ALU.subtract))
            step(tt(b2_l[:], fm[0:2 * E, 1, E:E + P], b2_h[:].bitcast(F32), ALU.subtract))
            step(tt(wg_l[:], fm[:, 1, 0:E], wg_h[:].bitcast(F32), ALU.subtract))
            step(tt(w1_l[:], gath[:, 0].rearrange("p a b -> p (a b)"), w1_h[:].bitcast(F32), ALU.subtract))
            step(dve.memset(base_xy[:], 0.0))
            settle()
            bxy = base_xy[:].rearrange("p (t b) n k -> p t (b n) k", b=2)
            own(stt(base_xy[:].rearrange("p g n k -> p g (n k)"), bo2.unsqueeze(1).to_broadcast([P, GROUPS, 16]), 4.0,
                    base_xy[:].rearrange("p g n k -> p g (n k)"), ALU.mult, ALU.add))
            own(ts(bxy[:, :, :, 0], bxy[:, :, :, 0], const[:, GX:GX + 1], ALU.add))
            own(tt(bxy[:, :, :, 1], bxy[:, :, :, 1],
                   const[:, GY:GY + QT_N].unsqueeze(2).to_broadcast([P, QT_N, 2 * NP_]), ALU.add))
            dve.wait_ge(*spare_rows.rise(Pair(0), 64))
            dve.sem_inc(setup.sem, 2)

            done = [None, 0]

            def stretch(n, pair):
                last, count = done
                assert not any(g.begun for g in staged), [g.begun for g in staged if g.begun]
                if last is not None:
                    assert steps[0] == count + STEPS[last], ("steps", last, steps[0] - count)
                if n == 2:
                    steps[0] = 0
                    before[0] = (pair, setup_steps + STEPS[0] + STEPS[1] - STEPS[2])
                    done[:] = [n, 0]
                elif n == 3:
                    before[0] = None
                    steps[0] = setup_steps + STEPS[0] + STEPS[1] + STEPS[2] * (PAIRS - 2)
                    done[:] = [n, steps[0]]
                else:
                    done[:] = [n, steps[0]]
                start[0] = steps[0]
                marks.clear()

            setup_steps = steps[0]
            drive(dve, {"off_hidden": parts(off_hidden), "off_gelu": parts(off_gelu), "off_points": parts(off_points),
                        "weigh": weigh, "scores": parts(scores), "values": parts(values),
                        "stats": stats, "moments": moments, "scale": parts(scale), "low": low,
                        "score_max": score_max, "heads": heads, "top2": parts(top2), "gates": parts(gates),
                        "gate_low": gate_low, "gated": gated, "residual": residual,
                        "finish": parts(finish)}, stretch)


STEPS = (34, 232, 384, 350, 152)


def kernel(**inputs):
    import concourse.bacc as bacc
    from concourse.bass_utils import run_bass_kernel_spmd as run

    a = {k: np.ascontiguousarray(v) for k, v in inputs.items()}
    arrays = {
        "x": a["x"], "txt": a["txt"], "const": constants(),
        "Wq_t": a["L0_tok_W_q"].T, "Wk_t": a["L0_tok_W_k"].T, "Wv_t": a["L0_tok_W_v"].T,
        "W_o1": a["L0_tok_W_o1"], "b_o1": a["L0_tok_b_o1"], "ln_g": a["L0_tok_ln_g"], "ln_b": a["L0_tok_ln_b"],
        "W_o2": a["L0_tok_W_o2"], "b_o2": a["L0_tok_b_o2"],
        "aWq": a["L0_attn_Wq"], "abq": a["L0_attn_bq"], "aWk": a["L0_attn_Wk"], "abk": a["L0_attn_bk"],
        "aWv": a["L0_attn_Wv"], "abv": a["L0_attn_bv"],
        "gate_w": a["L0_ffn_gate_w"], "gate_b": a["L0_ffn_gate_b"], "w1": a["L0_ffn_w1"],
        "b1_t": a["L0_ffn_b1"].T, "w2": a["L0_ffn_w2"], "b2": a["L0_ffn_b2"],
        "gamma": a["L0_ffn_gamma"], "beta": a["L0_ffn_beta"],
    }
    arrays = {f"in_{k}": np.ascontiguousarray(v) for k, v in arrays.items()}
    nc = bacc.Bacc("TRN2", target_bir_lowering=False, num_devices=1)
    nc.disable_value_cache = True
    w = {k[3:]: nc.dram_tensor(k, v.shape, mybir.dt.from_np(v.dtype), kind="ExternalInput").ap()
         for k, v in arrays.items()}
    out = nc.dram_tensor("out_0", (B, S, C), F32, kind="ExternalOutput").ap()
    tables = [nc.dram_tensor(f"table{n}", (2 * H * W, 2 * C), F32, kind="Internal").ap() for n in range(2)]
    build(nc, w["x"], w["txt"], w, out, tables)
    r = run(nc, [arrays], core_ids=[0])
    return r.results[0]["out_0"]
```
